# Optimizing a Trainium2 kernel written in Bass

```python
import numpy as np
import jax
import jax.numpy as jnp

def _softmax(x, axis=-1):
    return jax.nn.softmax(x, axis=axis)

def _gelu(x):
    return jax.nn.gelu(x, approximate=True)

def _silu(x):
    return jax.nn.silu(x)

def _sigmoid(x):
    return jax.nn.sigmoid(x)

def _layernorm(x, axis=-1, eps=1e-05):
    m = jnp.mean(x, axis=axis, keepdims=True)
    v = jnp.var(x, axis=axis, keepdims=True)
    return (x - m) / jnp.sqrt(v + eps)

def _scatter_add(tgt, idx, src, axis=0):
    return tgt.at[idx].add(src)

def _segment_sum(src, seg, n):
    return jax.ops.segment_sum(src, seg, n)
kernel_name = 'mk_flamingo_gated_d4_seqx_r8_09cd13'

def setup_inputs(seed: int=0):
    np.random.seed(seed)
    _w = jnp.asarray

    def _rec_inputs():
        import jax
        import jax.numpy as jnp
        _rk = jax.random.key(seed)
        x = -0.0002928 + 1 * jax.random.normal(jax.random.fold_in(_rk, 1), (8, 256, 128), jnp.float32)
        _lenS = 256 - jax.random.randint(jax.random.fold_in(_rk, 7), (8,), 0, max(1, 256 // 4) + 1, jnp.int32)
        _lenS2 = 64 - jax.random.randint(jax.random.fold_in(_rk, 8), (8,), 0, max(1, 64 // 4) + 1, jnp.int32)
        _ctx_1024P = jax.random.normal(jax.random.fold_in(_rk, 11), (8, 16, 128), jnp.float32)
        _ctx_1024c = jax.random.dirichlet(jax.random.fold_in(_rk, 511), 0.3 * jnp.ones((16,), jnp.float32), (8, 64))
        _ctx_1024t = jnp.einsum('bsk,bkd->bsd', _ctx_1024c, _ctx_1024P)
        _ctx_1024t = _ctx_1024t * jax.lax.rsqrt(jnp.mean(jnp.square(_ctx_1024t)) + 1e-12) * 0.953939
        ctx_1024 = -1.39393e-06 + 0.999914 * (_ctx_1024t + 0.3 * jax.random.normal(jax.random.fold_in(_rk, 611), (8, 64, 128), jnp.float32))
        _validS = jnp.arange(256)[None, :] < _lenS[:, None]
        _validS2 = jnp.arange(64)[None, :] < _lenS2[:, None]
        _causal = jnp.tril(jnp.ones((256, 256), dtype=bool))
        mask_Bx1xSxS2_ff0 = jnp.where(jnp.ones((8, 1, 256, 64), dtype=bool), 0.0, -1000000000.0).astype(jnp.float32)
        _g = jax.random.normal(jax.random.fold_in(_rk, 9001), (2, 4), jnp.float32)
        _g = jnp.sign(_g) * jnp.maximum(jnp.abs(_g), 1.0) + (_g == 0) * 1.0
        g_xattn = _g[0]
        g_ffn = _g[1]
        return (x, ctx_1024, mask_Bx1xSxS2_ff0, g_xattn, g_ffn)
    x, ctx_1024, mask_Bx1xSxS2_ff0, g_xattn, g_ffn = _rec_inputs()

    def _L0_xattn_setup():
        import jax, jax.numpy as jnp
        import numpy as np
        DIM = 128
        NUM_HEADS = 16
        HEAD_DIM = DIM // NUM_HEADS
        key = jax.random.key(seed)
        ks = jax.random.split(key, 8)
        B, N, N2 = (2, 256, 256)
        s = 1.0 / np.sqrt(DIM)
        return {'x': jax.random.normal(ks[0], (B, N, DIM), jnp.float32), 'y': jax.random.normal(ks[1], (B, N2, DIM), jnp.float32), 'Wq': jax.random.normal(ks[2], (DIM, DIM), jnp.float32) * s, 'bq': jnp.zeros((DIM,), jnp.float32), 'Wkv': jax.random.normal(ks[3], (DIM, 2 * DIM), jnp.float32) * s, 'bkv': jnp.zeros((2 * DIM,), jnp.float32), 'Wo': jax.random.normal(ks[4], (DIM, DIM), jnp.float32) * s, 'bo': jnp.zeros((DIM,), jnp.float32)}
    _L0_xattn_all = _L0_xattn_setup()
    _L0_xattn_in = {k: v for k, v in _L0_xattn_all.items() if k in ('Wq', 'bq', 'Wkv', 'bkv', 'Wo', 'bo')}
    del _L0_xattn_all

    def _L0_ffn_setup():
        import jax, jax.numpy as jnp
        import numpy as np
        DMODEL = 128
        N_EXPERTS = 16
        EXPERT_SIZE = 32
        K = 4
        key = jax.random.key(seed)
        k1, k2, k3, k4 = jax.random.split(key, 4)
        std_sel = 1.0 / np.sqrt(DMODEL)
        std_val = 1.0 / np.sqrt(N_EXPERTS * EXPERT_SIZE)
        return {'x': jax.random.normal(k1, (4, 256, DMODEL), dtype=jnp.float32), 'expert_sel': jax.random.normal(k2, (N_EXPERTS, DMODEL), dtype=jnp.float32) * std_sel, 'keys': jax.random.normal(k3, (N_EXPERTS, DMODEL, EXPERT_SIZE), dtype=jnp.float32) * std_sel, 'values': jax.random.normal(k4, (N_EXPERTS, EXPERT_SIZE, DMODEL), dtype=jnp.float32) * std_val, 'route_scale': jnp.ones((1,), dtype=jnp.float32)}
    _L0_ffn_all = _L0_ffn_setup()
    _L0_ffn_in = {k: v for k, v in _L0_ffn_all.items() if k in ('expert_sel', 'keys', 'values', 'route_scale')}
    del _L0_ffn_all

    def _L1_xattn_setup():
        import jax, jax.numpy as jnp
        import numpy as np
        B, N, P, DIM, H = (8, 128, 77, 128, 16)
        HD = DIM // H
        LN_EPS = 1e-05
        key = jax.random.key(seed)
        ks = jax.random.split(key, 8)
        s = 0.02
        return {'x': jax.random.normal(ks[0], (B, N, DIM), jnp.float32), 'x_text': jax.random.normal(ks[1], (B, P, DIM), jnp.float32), 'Wq': jax.random.normal(ks[2], (DIM, DIM), jnp.float32) * s, 'Wk': jax.random.normal(ks[3], (DIM, DIM), jnp.float32) * s, 'Wv': jax.random.normal(ks[4], (DIM, DIM), jnp.float32) * s, 'gate': jax.random.normal(ks[5], (1, H, 1, 1), jnp.float32) * 0.5, 'ln_g': jnp.ones((DIM,), jnp.float32), 'ln_b': jnp.zeros((DIM,), jnp.float32), 'Wp': jax.random.normal(ks[6], (DIM, DIM), jnp.float32) * s, 'bp': jnp.zeros((DIM,), jnp.float32)}
    _L1_xattn_all = _L1_xattn_setup()
    _L1_xattn_in = {k: v for k, v in _L1_xattn_all.items() if k in ('Wq', 'Wk', 'Wv', 'gate', 'ln_g', 'ln_b', 'Wp', 'bp')}
    del _L1_xattn_all

    def _L1_ffn_setup():
        import jax, jax.numpy as jnp
        import numpy as np
        D = 128
        F = 352
        E = 8
        TOP_K = 2
        key = jax.random.key(seed)
        ks = jax.random.split(key, 6)
        std = 0.02
        x = jax.random.normal(ks[0], (2, 256, D), dtype=jnp.float32)
        router_w = jax.random.normal(ks[1], (D, E), dtype=jnp.float32) * std
        w1 = jax.random.normal(ks[2], (E, D, F), dtype=jnp.float32) * std
        v1 = jax.random.normal(ks[3], (E, D, F), dtype=jnp.float32) * std
        w2 = jax.random.normal(ks[4], (E, F, D), dtype=jnp.float32) * std
        bias = jnp.zeros((D,), dtype=jnp.float32)
        return {'x': x, 'router_w': router_w, 'w1': w1, 'v1': v1, 'w2': w2, 'bias': bias}
    _L1_ffn_all = _L1_ffn_setup()
    _L1_ffn_in = {k: v for k, v in _L1_ffn_all.items() if k in ('router_w', 'w1', 'v1', 'w2', 'bias')}
    del _L1_ffn_all

    def _L2_xattn_setup():
        import jax, jax.numpy as jnp
        import numpy as np
        B, S, D, H = (2, 256, 128, 16)
        HD = D // H

        def _split_heads(x):
            b, s, _ = x.shape
            return x.reshape(b, s, H, HD).transpose(0, 2, 1, 3)
        key = jax.random.key(seed)
        ks = jax.random.split(key, 12)
        init = lambda k, shape: jax.random.normal(k, shape, dtype=jnp.float32) * (1.0 / np.sqrt(shape[0]))
        return {'q': jax.random.normal(ks[0], (B, S, D), dtype=jnp.float32), 'k': jax.random.normal(ks[1], (B, S, D), dtype=jnp.float32), 'v': jax.random.normal(ks[2], (B, S, D), dtype=jnp.float32), 'mask': jnp.zeros((B, 1, S, S), dtype=jnp.float32), 'Wq': init(ks[3], (D, D)), 'bq': jnp.zeros((D,), jnp.float32), 'Wk': init(ks[4], (D, D)), 'bk': jnp.zeros((D,), jnp.float32), 'Wv': init(ks[5], (D, D)), 'bv': jnp.zeros((D,), jnp.float32), 'Wo': init(ks[6], (D, D)), 'bo': jnp.zeros((D,), jnp.float32)}
    _L2_xattn_all = _L2_xattn_setup()
    _L2_xattn_in = {k: v for k, v in _L2_xattn_all.items() if k in ('Wq', 'bq', 'Wk', 'bk', 'Wv', 'bv', 'Wo', 'bo')}
    del _L2_xattn_all

    def _L2_ffn_setup():
        import jax, jax.numpy as jnp
        import numpy as np
        DIM = 128
        HIDDEN = 384
        SCALE = 1.0 / 127.0

        def _dequant(w_int, dtype):
            return w_int.astype(dtype) * jnp.asarray(SCALE, dtype)
        key = jax.random.key(seed)
        k_x, k_g, k_u, k_d = jax.random.split(key, 4)
        x = jax.random.normal(k_x, (4, 256, DIM), dtype=jnp.float32)
        w_gate = jax.random.randint(k_g, (HIDDEN, DIM), -127, 128, dtype=jnp.int32)
        w_up = jax.random.randint(k_u, (HIDDEN, DIM), -127, 128, dtype=jnp.int32)
        w_down = jax.random.randint(k_d, (DIM, HIDDEN), -127, 128, dtype=jnp.int32)
        return {'x': x, 'w_gate': w_gate, 'w_up': w_up, 'w_down': w_down}
    _L2_ffn_all = _L2_ffn_setup()
    _L2_ffn_in = {k: v for k, v in _L2_ffn_all.items() if k in ('w_gate', 'w_up', 'w_down')}
    del _L2_ffn_all

    def _L3_xattn_setup():
        import jax, jax.numpy as jnp
        import numpy as np
        DIM = 128
        NUM_HEADS = 8
        HEAD_DIM = 64
        INNER = NUM_HEADS * HEAD_DIM
        key = jax.random.key(seed)
        ks = jax.random.split(key, 7)
        B, N, M = (8, 64, 512)
        x = jax.random.normal(ks[0], (B, N, DIM), dtype=jnp.float32)
        context = jax.random.normal(ks[1], (B, M, DIM), dtype=jnp.float32)
        s_in = 1.0 / np.sqrt(DIM)
        s_inner = 1.0 / np.sqrt(INNER)
        Wq = jax.random.normal(ks[2], (DIM, INNER), dtype=jnp.float32) * s_in
        Wk = jax.random.normal(ks[3], (DIM, INNER), dtype=jnp.float32) * s_in
        Wv = jax.random.normal(ks[4], (DIM, INNER), dtype=jnp.float32) * s_in
        Wo = jax.random.normal(ks[5], (INNER, DIM), dtype=jnp.float32) * s_inner
        bo = jax.random.normal(ks[6], (DIM,), dtype=jnp.float32) * 0.01
        return {'x': x, 'context': context, 'Wq': Wq, 'Wk': Wk, 'Wv': Wv, 'Wo': Wo, 'bo': bo}
    _L3_xattn_all = _L3_xattn_setup()
    _L3_xattn_in = {k: v for k, v in _L3_xattn_all.items() if k in ('Wq', 'Wk', 'Wv', 'Wo', 'bo')}
    del _L3_xattn_all

    def _L3_ffn_setup():
        import jax, jax.numpy as jnp
        import numpy as np
        TOP_K = 2
        N_GROUP = 4
        TOPK_GROUP = 2
        ROUTED_SCALE = 2.5

        def _gate(xf, gate_w, gate_bias):
            logits = xf.astype(jnp.float32) @ gate_w.astype(jnp.float32)
            scores = jax.nn.sigmoid(logits)
            sfc = scores + gate_bias.astype(jnp.float32)[None]
            T, E = sfc.shape
            e_g = E // N_GROUP
            group_feat = sfc.reshape(T, N_GROUP, e_g)
            group_scores = jax.lax.top_k(group_feat, 2)[0].sum(axis=-1)
            _, group_idx = jax.lax.top_k(group_scores, TOPK_GROUP)
            group_mask = jax.nn.one_hot(group_idx, N_GROUP, dtype=sfc.dtype).sum(axis=1)
            score_mask = jnp.broadcast_to(group_mask[..., None], (T, N_GROUP, e_g)).reshape(T, E)
            tmp_scores = jnp.where(score_mask > 0, sfc, 0.0)
            _, topk_idx = jax.lax.top_k(tmp_scores, TOP_K)
            topk_w = jnp.take_along_axis(sfc, topk_idx, axis=-1)
            topk_w = topk_w / (topk_w.sum(axis=-1, keepdims=True) + 1e-20)
            return (topk_idx, topk_w * ROUTED_SCALE)
        key = jax.random.key(seed)
        ks = jax.random.split(key, 9)
        B, N, H, I, E, SH_I = (2, 128, 128, 64, 8, 128)
        s = lambda k, shape, scale: jax.random.normal(k, shape, jnp.float32) * scale
        return {'x': s(ks[0], (B, N, H), 1.0), 'gate_w': s(ks[1], (H, E), 0.02), 'gate_bias': s(ks[2], (E,), 0.02), 'w_gate': s(ks[3], (E, H, I), 0.02), 'w_up': s(ks[4], (E, H, I), 0.02), 'w_down': s(ks[5], (E, I, H), 0.02), 'sw_gate': s(ks[6], (H, SH_I), 0.02), 'sw_up': s(ks[7], (H, SH_I), 0.02), 'sw_down': s(ks[8], (SH_I, H), 0.02)}
    _L3_ffn_all = _L3_ffn_setup()
    _L3_ffn_in = {k: v for k, v in _L3_ffn_all.items() if k in ('gate_w', 'gate_bias', 'w_gate', 'w_up', 'w_down', 'sw_gate', 'sw_up', 'sw_down')}
    del _L3_ffn_all
    return {'x': x, 'ctx_1024': ctx_1024, 'mask_Bx1xSxS2_ff0': mask_Bx1xSxS2_ff0, 'g_xattn': g_xattn, 'g_ffn': g_ffn, 'L0_xattn_Wq': _L0_xattn_in['Wq'], 'L0_xattn_bq': _L0_xattn_in['bq'], 'L0_xattn_Wkv': _L0_xattn_in['Wkv'], 'L0_xattn_bkv': _L0_xattn_in['bkv'], 'L0_xattn_Wo': _L0_xattn_in['Wo'], 'L0_xattn_bo': _L0_xattn_in['bo'], 'L0_ffn_expert_sel': _L0_ffn_in['expert_sel'], 'L0_ffn_keys': _L0_ffn_in['keys'], 'L0_ffn_values': _L0_ffn_in['values'], 'L0_ffn_route_scale': _L0_ffn_in['route_scale'], 'L1_xattn_Wq': _L1_xattn_in['Wq'], 'L1_xattn_Wk': _L1_xattn_in['Wk'], 'L1_xattn_Wv': _L1_xattn_in['Wv'], 'L1_xattn_gate': _L1_xattn_in['gate'], 'L1_xattn_ln_g': _L1_xattn_in['ln_g'], 'L1_xattn_ln_b': _L1_xattn_in['ln_b'], 'L1_xattn_Wp': _L1_xattn_in['Wp'], 'L1_xattn_bp': _L1_xattn_in['bp'], 'L1_ffn_router_w': _L1_ffn_in['router_w'], 'L1_ffn_w1': _L1_ffn_in['w1'], 'L1_ffn_v1': _L1_ffn_in['v1'], 'L1_ffn_w2': _L1_ffn_in['w2'], 'L1_ffn_bias': _L1_ffn_in['bias'], 'L2_xattn_Wq': _L2_xattn_in['Wq'], 'L2_xattn_bq': _L2_xattn_in['bq'], 'L2_xattn_Wk': _L2_xattn_in['Wk'], 'L2_xattn_bk': _L2_xattn_in['bk'], 'L2_xattn_Wv': _L2_xattn_in['Wv'], 'L2_xattn_bv': _L2_xattn_in['bv'], 'L2_xattn_Wo': _L2_xattn_in['Wo'], 'L2_xattn_bo': _L2_xattn_in['bo'], 'L2_ffn_w_gate': _L2_ffn_in['w_gate'], 'L2_ffn_w_up': _L2_ffn_in['w_up'], 'L2_ffn_w_down': _L2_ffn_in['w_down'], 'L3_xattn_Wq': _L3_xattn_in['Wq'], 'L3_xattn_Wk': _L3_xattn_in['Wk'], 'L3_xattn_Wv': _L3_xattn_in['Wv'], 'L3_xattn_Wo': _L3_xattn_in['Wo'], 'L3_xattn_bo': _L3_xattn_in['bo'], 'L3_ffn_gate_w': _L3_ffn_in['gate_w'], 'L3_ffn_gate_bias': _L3_ffn_in['gate_bias'], 'L3_ffn_w_gate': _L3_ffn_in['w_gate'], 'L3_ffn_w_up': _L3_ffn_in['w_up'], 'L3_ffn_w_down': _L3_ffn_in['w_down'], 'L3_ffn_sw_gate': _L3_ffn_in['sw_gate'], 'L3_ffn_sw_up': _L3_ffn_in['sw_up'], 'L3_ffn_sw_down': _L3_ffn_in['sw_down']}

def reference(x, ctx_1024, mask_Bx1xSxS2_ff0, g_xattn, g_ffn, L0_xattn_Wq, L0_xattn_bq, L0_xattn_Wkv, L0_xattn_bkv, L0_xattn_Wo, L0_xattn_bo, L0_ffn_expert_sel, L0_ffn_keys, L0_ffn_values, L0_ffn_route_scale, L1_xattn_Wq, L1_xattn_Wk, L1_xattn_Wv, L1_xattn_gate, L1_xattn_ln_g, L1_xattn_ln_b, L1_xattn_Wp, L1_xattn_bp, L1_ffn_router_w, L1_ffn_w1, L1_ffn_v1, L1_ffn_w2, L1_ffn_bias, L2_xattn_Wq, L2_xattn_bq, L2_xattn_Wk, L2_xattn_bk, L2_xattn_Wv, L2_xattn_bv, L2_xattn_Wo, L2_xattn_bo, L2_ffn_w_gate, L2_ffn_w_up, L2_ffn_w_down, L3_xattn_Wq, L3_xattn_Wk, L3_xattn_Wv, L3_xattn_Wo, L3_xattn_bo, L3_ffn_gate_w, L3_ffn_gate_bias, L3_ffn_w_gate, L3_ffn_w_up, L3_ffn_w_down, L3_ffn_sw_gate, L3_ffn_sw_up, L3_ffn_sw_down):
    import jax
    import jax.numpy as jnp

    def _L0_xattn_ref(x, y, Wq, bq, Wkv, bkv, Wo, bo):
        import jax, jax.numpy as jnp
        import numpy as np
        DIM = 128
        NUM_HEADS = 16
        HEAD_DIM = DIM // NUM_HEADS
        B, N, C = x.shape
        B2, N2, _ = y.shape
        H, hd = (NUM_HEADS, HEAD_DIM)
        scaling = hd ** (-0.5)
        q = (x @ Wq + bq).reshape(B, N, H, hd).transpose(0, 2, 1, 3)
        kv = (y @ Wkv + bkv).reshape(B2, N2, 2, H, hd).transpose(0, 3, 2, 1, 4)
        k, v = (kv[:, :, 0], kv[:, :, 1])
        attn = jnp.einsum('bhnd,bhmd->bhnm', q * scaling, k)
        attn = jax.nn.softmax(attn, axis=-1)
        out = jnp.einsum('bhnm,bhmd->bhnd', attn, v)
        out = out.transpose(0, 2, 1, 3).reshape(B, N, C)
        return out @ Wo + bo

    def _L0_ffn_ref(x, expert_sel, keys, values, route_scale):
        import jax, jax.numpy as jnp
        import numpy as np
        DMODEL = 128
        N_EXPERTS = 16
        EXPERT_SIZE = 32
        K = 4
        sel_logits = jnp.einsum('btd,ed->bte', x, expert_sel)
        sel_probs = jax.nn.sigmoid(sel_logits)
        _, sel_index = jax.lax.top_k(sel_probs, K)
        sel_val = jnp.take_along_axis(sel_probs, sel_index, axis=-1)
        sel_val = sel_val / jnp.clip(sel_val.sum(-1, keepdims=True), 1e-09)
        sel_val = sel_val * route_scale
        scores_all = jax.nn.relu(jnp.einsum('btd,edh->bteh', x, keys))
        values_all = jnp.einsum('bteh,ehv->btev', scores_all, values)
        sel_idx_exp = sel_index[..., None]
        selected = jnp.take_along_axis(values_all, sel_idx_exp, axis=2)
        out = (selected * sel_val[..., None]).sum(axis=2)
        return out

    def _L1_xattn_ref(x, x_text, Wq, Wk, Wv, gate, ln_g, ln_b, Wp, bp):
        import jax, jax.numpy as jnp
        import numpy as np
        B, N, P, DIM, H = (8, 128, 77, 128, 16)
        HD = DIM // H
        LN_EPS = 1e-05
        b, n, c = x.shape
        h = gate.shape[1]
        q = x @ Wq.T
        k = jnp.concatenate([x_text @ Wk.T, x @ Wk.T], axis=1)
        v = jnp.concatenate([x_text @ Wv.T, x @ Wv.T], axis=1)
        kv = k.shape[1]
        q = q.reshape(b, n, h, -1).transpose(0, 2, 1, 3)
        k = k.reshape(b, kv, h, -1).transpose(0, 2, 1, 3)
        v = v.reshape(b, kv, h, -1).transpose(0, 2, 1, 3)
        d = q.shape[-1]
        scores = jnp.einsum('bhnd,bhkd->bhnk', q, k) / jnp.sqrt(jnp.float32(d))
        first = jnp.tanh(gate) * jnp.ones_like(scores[..., :1])
        rest = jax.nn.softmax(scores[..., 1:], axis=-1)
        attn = jnp.concatenate([first, rest], axis=-1)
        out = jnp.einsum('bhnk,bhkd->bhnd', attn, v)
        out = out.transpose(0, 2, 1, 3).reshape(b, n, -1)
        out = out.astype(jnp.bfloat16).astype(jnp.float32)
        mu = jnp.mean(out, axis=-1, keepdims=True)
        var = jnp.var(out, axis=-1, keepdims=True)
        out = (out - mu) / jnp.sqrt(var + LN_EPS) * ln_g + ln_b
        return out @ Wp.T + bp

    def _L1_ffn_ref(x, router_w, w1, v1, w2, bias):
        import jax, jax.numpy as jnp
        import numpy as np
        D = 128
        F = 352
        E = 8
        TOP_K = 2
        B, S, d = x.shape
        xt = x.reshape(B * S, d)
        scores = jax.nn.softmax(xt @ router_w, axis=-1)
        expert_weights, expert_idx = jax.lax.top_k(scores, TOP_K)
        h = jax.nn.gelu(jnp.einsum('td,edf->tef', xt, w1), approximate=False) * jnp.einsum('td,edf->tef', xt, v1)
        y = jnp.einsum('tef,efd->ted', h, w2)
        yk = jnp.take_along_axis(y, expert_idx[:, :, None], axis=1)
        out = jnp.sum(expert_weights[:, :, None] * yk, axis=1) + bias
        return out.reshape(B, S, d)

    def _L2_xattn_ref(q, k, v, mask, Wq, bq, Wk, bk, Wv, bv, Wo, bo):
        import jax, jax.numpy as jnp
        import numpy as np
        B, S, D, H = (2, 256, 128, 16)
        HD = D // H

        def _split_heads(x):
            b, s, _ = x.shape
            return x.reshape(b, s, H, HD).transpose(0, 2, 1, 3)
        qh = _split_heads(q @ Wq + bq)
        kh = _split_heads(k @ Wk + bk)
        vh = _split_heads(v @ Wv + bv)
        scores = jnp.einsum('bhqd,bhkd->bhqk', qh, kh) / jnp.sqrt(jnp.float32(D))
        scores = scores + mask * -1000000000.0
        attn = jax.nn.softmax(scores, axis=-1)
        out = jnp.einsum('bhqk,bhkd->bhqd', attn, vh)
        out = out.transpose(0, 2, 1, 3).reshape(q.shape[0], -1, D)
        return out @ Wo + bo

    def _L2_ffn_ref(x, w_gate, w_up, w_down):
        import jax, jax.numpy as jnp
        import numpy as np
        DIM = 128
        HIDDEN = 384
        SCALE = 1.0 / 127.0

        def _dequant(w_int, dtype):
            return w_int.astype(dtype) * jnp.asarray(SCALE, dtype)
        wg = _dequant(w_gate, x.dtype)
        wu = _dequant(w_up, x.dtype)
        wd = _dequant(w_down, x.dtype)
        gate = jnp.einsum('bsd,hd->bsh', x, wg)
        up = jnp.einsum('bsd,hd->bsh', x, wu)
        h = jax.nn.silu(gate) * up
        return jnp.einsum('bsh,dh->bsd', h, wd)

    def _L3_xattn_ref(x, context, Wq, Wk, Wv, Wo, bo):
        import jax, jax.numpy as jnp
        import numpy as np
        DIM = 128
        NUM_HEADS = 8
        HEAD_DIM = 64
        INNER = NUM_HEADS * HEAD_DIM
        B, N, _ = x.shape
        M = context.shape[1]
        scale = HEAD_DIM ** (-0.5)
        q = (x @ Wq).reshape(B, N, NUM_HEADS, HEAD_DIM).transpose(0, 2, 1, 3)
        k = (context @ Wk).reshape(B, M, NUM_HEADS, HEAD_DIM).transpose(0, 2, 1, 3)
        v = (context @ Wv).reshape(B, M, NUM_HEADS, HEAD_DIM).transpose(0, 2, 1, 3)
        attn = jax.nn.softmax(jnp.einsum('bhnd,bhmd->bhnm', q, k) * scale, axis=-1)
        out = jnp.einsum('bhnm,bhmd->bhnd', attn, v)
        out = out.transpose(0, 2, 1, 3).reshape(B, N, INNER)
        return out @ Wo + bo

    def _L3_ffn_ref(x, gate_w, gate_bias, w_gate, w_up, w_down, sw_gate, sw_up, sw_down):
        import jax, jax.numpy as jnp
        import numpy as np
        TOP_K = 2
        N_GROUP = 4
        TOPK_GROUP = 2
        ROUTED_SCALE = 2.5

        def _gate(xf, gate_w, gate_bias):
            logits = xf.astype(jnp.float32) @ gate_w.astype(jnp.float32)
            scores = jax.nn.sigmoid(logits)
            sfc = scores + gate_bias.astype(jnp.float32)[None]
            T, E = sfc.shape
            e_g = E // N_GROUP
            group_feat = sfc.reshape(T, N_GROUP, e_g)
            group_scores = jax.lax.top_k(group_feat, 2)[0].sum(axis=-1)
            _, group_idx = jax.lax.top_k(group_scores, TOPK_GROUP)
            group_mask = jax.nn.one_hot(group_idx, N_GROUP, dtype=sfc.dtype).sum(axis=1)
            score_mask = jnp.broadcast_to(group_mask[..., None], (T, N_GROUP, e_g)).reshape(T, E)
            tmp_scores = jnp.where(score_mask > 0, sfc, 0.0)
            _, topk_idx = jax.lax.top_k(tmp_scores, TOP_K)
            topk_w = jnp.take_along_axis(sfc, topk_idx, axis=-1)
            topk_w = topk_w / (topk_w.sum(axis=-1, keepdims=True) + 1e-20)
            return (topk_idx, topk_w * ROUTED_SCALE)
        B, N, H = x.shape
        xf = x.reshape(-1, H)
        topk_idx, topk_w = _gate(xf, gate_w, gate_bias)
        g = jax.nn.silu(jnp.einsum('th,ehi->tei', xf, w_gate))
        u = jnp.einsum('th,ehi->tei', xf, w_up)
        experts_y = jnp.einsum('tei,eih->teh', g * u, w_down)
        masked_y = jnp.take_along_axis(experts_y, topk_idx[:, :, None], axis=1)
        y = jnp.einsum('tkh,tk->th', masked_y, topk_w.astype(x.dtype)).reshape(B, N, H)
        shared = jax.nn.silu(x @ sw_gate) * (x @ sw_up) @ sw_down
        return y + shared
    x = x + jnp.tanh(g_xattn[0]) * _L0_xattn_ref(_layernorm(x, axis=-1), ctx_1024, L0_xattn_Wq, L0_xattn_bq, L0_xattn_Wkv, L0_xattn_bkv, L0_xattn_Wo, L0_xattn_bo)
    x = x + jnp.tanh(g_ffn[0]) * _L0_ffn_ref(_layernorm(x, axis=-1), L0_ffn_expert_sel, L0_ffn_keys, L0_ffn_values, L0_ffn_route_scale)
    x = x + jnp.tanh(g_xattn[1]) * _L1_xattn_ref(_layernorm(x, axis=-1), ctx_1024, L1_xattn_Wq, L1_xattn_Wk, L1_xattn_Wv, L1_xattn_gate, L1_xattn_ln_g, L1_xattn_ln_b, L1_xattn_Wp, L1_xattn_bp)
    x = x + jnp.tanh(g_ffn[1]) * _L1_ffn_ref(_layernorm(x, axis=-1), L1_ffn_router_w, L1_ffn_w1, L1_ffn_v1, L1_ffn_w2, L1_ffn_bias)
    x = x + jnp.tanh(g_xattn[2]) * _L2_xattn_ref(_layernorm(x, axis=-1), ctx_1024, ctx_1024, mask_Bx1xSxS2_ff0, L2_xattn_Wq, L2_xattn_bq, L2_xattn_Wk, L2_xattn_bk, L2_xattn_Wv, L2_xattn_bv, L2_xattn_Wo, L2_xattn_bo)
    x = x + jnp.tanh(g_ffn[2]) * _L2_ffn_ref(_layernorm(x, axis=-1), L2_ffn_w_gate, L2_ffn_w_up, L2_ffn_w_down)
    x = x + jnp.tanh(g_xattn[3]) * _L3_xattn_ref(_layernorm(x, axis=-1), ctx_1024, L3_xattn_Wq, L3_xattn_Wk, L3_xattn_Wv, L3_xattn_Wo, L3_xattn_bo)
    x = x + jnp.tanh(g_ffn[3]) * _L3_ffn_ref(_layernorm(x, axis=-1), L3_ffn_gate_w, L3_ffn_gate_bias, L3_ffn_w_gate, L3_ffn_w_up, L3_ffn_w_down, L3_ffn_sw_gate, L3_ffn_sw_up, L3_ffn_sw_down)
    return x

_drawn_inputs = setup_inputs


def setup_inputs(seed=0):
    import zlib

    import numpy as np

    out = dict(_drawn_inputs(seed))
    spreads = {'L0_xattn_bq': (0.0, 0.291),
     'L0_xattn_bkv': (0.0, 0.1),
     'L0_xattn_bo': (0.0, 0.1),
     'L1_xattn_ln_g': (1.0, 0.2),
     'L1_xattn_ln_b': (0.0, 0.301),
     'L1_xattn_bp': (0.0, 0.1),
     'L1_ffn_bias': (0.0, 0.1),
     'L2_xattn_bq': (0.0, 2.0),
     'L2_xattn_bk': (0.0, 2.0),
     'L2_xattn_bv': (0.0, 0.1),
     'L2_xattn_bo': (0.0, 0.1)}
    factors = {'g_ffn': 8.0,
     'L1_xattn_Wq': 8.0,
     'L1_xattn_Wk': 8.0,
     'L1_ffn_router_w': 8.0,
     'L1_ffn_w1': 8.0,
     'L1_ffn_v1': 8.0,
     'L1_ffn_w2': 8.0,
     'L3_xattn_Wq': 8.0,
     'L3_xattn_Wk': 8.0,
     'L3_xattn_Wv': 8.0,
     'L3_xattn_Wo': 8.0,
     'L3_xattn_bo': 64.0,
     'L3_ffn_gate_w': 38.894,
     'L3_ffn_gate_bias': 56.386,
     'L3_ffn_w_gate': 35.243,
     'L3_ffn_w_up': 31.482,
     'L3_ffn_w_down': 31.858,
     'L3_ffn_sw_gate': 45.559,
     'L3_ffn_sw_up': 39.657,
     'L3_ffn_sw_down': 40.347,
     'L2_xattn_Wq': 3.089}
    for name, (base, spread) in spreads.items():
        noise = np.random.default_rng([zlib.crc32(name.encode()), seed]).standard_normal(out[name].shape)
        drawn = base * np.exp(spread * noise) if base else spread * noise
        out[name] = jnp.asarray(drawn.astype(out[name].dtype))
    for name, factor in factors.items():
        out[name] = (out[name] * factor).astype(out[name].dtype)
    return out
```

```python
from contextlib import ExitStack

import concourse.bass as bass
from concourse import mybir

F32 = mybir.dt.float32
F32R = mybir.dt.float32r
BF16 = mybir.dt.bfloat16
I32 = mybir.dt.int32
ALU = mybir.AluOpType
ACT = mybir.ActivationFunctionType
AX_X = mybir.AxisListType.X

P = 128
B, S, D, S2 = 8, 256, 128, 64
NT = B * S // P
LN_EPS = 1e-5
H, HD = 16, 8
NG, GH = 4, 4
H3, HD3 = 8, 64
E0, K0, X0 = 16, 4, 32
E1, K1, X1 = 8, 2, 352
HID2 = 384
E3, K3, X3 = 8, 2, 64
NG3 = 4
SC3 = 2.5
TOK = 512
NI = B * S // TOK
LOWEST = -1e30

CONST = {}
_at = 0
for _name, _n in (("ident", 128), ("aq", 1), ("ak", 1), ("am", 1), ("amask", 1), ("a8", 1), ("a16", 1), ("half", 2), ("head4", 4),
                  ("selc", 256), ("selc0", 256), ("negs", 128), ("i2", 128), ("self0", 512), ("self3", 512), ("e8", 8),
                  ("onesb", 128)):
    CONST[_name] = (_at, _n)
    _at += _n
NCONST = _at


def need(eng, sem, value):
    if isinstance(value, int) and value <= 0:
        return
    eng.wait_ge(sem, value)


def settled(dve, sem):
    dve.sem_inc(sem["settled"], 1)


class Program:

    def __init__(self, nc, ctx, ins, out):
        self.nc, self.ins, self.out = nc, ins, out
        self.ctx = ctx
        sb = self.sb
        self.x = sb("x", [P, NT, D], F32)
        self.const = sb("const", [P, NCONST], F32)
        self.ctx_t2 = sb("ctx_t2", [P, B, 2, S2], F32)
        self.ctx_hi = sb("ctx_hi", [P, B * S2], F32R)
        self.ctx_lo = sb("ctx_lo", [P, B * S2], F32R)
        self.gates = sb("gates", [P, 8], F32)
        self.w_att = sb("w_att", [P, 3, 4, D], F32)
        self.big_hi = sb("big_hi", [P, 8704], F32R)
        self.big_lo = sb("big_lo", [P, 8704], F32R)
        self.eps = sb("eps", [P, 2], F32)
        self.neg_half = sb("neg_half", [P, 2], F32)
        self.bank = [ctx.enter_context(nc.psum_tensor(f"bank{i}", [P, 512], F32)) for i in range(8)]
        self.nsem = 0

    def sb(self, name, shape, dt):
        return self.ctx.enter_context(self.nc.sbuf_tensor(name, shape, dt))

    def sem(self, name):
        self.nsem += 1
        return self.nc.alloc_semaphore(name=f"s{self.nsem}_{name}")

    def sems(self, *names):
        return {name: self.sem(name) for name in names}

    def c(self, name):
        a, n = CONST[name]
        return self.const[:, a:a + n]

    def id(self, n=P):
        return self.const[0:n, 0:n]


def tiles(b, n):
    return bass.ds(b * n, n)



def setup(pr):
    nc, ins = pr.nc, pr.ins
    with nc.cleanup_on_exit(), ExitStack() as scope:
        tmp = scope.enter_context(nc.sbuf_tensor("ctx_rows", [P, 4, D], F32))
        x_in, const_in, ctx_in, g_in, w_in = (pr.sem(n) for n in ("x_in", "const_in", "ctx_in", "g_in", "w_in"))
        eps_set, ctx_turned, ctx_hi, ctx_lo = (pr.sem(n) for n in ("eps_set", "ctx_turned", "ctx_hi", "ctx_lo"))
        turn = pr.bank[0]
        with nc.Block() as block:
            @block.sync
            def _(sp):
                sp.dma_start(pr.const[:], ins["const"]).then_inc(const_in, 16)
                sp.dma_start(tmp[:], ins["ctx_1024"].rearrange("(a b) s d -> (b s) a d", b=2)).then_inc(ctx_in, 16)
                xv = ins["x"].rearrange("b (t p) d -> p (b t) d", p=P)
                for h in range(2):
                    sp.dma_start(pr.x[:, 8 * h:8 * h + 8], xv[:, 8 * h:8 * h + 8]).then_inc(x_in, 16)
                sp.dma_start(pr.gates[:, 0:4], ins["g_xattn"].partition_broadcast(P)).then_inc(g_in, 16)
                sp.dma_start(pr.gates[:, 4:8], ins["g_ffn"].partition_broadcast(P)).then_inc(g_in, 16)
                w = pr.w_att
                for dst, src in (
                        (w[:, 0, 0], ins["L0_xattn_Wq"]), (w[:, 0, 1:3], ins["L0_xattn_Wkv"].rearrange("p (a n) -> p a n", a=2)),
                        (w[:, 0, 3], ins["L0_xattn_Wo"]),
                        (w[:, 1, 0], ins["L1_xattn_Wq"]), (w[:, 1, 1], ins["L1_xattn_Wk"]),
                        (w[:, 1, 2], ins["L1_xattn_Wv"]), (w[:, 1, 3], ins["L1_xattn_Wp"]),
                        (w[:, 2, 0], ins["L2_xattn_Wq"]), (w[:, 2, 1], ins["L2_xattn_Wk"]),
                        (w[:, 2, 2], ins["L2_xattn_Wv"]), (w[:, 2, 3], ins["L2_xattn_Wo"])):
                    sp.dma_start(dst, src).then_inc(w_in, 16)
                sp.wait_ge(x_in, 32)
                sp.wait_ge(w_in, 11 * 16)

            @block.tensor
            def _(pe):
                pe.wait_ge(const_in, 16)
                pe.wait_ge(ctx_in, 16)
                for a in range(4):
                    last = pe.transpose(turn[:, a * P:(a + 1) * P], tmp[:, a], pr.id())
                last.then_inc(ctx_turned, 1)

            @block.scalar
            def _(act):
                act.wait_ge(g_in, 32)
                act.activation(pr.gates[:], pr.gates[:], ACT.Tanh)
                act.wait_ge(ctx_turned, 1)
                act.copy(pr.ctx_hi[:], turn[:]).then_inc(ctx_hi, 1)

            @block.vector
            def _(dve):
                dve.memset(pr.eps[:], LN_EPS)
                dve.memset(pr.neg_half[:], -0.5)
                dve.wait_ge(ctx_hi, 1)
                turned = turn[:].rearrange("p (b s) -> p b s", s=S2)
                dve.tensor_tensor(pr.ctx_lo[:], turn[:], pr.ctx_hi[:].bitcast(F32), ALU.subtract)
                dve.tensor_copy(pr.ctx_t2[:], turned.unsqueeze(2).to_broadcast([P, B, 2, S2]))



def attention(pr, layer, own_keys, masked, biased, scale, extra=None):
    nc, ins = pr.nc, pr.ins
    gated = own_keys
    n = f"L{layer}"
    NS = 5 if own_keys else 1
    U = NG * NS
    MASK_SCALE = -1e9 / scale
    with nc.cleanup_on_exit(), ExitStack() as scope:
        def sb(name, shape, dt=F32):
            return scope.enter_context(nc.sbuf_tensor(f"{n}_{name}", shape, dt))

        wf = sb("wf", [P, 4, D]) if gated else None
        wx = sb("wx", [P, 4, NG * P], F32R)
        kc_all = sb("kc_all", [P, NG, B, S2], F32R)
        kc = sb("kc", [P, NG, GH, S2], F32R)
        vc_all = sb("vc_all", [P, B, D])
        vc = sb("vc", [P, H // 2, 32])
        bias_row = sb("bias_row", [1, 4, D]) if biased else None
        bias_x = sb("bias_x", [1, 2, NG * P]) if biased else None
        bias_c = sb("bias_c", [P, 2, NG])
        bias_ca = sb("bias_ca", [P, 2, NG])
        ones1 = sb("ones1", [1, P])
        hk = sb("hk", [P, 512])
        bo = sb("bo", [P, D])
        selc = sb("selc", [P, 2, P], F32R)
        st6 = sb("st6", [P, 2, 6])
        mv = sb("mv", [P, 2, 2])
        ve = sb("ve", [P, 2])
        rstd = sb("rstd", [P, 2])
        xn = sb("xn", [P, 2, D])
        xt_hi = sb("xt_hi", [P, S], F32R)
        xt_lo = sb("xt_lo", [P, S], F32R)
        part = sb("part", [P, 2, S])
        q = sb("q", [P, NG, S], F32R)
        mc = sb("mc", [P, 2, GH])
        mx = sb("mx", [P, 2, 2, GH, 32])
        hm = sb("hm", [P, S])
        mt = sb("mt", [P, 2, S], F32R)
        pt = sb("pt", [P, 2, 2 * NS, 512])
        ot = sb("ot", [P, 2, S])
        rc = sb("rc", [P, 2 * H])
        on = sb("on", [P, 2, D])
        o2t = sb("o2t", [P, S])
        if own_keys:
            xt_raw = sb("xt_raw", [P, S])
            k = sb("k", [P, NG, S], F32R)
            ms = sb("ms", [P, 2, GH])
            vs = sb("vs", [P, 2, H, 32])
            negs = sb("negs", [P, P], F32R)
            gate_row = sb("gate_row", [P, H])
            wvg = sb("wvg", [P, D])
            vg_all = sb("vg_all", [P, B, D])
            ln_gb = sb("ln_gb", [P, 2])
            o16 = sb("o16", [P, 2, D], BF16)
            st6b = sb("st6b", [P, 2, 6])
            mvb = sb("mvb", [P, 2, 2])
            veb = sb("veb", [P, 2])
            rstdb = sb("rstdb", [P, 2])
            raw = sb("raw", [P, 1, 1088])
        if masked:
            mask2 = sb("mask2", [P, NT, 2, S2])
            mk = sb("mk", [P, 2, P])
            hmk = sb("hmk", [P, S])
            msk = sb("msk", [P, S], F32R)
            i2 = sb("i2", [P, P], F32R)
        if layer == 0:
            raw0 = sb("raw0", [P, 2, 512])

        sem = pr.sems("loaded", "prep_pe", "prep_act", "prep_dve", "settled", "prep_pool", "stats", "moments", "var_eps",
                     "rstd", "xn_ready", "xn_turned", "xt_hi", "xt_lo", "proj_done", "proj_hi", "qk_split", "kc_ready",
                     "sc_done", "sc_taken", "m_ready", "m_turned", "m_hi", "m_split", "st_done", "exp_done", "v_proj",
                     "v_ready", "vc_ready", "pv_done", "ot_taken", "o_turned", "rc_ready", "o_norm", "o_stats", "o_moments", "o_round",
                     "o_var", "o_rstd", "on_ready", "on_turned", "o2t_ready", "y_done", "x_bias", "x_done", "mk_ready",
                     "mk_turned", "mk_hi", "mk_split", "stage_in", "stage_hi", "stage_split", "w0_in")
        mask_a = sb("mask_a", [P, 1])
        DVE_WEIGHTS = 10 if biased else 7
        DVE_READY = DVE_WEIGHTS + 4 + (5 if gated else 0) + 1 + (2 if masked else 0)
        ACT_READY = 6 + (4 if gated else 0)
        POOL_READY = 6 + (7 if gated else 0)
        LOADED = 16 * {0: 4, 1: 4, 2: 7}[layer]
        on_ready = sem["on_ready"] if gated else sem["o_norm"]
        b_proj, b_turn, b_sc, b_st, b_mt, b_o = (pr.bank[0], pr.bank[1], pr.bank[2:4], pr.bank[4:6], pr.bank[6], pr.bank[7])
        w = [wf[:, i] if gated else pr.w_att[:, layer, i] for i in range(4)]
        w_raw = [pr.w_att[:, layer, i] for i in range(4)]
        tg = pr.gates[:, layer:layer + 1]

        first = [("norm", 0), ("scale", 0), ("turn", 0), ("mask", 0)] + [s for g in range(NG) for s in (("proj", 0, g), ("keys", 0, g))] \
            + [("scores", 0, 0)]

        def order(b):
            steps = []
            more = not (isinstance(b, int) and b == B - 1)
            late = not (isinstance(b, int) and b == 0)
            if late:
                steps += [("pv", b - 1, 1)]
            steps += [("maxima", b, 0), ("scores", b, 1)]
            if late:
                steps += [("o_turn", b - 1)]
            steps += [("values", b), ("weights", b, 0)]
            if more:
                steps += [("norm", b + 1)]
            if late:
                steps += [("o_norm", b - 1)]
            steps += [("maxima", b, 1), ("scores", b, 2), ("weights", b, 1)]
            if more:
                steps += [("scale", b + 1)]
            if late:
                steps += [("o_scale", b - 1), ("on_turn", b - 1)]
            steps += [("maxima", b, 2), ("pv", b, 0), ("scores", b, 3)]
            if late:
                steps += [("y", b - 1)]
            steps += [("weights", b, 2)]
            if more:
                steps += [("turn", b + 1)]
            steps += [("maxima", b, 3)]
            if more:
                steps += [s for g in (0, 1, 2) for s in (("proj", b + 1, g), ("keys", b + 1, g))]
            steps += [("weights", b, 3)]
            if more:
                steps += [("mask", b + 1), ("proj", b + 1, 3), ("keys", b + 1, 3), ("scores", b + 1, 0)]
            return steps

        flush = [("pv", B - 1, 1), ("o_turn", B - 1), ("o_norm", B - 1), ("o_scale", B - 1), ("on_turn", B - 1), ("y", B - 1)]

        def passes(eng, does):
            def run(steps):
                for step, *at in steps:
                    if step in does:
                        does[step](*at)
            run(first)
            run(order(0))
            run(order(1))
            with eng.Fori(2, B - 1) as b:
                run(order(b))
            run(order(B - 1))
            run(flush)

        with nc.Block() as block:
            @block.sync
            def _(sp):
                if biased:
                    names = {0: ("L0_xattn_bq", "L0_xattn_bkv", "L0_xattn_bo"), 2: ("L2_xattn_bq", "L2_xattn_bk", "L2_xattn_bv", "L2_xattn_bo")}[layer]
                    at = 0
                    for name in names:
                        m = ins[name].shape[0]
                        sp.dma_start(bias_row[0:1, :, :].rearrange("a r d -> a (r d)")[:, at:at + m],
                                     ins[name].rearrange("(a n) -> a n", a=1)).then_inc(sem["loaded"], 16)
                        at += m
                    total = 16 * len(names)
                else:
                    total = 0
                sp.dma_start(bo[:], ins[{0: "L0_xattn_bo", 1: "L1_xattn_bp", 2: "L2_xattn_bo"}[layer]].partition_broadcast(P)).then_inc(sem["loaded"], 16)
                if gated:
                    sp.dma_start(gate_row[:], ins["L1_xattn_gate"].rearrange("a h b c -> (a h b c)").partition_broadcast(P)).then_inc(sem["loaded"], 16)
                    sp.dma_start(ln_gb[:, 0:1], ins["L1_xattn_ln_g"].rearrange("(p a) -> p a", a=1)).then_inc(sem["loaded"], 16)
                    sp.dma_start(ln_gb[:, 1:2], ins["L1_xattn_ln_b"].rearrange("(p a) -> p a", a=1)).then_inc(sem["loaded"], 16)
                if masked:
                    for h in range(2):
                        sp.dma_start(mask2[:, :, h], ins["mask_Bx1xSxS2_ff0"].rearrange("b a (t p) s -> p (b a t) s", p=P)).then_inc(sem["loaded"], 16)
                if layer == 0:
                    sp.dma_start(raw0[:, 0].rearrange("p (e h) -> p e h", e=E0), ins["L0_ffn_keys"].rearrange("e p h -> p e h")).then_inc(sem["w0_in"], 16)
                    sp.dma_start(raw0[:, 1].rearrange("p (c v) -> p c v", c=4),
                                 ins["L0_ffn_values"].rearrange("(c e) h v -> (e h) c v", e=4)).then_inc(sem["w0_in"], 16)
                if own_keys:
                    def expert(e):
                        dst = raw[:, 0]
                        es = bass.ds(e, 1)
                        sp.dma_start(dst[:, 0:352].unsqueeze(1), ins["L1_ffn_w1"][es].rearrange("e p f -> p e f")).then_inc(sem["stage_in"], 16)
                        sp.dma_start(dst[:, 352:704].unsqueeze(1), ins["L1_ffn_v1"][es].rearrange("e p f -> p e f")).then_inc(sem["stage_in"], 16)
                        sp.dma_start(dst[:, 704:960].rearrange("p (e k v) -> p e k v", e=1, k=2),
                                     ins["L1_ffn_w2"][es, 0:256].rearrange("e (k p) v -> p e k v", p=P)).then_inc(sem["stage_in"], 16)
                        sp.dma_start(dst[0:96, 960:1088].unsqueeze(1), ins["L1_ffn_w2"][es, 256:352].rearrange("e p v -> p e v")).then_inc(sem["stage_in"], 16)
                    expert(0)
                    with sp.Fori(0, B - 1) as e:
                        sp.wait_ge(sem["stage_split"], e + 1)
                        expert(e + 1)

            @block.gpsimd
            def _(pool):
                pool.memset(mx[:], 0.0).then_inc(sem["prep_pool"], 1)
                pool.memset(kc[:].bitcast(F32), 0.0).then_inc(sem["prep_pool"], 1)
                pool.memset(vc[:], 0.0).then_inc(sem["prep_pool"], 1)
                pool.wait_ge(sem["prep_pool"], 3)
                pool.memset(vc[0:64, :, 8:9], 1.0).then_inc(sem["prep_pool"], 1)
                pool.wait_ge(sem["prep_pool"], 4)
                pool.memset(vc[64:128, :, 24:25], 1.0).then_inc(sem["prep_pool"], 1)
                pool.wait_ge(sem["prep_pool"], 5)
                if own_keys:
                    pool.memset(vs[:], 0.0).then_inc(sem["prep_pool"], 1)
                    pool.wait_ge(sem["prep_pool"], 6)
                    by_pair = vs[:].rearrange("p k (a s) c -> p k a s c", s=2)
                    for kt in range(2):
                        pool.memset(by_pair[:, kt, :, 0, 8:9], 1.0).then_inc(sem["prep_pool"], 1)
                        pool.memset(by_pair[:, kt, :, 1, 24:25], 1.0).then_inc(sem["prep_pool"], 1)
                    pool.wait_ge(sem["prep_pool"], 10)
                    for r, row in enumerate((0, 64)):
                        pool.memset(vc[row:row + 1], 0.0).then_inc(sem["prep_pool"], 1)
                        pool.wait_ge(sem["prep_pool"], 11 + r)
                pool.wait_ge(sem["loaded"], LOADED)
                pool.tensor_scalar(bo[:], bo[:], tg, None, ALU.mult).then_inc(sem["prep_pool"], 1)
                pool.wait_ge(sem["prep_dve"], DVE_READY)
                pool.wait_ge(sem["prep_act"], ACT_READY)

                def norm(b):
                    pool.wait_ge(sem["moments"], b + 1)
                    pool.tensor_tensor(ve[:], mv[:, :, 1], pr.eps[:], ALU.add).then_inc(sem["var_eps"], 1)
                    pool.wait_ge(sem["var_eps"], b + 1)
                    pool.tensor_tensor(rstd[:], ve[:], pr.neg_half[:], ALU.pow).then_inc(sem["rstd"], 1)

                def turn(b):
                    pool.wait_ge(sem["xn_ready"], b + 1)
                    xb = pr.x[:, tiles(b, 2)]
                    pool.tensor_tensor(xb, xb, bo[:].unsqueeze(1).to_broadcast([P, 2, D]), ALU.add).then_inc(sem["x_bias"], 1)

                def keys(b, g):
                    need(pool, sem["st_done"], b * U + (g + 1) * NS - U)
                    pool.tensor_tensor(kc[:, g], kc_all[:, g, bass.ds(b, 1)].bitcast(F32).to_broadcast([P, GH, S2]),
                                       pr.c("head4").unsqueeze(2).to_broadcast([P, GH, S2]), ALU.mult).then_inc(sem["kc_ready"], 1)

                def values(b):
                    need(pool, sem["pv_done"], b * 2)
                    src = vc_all[:, bass.ds(b, 1)].rearrange("p e (a s d) -> p (e a) s d", s=2, d=HD)
                    for s in range(2):
                        last = pool.tensor_tensor(vc[:, :, 16 * s:16 * s + HD], src[:, :, s],
                                                  pr.c("half")[:, s:s + 1].unsqueeze(2).to_broadcast([P, H // 2, HD]), ALU.mult)
                    last.then_inc(sem["vc_ready"], 1)
                    if layer == 0 and isinstance(b, int) and b == 0:
                        split0()
                    if own_keys:
                        split(b)

                def split0():
                    pool.wait_ge(sem["w0_in"], 32)
                    for i in range(2):
                        part_of = slice(512 * i, 512 * i + 512)
                        pool.tensor_copy(pr.big_hi[:, part_of], raw0[:, i]).then_inc(sem["stage_hi"], 1)
                        pool.wait_ge(sem["stage_hi"], i + 1)
                        pool.tensor_tensor(pr.big_lo[:, part_of], raw0[:, i], pr.big_hi[:, part_of].bitcast(F32), ALU.subtract)

                def split(e):
                    pool.wait_ge(sem["stage_in"], e * 64 + 64)
                    for dst, op, in1 in ((pr.big_hi, None, None), (pr.big_lo, ALU.subtract, pr.big_hi)):
                        if op is not None:
                            pool.wait_ge(sem["stage_hi"], e + 1)
                        for rows, a, m, at in ((P, 0, 352, e * 352), (P, 352, 352, e * 352 + 2816), (P, 704, 256, e * 384 + 5632),
                                               (96, 960, 128, e * 384 + 5632 + 256)):
                            o = dst[0:rows, bass.ds(at, m)]
                            i0 = raw[0:rows, 0, a:a + m]
                            if op is None:
                                last = pool.tensor_copy(o, i0)
                            else:
                                last = pool.tensor_tensor(o, i0, in1[0:rows, bass.ds(at, m)].bitcast(F32), op)
                        last.then_inc(sem["stage_hi"] if op is None else sem["stage_split"], 1)

                def mask(b):
                    if masked:
                        need(pool, sem["mk_turned"], b)
                        pool.tensor_copy(mk[:], mask2[:, tiles(b, 2)].rearrange("p t h s -> p t (h s)")).then_inc(sem["mk_ready"], 1)

                def o_norm(b):
                    if gated:
                        pool.wait_ge(sem["o_moments"], b + 1)
                        pool.tensor_tensor(veb[:], mvb[:, :, 1], pr.eps[:], ALU.add).then_inc(sem["o_var"], 1)
                        pool.wait_ge(sem["o_var"], b + 1)
                        pool.tensor_tensor(rstdb[:], veb[:], pr.neg_half[:], ALU.pow).then_inc(sem["o_rstd"], 1)

                passes(pool, {"norm": norm, "turn": turn, "keys": keys, "values": values, "mask": mask, "o_norm": o_norm})

            @block.tensor
            def _(pe):
                if gated:
                    for i in range(4):
                        last = pe.transpose(b_sc[0][:, i * P:(i + 1) * P], w_raw[i], pr.id())
                    last.then_inc(sem["prep_pe"], 1)
                if biased:
                    pe.wait_ge(sem["prep_dve"], 3)
                    for i in range(2):
                        for g in range(NG):
                            last = pe.matmul(b_sc[1][:, i * NG + g:i * NG + g + 1], bias_x[0:1, i, g * P:(g + 1) * P], ones1[0:1, 0:1],
                                             start=True, stop=True)
                    last.then_inc(sem["prep_pe"], 1)
                pe.wait_ge(sem["prep_dve"], DVE_WEIGHTS)
                for g, bank in enumerate((b_st[0], b_st[1], b_mt, b_o)):
                    cols = slice(g * P, (g + 1) * P)
                    pe.matmul(bank[:], wx[:, 2, cols], pr.ctx_hi[:], start=True, stop=False)
                    pe.matmul(bank[:], wx[:, 2, cols], pr.ctx_lo[:], start=False, stop=False)
                    pe.matmul(bank[:], wx[:, 3, cols], pr.ctx_hi[:], start=False, stop=True).then_inc(sem["prep_pe"], 1)
                for h, bank in enumerate((b_proj, b_turn)):
                    if biased:
                        pe.matmul(bank[:], ones1[:], bias_row[0:1, 2:3, :].to_broadcast([1, 4, D]), start=True, stop=False, skip_group_check=True)
                    for e in range(4):
                        last = pe.matmul(bank[:, e * D:(e + 1) * D], pr.ctx_t2[:, 4 * h + e].rearrange("p a s -> p (a s)"), w[2],
                                         start=not biased, stop=True, skip_group_check=True)
                    last.then_inc(sem["prep_pe"], 1)
                if gated:
                    for h in range(2):
                        pe.wait_ge(sem["prep_dve"], DVE_READY)
                        for e in range(4):
                            last = pe.matmul(b_sc[h][:, e * D:(e + 1) * D], pr.ctx_t2[:, 4 * h + e, 0, 0:1].to_broadcast([P, P]), wvg[:],
                                             start=True, stop=True, skip_group_check=True)
                        last.then_inc(sem["prep_pe"], 1)
                pe.wait_ge(sem["prep_dve"], DVE_READY)
                pe.wait_ge(sem["prep_act"], ACT_READY)
                pe.wait_ge(sem["prep_pool"], POOL_READY)

                def turn(b):
                    pe.wait_ge(sem["xn_ready"], b + 1)
                    if own_keys:
                        need(pe, sem["v_ready"], b)
                    need(pe, sem["x_done"], b - 1)
                    need(pe, sem["xt_lo"], b)
                    for t in range(2):
                        last = pe.transpose(b_turn[:, t * P:(t + 1) * P], xn[:, t], pr.id())
                    last.then_inc(sem["xn_turned"], 1)

                def mask(b):
                    if masked:
                        pe.wait_ge(sem["mk_ready"], b + 1)
                        need(pe, sem["m_split"], b * NG)
                        for t in range(2):
                            last = pe.transpose(b_mt[:, t * P:(t + 1) * P], mk[:, t], pr.id())
                        last.then_inc(sem["mk_turned"], 1)

                def proj(b, g):
                    pe.wait_ge(sem["xt_lo"], b + 1)
                    need(pe, sem["qk_split"], b * NG + g)
                    cols = slice(g * P, (g + 1) * P)
                    for i in range(2 if own_keys else 1):
                        o = b_proj[:, i * S:(i + 1) * S]
                        pe.matmul(o, wx[:, 2 * i, cols], xt_hi[:], start=True, stop=False)
                        pe.matmul(o, wx[:, 2 * i, cols], xt_lo[:], start=False, stop=False)
                        last = pe.matmul(o, wx[:, 2 * i + 1, cols], xt_hi[:], start=False, stop=True)
                    last.then_inc(sem["proj_done"], 1)

                def scores(b, g):
                    pe.wait_ge(sem["qk_split"], b * NG + g + 1)
                    pe.wait_ge(sem["kc_ready"], b * NG + g + 1)
                    if masked:
                        pe.wait_ge(sem["mk_split"], b + 1)
                    at = g * NS

                    def bank(i):
                        need(pe, sem["sc_taken"], b * U + (at + i - 1))
                        return b_sc[(at + i) % 2]
                    o = bank(0)
                    for t in range(2):
                        ts = slice(t * P, (t + 1) * P)
                        last = pe.matmul(o[:, t * S:(t + 1) * S], q[:, g, ts], kc[:, g], start=True, stop=not masked)
                        if masked:
                            last = pe.matmul(o[:, t * S:(t + 1) * S], msk[:, ts], i2[:, 0:S2].unsqueeze(1).to_broadcast([P, GH, S2]),
                                             start=False, stop=True)
                    last.then_inc(sem["sc_done"], 1)
                    for i in range(1, NS):
                        o = bank(i)
                        rows = slice(32 * (i - 1), 32 * i)
                        for t in range(2):
                            last = pe.matmul(o[:, t * S:(t + 1) * S], q[rows, g, t * P:(t + 1) * P], k[rows, g], start=True, stop=True)
                        last.then_inc(sem["sc_done"], 1)

                def maxima(b, g):
                    pe.wait_ge(sem["m_ready"], b * NG + g + 1)
                    need(pe, sem["m_split"], b * NG + g)
                    if masked:
                        pe.wait_ge(sem["mk_split"], b + 1)
                    for t in range(2):
                        last = pe.transpose(b_mt[:, t * P:(t + 1) * P], mx[:, g % 2, t].rearrange("p j c -> p (j c)"), pr.id())
                    last.then_inc(sem["m_turned"], 1)

                def weights(b, g):
                    pe.wait_ge(sem["m_split"], b * NG + g + 1)
                    at = g * NS

                    def bank(i):
                        need(pe, sem["exp_done"], b * U + (at + i - 1))
                        return b_st[(at + i) % 2]
                    o = bank(0)
                    for pair in range(2):
                        op = o[:, pair * S:(pair + 1) * S]
                        pe.matmul(op, kc[:, g, 2 * pair:2 * pair + 2].rearrange("p j s -> p (j s)"), q[:, g], start=True, stop=False)
                        if masked:
                            pe.matmul(op, i2[:], msk[:], start=False, stop=False)
                        last = pe.matmul(op, selc[:, pair], mt[:, g % 2], start=False, stop=True)
                    last.then_inc(sem["st_done"], 1)
                    for i in range(1, NS):
                        o = bank(i)
                        rows = slice(32 * (i - 1), 32 * i)
                        for kt in range(2):
                            op = o[:, kt * S:(kt + 1) * S]
                            pe.matmul(op, k[rows, g, kt * P:(kt + 1) * P], q[rows, g], start=True, stop=False)
                            last = pe.matmul(op, negs[rows], mt[rows, g % 2], start=False, stop=True)
                        last.then_inc(sem["st_done"], 1)

                def values(b):
                    if own_keys:
                        need(pe, sem["o_norm"], b)
                        pe.wait_ge(sem["xt_lo"], b + 1)
                        for kt in range(2):
                            last = pe.matmul(b_turn[:, kt * P:(kt + 1) * P], xt_raw[:, kt * P:(kt + 1) * P], w[2], start=True, stop=True)
                        last.then_inc(sem["v_proj"], 1)

                def pv(b, o):
                    pe.wait_ge(sem["exp_done"], b * U + (2 * o + 2) * NS)
                    pe.wait_ge(sem["vc_ready"], b + 1)
                    if own_keys:
                        pe.wait_ge(sem["v_ready"], b + 1)
                    need(pe, sem["ot_taken"], b * 2 + o)
                    for i in range(NS):
                        for quad in range(4):
                            g, pair = divmod(quad, 2)
                            out = b_o[32 * quad:32 * quad + 32, 0:S]
                            if i == 0:
                                lhs, rhs = vc[:, 4 * o + quad], pt[:, o, g * NS, pair * S:(pair + 1) * S]
                            else:
                                s, kt = divmod(i - 1, 2)
                                lhs = vs[:, kt, 8 * o + 2 * quad + s]
                                rhs = pt[:, o, g * NS + 1 + 2 * pair + s, kt * S:(kt + 1) * S]
                            last = pe.matmul(out, lhs, rhs, start=(i == 0), stop=(i == NS - 1))
                    last.then_inc(sem["pv_done"], 1)

                def o_turn(b):
                    pe.wait_ge(sem["ot_taken"], b * 2 + 2)
                    if isinstance(b, int) and b == B - 1:
                        pe.wait_ge(sem["x_done"], B - 1)
                    else:
                        pe.wait_ge(sem["xt_lo"], b + 2)
                    if own_keys and not (isinstance(b, int) and b == B - 1):
                        pe.wait_ge(sem["v_ready"], b + 1)
                    for t in range(2):
                        for o in range(2):
                            last = pe.transpose(b_turn[:, (2 * t + o) * P:(2 * t + o + 1) * P], ot[:, o, t * P:(t + 1) * P], pr.id())
                    last.then_inc(sem["o_turned"], 1)

                def on_turn(b):
                    pe.wait_ge(on_ready, b + 1)
                    if own_keys and not (isinstance(b, int) and b == B - 1):
                        pe.wait_ge(sem["v_ready"], b + 2)
                    for t in range(2):
                        last = pe.transpose(b_turn[:, t * P:(t + 1) * P], on[:, t], pr.id())
                    last.then_inc(sem["on_turned"], 1)

                def y(b):
                    pe.wait_ge(sem["o2t_ready"], b + 1)
                    for t in range(2):
                        last = pe.matmul(b_turn[:, t * P:(t + 1) * P], o2t[:, t * P:(t + 1) * P], w[3], start=True, stop=True)
                    last.then_inc(sem["y_done"], 1)

                passes(pe, {"turn": turn, "mask": mask, "proj": proj, "scores": scores, "maxima": maxima, "weights": weights,
                            "values": values, "pv": pv, "o_turn": o_turn, "on_turn": on_turn, "y": y})

            @block.scalar
            def _(act):
                if gated:
                    act.wait_ge(sem["prep_pe"], 1)
                    act.copy(wf[:], b_sc[0][:].rearrange("p (i n) -> p i n", i=4)).then_inc(sem["prep_act"], 1)
                    act.wait_ge(sem["loaded"], LOADED)
                    act.activation(gate_row[:], gate_row[:], ACT.Tanh).then_inc(sem["prep_act"], 1)
                pe_at = 1 if gated or biased else 0
                n_act = 2 if gated else 0
                for g, bank in enumerate((b_st[0], b_st[1], b_mt, b_o)):
                    act.wait_ge(sem["prep_pe"], pe_at + g + 1)
                    act.wait_ge(sem["prep_dve"], DVE_WEIGHTS + g)
                    act.activation(hk[:].bitcast(F32R), bank[:], ACT.Identity, bias=bias_ca[:, 1, g:g + 1], scale=pr.c("ak")).then_inc(sem["prep_act"], 1)
                for h, bank in enumerate((b_proj, b_turn)):
                    act.wait_ge(sem["prep_pe"], pe_at + 5 + h)
                    act.copy(vc_all[:, 4 * h:4 * h + 4].rearrange("p e d -> p (e d)"), bank[:]).then_inc(sem["prep_act"], 1)
                if gated:
                    for h in range(2):
                        act.wait_ge(sem["prep_pe"], pe_at + 7 + h)
                        act.copy(vg_all[:, 4 * h:4 * h + 4].rearrange("p e d -> p (e d)"), b_sc[h][:]).then_inc(sem["prep_act"], 1)

                def turn(b):
                    act.wait_ge(sem["xn_turned"], b + 1)
                    need(act, sem["proj_done"], b * NG)
                    if own_keys:
                        need(act, sem["v_proj"], b)
                        act.copy(xt_raw[:], b_turn[:, 0:S])
                    act.copy(xt_hi[:], b_turn[:, 0:S]).then_inc(sem["xt_hi"], 1)

                def mask(b):
                    if masked:
                        act.wait_ge(sem["mk_turned"], b + 1)
                        need(act, sem["mk_split"], b)
                        act.activation(hmk[:].bitcast(F32R), b_mt[:, 0:S], ACT.Copy, scale=mask_a[:]).then_inc(sem["mk_hi"], 1)

                def proj(b, g):
                    act.wait_ge(sem["proj_done"], b * NG + g + 1)
                    need(act, sem["qk_split"], b * NG + g)
                    for i in range(2 if own_keys else 1):
                        last = act.activation(part[:, i].bitcast(F32R), b_proj[:, i * S:(i + 1) * S], ACT.Identity,
                                              bias=bias_ca[:, i, g:g + 1], scale=pr.c("ak" if i else "aq"))
                    last.then_inc(sem["proj_hi"], 1)

                def maxima(b, g):
                    act.wait_ge(sem["m_turned"], b * NG + g + 1)
                    need(act, sem["m_split"], b * NG + g)
                    act.activation(hm[:].bitcast(F32R), b_mt[:, 0:S], ACT.Copy, scale=pr.c("am")).then_inc(sem["m_hi"], 1)

                def weights(b, g):
                    need(act, sem["pv_done"], b * 2 + (g // 2 - 1))
                    for i in range(NS):
                        act.wait_ge(sem["st_done"], b * U + (g * NS + i + 1))
                        act.activation(pt[:, g // 2, (g % 2) * NS + i], b_st[(g * NS + i) % 2][:], ACT.Exp, scale=scale).then_inc(sem["exp_done"], 1)

                def values(b):
                    if own_keys:
                        act.wait_ge(sem["v_proj"], b + 1)
                        need(act, sem["pv_done"], b * 2)
                        dst = vs[:].rearrange("p k (a s) c -> p k a (s c)", s=2)
                        for kt in range(2):
                            for s in range(2):
                                src = b_turn[:, kt * P:(kt + 1) * P].rearrange("p (a s d) -> p a s d", s=2, d=HD)[:, :, s]
                                last = act.copy(dst[:, kt, :, 48 * s:48 * s + HD], src)
                        last.then_inc(sem["v_ready"], 1)

                def pv(b, o):
                    act.wait_ge(sem["pv_done"], b * 2 + o + 1)
                    need(act, sem["o_turned"], b)
                    act.copy(ot[:, o], b_o[:, 0:S]).then_inc(sem["ot_taken"], 1)

                def on_turn(b):
                    act.wait_ge(sem["on_turned"], b + 1)
                    need(act, sem["y_done"], b)
                    if gated:
                        act.activation(o2t[:], b_turn[:, 0:S], ACT.Identity, bias=ln_gb[:, 1:2], scale=ln_gb[:, 0:1]).then_inc(sem["o2t_ready"], 1)
                    else:
                        act.copy(o2t[:], b_turn[:, 0:S]).then_inc(sem["o2t_ready"], 1)

                passes(act, {"turn": turn, "mask": mask, "proj": proj, "maxima": maxima, "weights": weights, "values": values,
                             "pv": pv, "on_turn": on_turn})

            @block.vector
            def _(dve):
                count = [0]

                def prep(ins_, wait=True):
                    count[0] += 1
                    ins_.then_inc(sem["prep_dve"], 1)
                    if wait:
                        dve.wait_ge(sem["prep_dve"], count[0])
                prep(dve.memset(ones1[:], 1.0))
                if biased:
                    dve.wait_ge(sem["loaded"], LOADED)
                    prep(dve.tensor_copy(bias_x[:].rearrange("a i (h t d) -> a i h t d", t=4, d=HD)[:, 0],
                                         bias_row[0:1, 0, :].rearrange("a (h d) -> a h d", d=HD).unsqueeze(2).to_broadcast([1, H, 4, HD])))
                    dve.tensor_copy(bias_x[:].rearrange("a i (h t d) -> a i h t d", t=4, d=HD)[:, 1],
                                    bias_row[0:1, 1, :].rearrange("a (h d) -> a h d", d=HD).unsqueeze(2).to_broadcast([1, H, 4, HD])).then_inc(sem["prep_dve"], 1)
                    count[0] += 1
                if gated:
                    dve.wait_ge(sem["prep_act"], 1)
                for i in range(2):
                    src = w[i].rearrange("p (h d) -> p h d", d=HD).unsqueeze(2).to_broadcast([P, H, 4, HD])
                    hi, lo = (wx[:, 2 * i + e].rearrange("p (h t d) -> p h t d", t=4, d=HD) for e in range(2))
                    prep(dve.tensor_copy(hi, src))
                    prep(dve.tensor_tensor(lo, src, hi.bitcast(F32), ALU.subtract))
                if biased:
                    dve.wait_ge(sem["prep_pe"], 1)
                    prep(dve.tensor_copy(bias_c[:].rearrange("p i g -> p (i g)"), b_sc[1][:, 0:2 * NG]))
                    prep(dve.tensor_scalar(bias_ca[:, 0], bias_c[:, 0], pr.c("aq"), None, ALU.mult))
                    prep(dve.tensor_scalar(bias_ca[:, 1], bias_c[:, 1], pr.c("ak"), None, ALU.mult))
                else:
                    prep(dve.memset(bias_c[:], 0.0))
                    prep(dve.memset(bias_ca[:], 0.0))
                assert count[0] == DVE_WEIGHTS, count
                n_act = 2 if gated else 0
                for g, bank in enumerate((b_st[0], b_st[1], b_mt, b_o)):
                    dve.wait_ge(sem["prep_act"], n_act + g + 1)
                    prep(dve.scalar_tensor_tensor(kc_all[:, g].rearrange("p b s -> p (b s)"), bank[:], bias_c[:, 1, g:g + 1], hk[:], ALU.add, ALU.add))
                if gated:
                    dve.wait_ge(sem["prep_act"], n_act + 6)
                    prep(dve.memset(kc_all[:].rearrange("p g b s -> p (g b) s")[:, :, 0:1].bitcast(F32), 0.0))
                    for row in (0, 64):
                        prep(dve.memset(vc_all[row:row + 1], 0.0))
                    prep(dve.tensor_copy(negs[:], pr.c("negs")))
                    prep(dve.tensor_tensor(wvg[:].rearrange("p (h d) -> p h d", d=HD), w[2].rearrange("p (h d) -> p h d", d=HD),
                                           gate_row[:].unsqueeze(2).to_broadcast([P, H, HD]), ALU.mult))
                prep(dve.tensor_copy(selc[:].rearrange("p a n -> p (a n)"), pr.c("selc0" if gated else "selc")))
                if masked:
                    dve.wait_ge(sem["loaded"], LOADED)
                    prep(dve.tensor_copy(i2[:], pr.c("i2")))
                    prep(dve.tensor_scalar(mask_a[:], pr.c("amask"), MASK_SCALE, None, ALU.mult))
                assert count[0] == DVE_READY, count

                def norm(b):
                    for t in range(2):
                        dve.bn_stats(st6[:, t:t + 1], pr.x[:, bass.ds(b * 2 + t, 1)]).then_inc(sem["stats"], 1)
                    need(dve, sem["rstd"], b)
                    dve.wait_ge(sem["stats"], b * 2 + 2)
                    settled(dve, sem)
                    for t in range(2):
                        last = dve.bn_aggr(mv[:, t], st6[:, t])
                    last.then_inc(sem["moments"], 1)

                def scale_x(b):
                    dve.wait_ge(sem["rstd"], b + 1)
                    need(dve, sem["xn_turned"], b)
                    for t in range(2):
                        last = dve.tensor_scalar(xn[:, t:t + 1], pr.x[:, bass.ds(b * 2 + t, 1)], mv[:, t, 0:1], rstd[:, t:t + 1],
                                                 ALU.subtract, ALU.mult)
                    last.then_inc(sem["xn_ready"], 1)

                def turn(b):
                    dve.wait_ge(sem["xt_hi"], b + 1)
                    need(dve, sem["proj_done"], b * NG)
                    dve.tensor_tensor(xt_lo[:], b_turn[:, 0:S], xt_hi[:].bitcast(F32), ALU.subtract).then_inc(sem["xt_lo"], 1)

                def mask(b):
                    if masked:
                        dve.wait_ge(sem["mk_hi"], b + 1)
                        need(dve, sem["st_done"], b * U)
                        dve.scalar_tensor_tensor(msk[:], b_mt[:, 0:S], MASK_SCALE, hmk[:], ALU.mult, ALU.add).then_inc(sem["mk_split"], 1)

                def proj(b, g):
                    dve.wait_ge(sem["proj_hi"], b * NG + g + 1)
                    need(dve, sem["st_done"], b * U + (g + 1) * NS - U)
                    for i in range(2 if own_keys else 1):
                        last = dve.scalar_tensor_tensor((k if i else q)[:, g], b_proj[:, i * S:(i + 1) * S], bias_c[:, i, g:g + 1],
                                                        part[:, i], ALU.add, ALU.add)
                    last.then_inc(sem["qk_split"], 1)

                def scores(b, g):
                    start = 1 if gated else 0
                    at = g * NS
                    dve.wait_ge(sem["sc_done"], b * U + (at + 1))
                    by_head = b_sc[at % 2][:].rearrange("p (t j s) -> p (t j) s", t=2, s=S2)
                    dve.tensor_reduce(mc[:].rearrange("p t j -> p (t j)"), by_head[:, :, start:], AX_X, ALU.max).then_inc(sem["sc_taken"], 1)
                    for i in range(1, NS):
                        dve.wait_ge(sem["sc_done"], b * U + (at + i + 1))
                        dve.tensor_reduce(ms[:, :, i - 1], b_sc[(at + i) % 2][:].rearrange("p (t s) -> p t s", s=S),
                                          AX_X, ALU.max).then_inc(sem["sc_taken"], 1)
                    dve.wait_ge(sem["sc_taken"], b * U + (at + NS))
                    need(dve, sem["m_turned"], b * NG + (g - 1))
                    dst = mx[:, g % 2].rearrange("p t j c -> p (t j) c")[:, :, 0:2]
                    mcb = mc[:].rearrange("p t j -> p (t j)").unsqueeze(2).to_broadcast([P, 2 * GH, 2])
                    if own_keys:
                        msb = ms[:].rearrange("p t j -> p (t j)").unsqueeze(2).to_broadcast([P, 2 * GH, 2])
                        dve.tensor_tensor(dst, mcb, msb, ALU.max).then_inc(sem["m_ready"], 1)
                    else:
                        dve.tensor_copy(dst, mcb).then_inc(sem["m_ready"], 1)

                def maxima(b, g):
                    dve.wait_ge(sem["m_hi"], b * NG + g + 1)
                    need(dve, sem["st_done"], b * U + (g - 1) * NS)
                    dve.tensor_tensor(mt[:, g % 2], b_mt[:, 0:S], hm[:], ALU.add).then_inc(sem["m_split"], 1)

                def o_norm(b):
                    dve.wait_ge(sem["o_turned"], b + 1)
                    by_head = b_turn[:].rearrange("p (h c) -> p h c", c=16)
                    dve.reciprocal(rc[:], by_head[:, :, 8]).then_inc(sem["rc_ready"], 1)
                    dve.wait_ge(sem["rc_ready"], b + 1)
                    need(dve, sem["on_turned"], b)
                    last = dve.tensor_tensor(on[:].rearrange("p t (h d) -> p (t h) d", d=HD), by_head[:, :, 0:HD],
                                             rc[:].unsqueeze(2).to_broadcast([P, 2 * H, HD]), ALU.mult)
                    last.then_inc(sem["o_norm"], 1)
                    if gated:
                        dve.wait_ge(sem["o_norm"], b + 1)
                        dve.tensor_tensor(o16[:], on[:], vg_all[:, bass.ds(b, 1)].to_broadcast([P, 2, D]), ALU.add).then_inc(sem["o_round"], 1)
                        dve.wait_ge(sem["o_round"], b + 1)
                        for t in range(2):
                            dve.bn_stats(st6b[:, t], o16[:, t]).then_inc(sem["o_stats"], 1)
                        need(dve, sem["o_rstd"], b)
                        dve.wait_ge(sem["o_stats"], b * 2 + 2)
                        settled(dve, sem)
                        for t in range(2):
                            last = dve.bn_aggr(mvb[:, t], st6b[:, t])
                        last.then_inc(sem["o_moments"], 1)

                def o_scale(b):
                    if gated:
                        dve.wait_ge(sem["o_rstd"], b + 1)
                        for t in range(2):
                            last = dve.tensor_scalar(on[:, t], o16[:, t], mvb[:, t, 0:1], rstdb[:, t:t + 1], ALU.subtract, ALU.mult)
                        last.then_inc(sem["on_ready"], 1)

                def y(b):
                    dve.wait_ge(sem["y_done"], b + 1)
                    dve.wait_ge(sem["x_bias"], b + 1)
                    xb = pr.x[:, tiles(b, 2)]
                    dve.scalar_tensor_tensor(xb, b_turn[:, 0:S].rearrange("p (t d) -> p t d", t=2), tg, xb, ALU.mult, ALU.add).then_inc(sem["x_done"], 1)

                passes(dve, {"norm": norm, "scale": scale_x, "turn": turn, "mask": mask, "proj": proj, "scores": scores, "maxima": maxima,
                             "o_norm": o_norm, "o_scale": o_scale, "y": y})



def attention3(pr):
    nc, ins = pr.nc, pr.ins
    scale = HD3 ** -0.5
    NC = 4
    with nc.cleanup_on_exit(), ExitStack() as scope:
        def sb(name, shape, dt=F32):
            return scope.enter_context(nc.sbuf_tensor(f"L3_{name}", shape, dt))

        wq = sb("wq", [P, 512])
        wk = sb("wk", [P, 512])
        wv = sb("wv", [P, 512])
        wo = sb("wo", [P, NC, D])
        wq_hi = sb("wq_hi", [P, 512], F32R)
        wq_lo = sb("wq_lo", [P, 512], F32R)
        bo = sb("bo", [P, D])
        kt_all = sb("kt_all", [P, NC, B, S2])
        v_all = sb("v_all", [P, B, 512])
        kb = sb("kb", [P, NC, 2, S2])
        vb = sb("vb", [P, NC, 2, HD3])
        sel3 = sb("sel3", [P, NC, P], F32R)
        raw3 = sb("raw3", [P, 1920])
        st6 = sb("st6", [P, 2, 6])
        mv = sb("mv", [P, 2, 2])
        ve = sb("ve", [P, 2])
        rstd = sb("rstd", [P, 2])
        xn = sb("xn", [P, 2, D])
        xt_hi = sb("xt_hi", [P, S], F32R)
        xt_lo = sb("xt_lo", [P, S], F32R)
        q = sb("q", [P, NC, S])
        mc = sb("mc", [P, 2, H3])
        mx = sb("mx", [P, 2, H3, 16])
        hm = sb("hm", [P, S])
        mt = sb("mt", [P, S], F32R)
        pt = sb("pt", [P, NC, S])
        rs = sb("rs", [P, NC, S])
        on = sb("on", [P, NC, S])
        sem = pr.sems("loaded", "w3_in", "prep_pe", "prep_act", "prep_dve", "settled", "prep_pool", "stats", "moments", "var_eps", "rstd",
                     "xn_ready", "xn_turned", "xt_hi", "xt_lo", "q_done", "q_taken", "kb_ready", "sc_done", "sc_taken", "m_ready",
                     "m_turned", "m_hi", "m_split", "st_done", "exp_done", "sum_done", "sum_taken", "o_done", "o_taken", "y_done",
                     "x_bias", "x_done", "w3_hi", "vb_ready")
        b_q, b_turn, b_sc, b_sum, b_st, b_mt, b_o = (pr.bank[0], pr.bank[1], pr.bank[2], pr.bank[3], pr.bank[4:6], pr.bank[6], pr.bank[7])
        tg = pr.gates[:, 3:4]

        first = [("norm", 0), ("scale", 0), ("turn", 0), ("proj", 0), ("keys", 0), ("scores", 0)]

        def order(b):
            steps = []
            more = not (isinstance(b, int) and b == B - 1)
            late = not (isinstance(b, int) and b == 0)
            steps += [("maxima", b)]
            if more:
                steps += [("norm", b + 1)]
            if late:
                steps += [("pv", b - 1)]
            steps += [("weights", b)]
            if more:
                steps += [("scale", b + 1), ("turn", b + 1), ("proj", b + 1)]
            if late:
                steps += [("y", b - 1)]
            if more:
                steps += [("keys", b + 1), ("scores", b + 1)]
            return steps

        flush = [("pv", B - 1), ("y", B - 1)]

        def passes(eng, does):
            def run(steps):
                for step, at in steps:
                    if step in does:
                        does[step](at)
            run(first)
            run(order(0))
            run(order(1))
            with eng.Fori(2, B - 1) as b:
                run(order(b))
            run(order(B - 1))
            run(flush)

        with nc.Block() as block:
            @block.sync
            def _(sp):
                for dst, src in ((wq[:], ins["L3_xattn_Wq"]), (wk[:], ins["L3_xattn_Wk"]), (wv[:], ins["L3_xattn_Wv"]),
                                 (wo[:], ins["L3_xattn_Wo"].rearrange("(c p) n -> p c n", p=P)),
                                 (bo[:], ins["L3_xattn_bo"].partition_broadcast(P))):
                    sp.dma_start(dst, src).then_inc(sem["loaded"], 16)
                for a, name in ((0, "L3_ffn_w_gate"), (512, "L3_ffn_w_up")):
                    sp.dma_start(raw3[:, a:a + 512].rearrange("p (e i) -> p e i", e=E3), ins[name].rearrange("e p i -> p e i")).then_inc(sem["w3_in"], 16)
                sp.dma_start(raw3[:, 1024:1536].rearrange("p (c v) -> p c v", c=4), ins["L3_ffn_w_down"].rearrange("(c e) i v -> (e i) c v", e=2)).then_inc(sem["w3_in"], 16)
                for a, name in ((1536, "L3_ffn_sw_gate"), (1664, "L3_ffn_sw_up"), (1792, "L3_ffn_sw_down")):
                    sp.dma_start(raw3[:, a:a + P], ins[name]).then_inc(sem["w3_in"], 16)

            @block.gpsimd
            def _(pool):
                pool.memset(kb[:], 0.0).then_inc(sem["prep_pool"], 1)
                pool.memset(vb[:], 0.0).then_inc(sem["prep_pool"], 1)
                pool.memset(mx[:], 0.0).then_inc(sem["prep_pool"], 1)
                pool.wait_ge(sem["loaded"], 80)
                pool.tensor_scalar(bo[:], bo[:], tg, None, ALU.mult).then_inc(sem["prep_pool"], 1)
                pool.wait_ge(sem["prep_pool"], 4)
                pool.wait_ge(sem["prep_act"], 12)

                def norm(b):
                    pool.wait_ge(sem["moments"], b + 1)
                    pool.tensor_tensor(ve[:], mv[:, :, 1], pr.eps[:], ALU.add).then_inc(sem["var_eps"], 1)
                    pool.wait_ge(sem["var_eps"], b + 1)
                    pool.tensor_tensor(rstd[:], ve[:], pr.neg_half[:], ALU.pow).then_inc(sem["rstd"], 1)

                def turn(b):
                    pool.wait_ge(sem["xn_ready"], b + 1)
                    xb = pr.x[:, tiles(b, 2)]
                    pool.tensor_tensor(xb, xb, bo[:].unsqueeze(1).to_broadcast([P, 2, D]), ALU.add).then_inc(sem["x_bias"], 1)

                def keys(b):
                    need(pool, sem["st_done"], b * 2)
                    for s in range(2):
                        last = pool.tensor_tensor(kb[:, :, s], kt_all[:, :, bass.ds(b, 1)].rearrange("p c e s -> p (c e) s"),
                                                  pr.c("half")[:, s:s + 1].unsqueeze(2).to_broadcast([P, NC, S2]), ALU.mult)
                    last.then_inc(sem["kb_ready"], 1)
                    if isinstance(b, int) and b == 0:
                        pool.wait_ge(sem["w3_in"], 96)
                        pool.tensor_copy(pr.big_hi[:, 1152:1152 + 1920], raw3[:]).then_inc(sem["w3_hi"], 1)
                        pool.wait_ge(sem["w3_hi"], 1)
                        pool.tensor_tensor(pr.big_lo[:, 1152:1152 + 1920], raw3[:], pr.big_hi[:, 1152:1152 + 1920].bitcast(F32), ALU.subtract)

                def weights(b):
                    need(pool, sem["o_done"], b * 2)
                    src = v_all[:, bass.ds(b, 1)].rearrange("p e (c s d) -> p (e c) s d", c=NC, s=2)
                    for s in range(2):
                        last = pool.tensor_tensor(vb[:, :, s], src[:, :, s],
                                                  pr.c("half")[:, s:s + 1].unsqueeze(2).to_broadcast([P, NC, HD3]), ALU.mult)
                    last.then_inc(sem["vb_ready"], 1)

                passes(pool, {"norm": norm, "turn": turn, "keys": keys, "weights": weights})

            @block.tensor
            def _(pe):
                pe.wait_ge(sem["loaded"], 80)
                for c in range(NC):
                    pe.matmul(pr.bank[c][:], wk[:, c * P:(c + 1) * P], pr.ctx_t2[:, :, 0], start=True, stop=True).then_inc(sem["prep_pe"], 1)
                for e in range(B):
                    bank = pr.bank[(NC + e) % 8]
                    if e >= 4:
                        pe.wait_ge(sem["prep_act"], e - 4 + 1)
                    pe.matmul(bank[:], pr.ctx_t2[:, e].rearrange("p a s -> p (a s)"), wv[:], start=True, stop=True).then_inc(sem["prep_pe"], 1)
                pe.wait_ge(sem["prep_act"], 12)
                pe.wait_ge(sem["prep_dve"], 3)
                pe.wait_ge(sem["prep_pool"], 4)

                def turn(b):
                    pe.wait_ge(sem["xn_ready"], b + 1)
                    need(pe, sem["xt_lo"], b)
                    need(pe, sem["x_done"], b - 2)
                    for t in range(2):
                        last = pe.transpose(b_turn[:, t * P:(t + 1) * P], xn[:, t], pr.id())
                    last.then_inc(sem["xn_turned"], 1)

                def proj(b):
                    pe.wait_ge(sem["xt_lo"], b + 1)
                    for h in range(2):
                        need(pe, sem["q_taken"], b * 2 + h)
                        for e in range(2):
                            cols = slice((2 * h + e) * P, (2 * h + e + 1) * P)
                            o = b_q[:, e * S:(e + 1) * S]
                            pe.matmul(o, wq_hi[:, cols], xt_hi[:], start=True, stop=False)
                            pe.matmul(o, wq_hi[:, cols], xt_lo[:], start=False, stop=False)
                            last = pe.matmul(o, wq_lo[:, cols], xt_hi[:], start=False, stop=True)
                        last.then_inc(sem["q_done"], 1)

                def scores(b):
                    pe.wait_ge(sem["q_taken"], b * 2 + 2)
                    pe.wait_ge(sem["kb_ready"], b + 1)
                    for t in range(2):
                        need(pe, sem["sc_taken"], b * 2 + t)
                        for c in range(NC):
                            last = pe.matmul(b_sc[:, c * P:(c + 1) * P], q[:, c, t * P:(t + 1) * P], kb[:, c].rearrange("p h s -> p (h s)"),
                                             start=True, stop=True)
                        last.then_inc(sem["sc_done"], 1)

                def maxima(b):
                    pe.wait_ge(sem["m_ready"], b + 1)
                    need(pe, sem["m_split"], b)
                    for t in range(2):
                        last = pe.transpose(b_mt[:, t * P:(t + 1) * P], mx[:, t].rearrange("p j c -> p (j c)"), pr.id())
                    last.then_inc(sem["m_turned"], 1)

                def weights(b):
                    pe.wait_ge(sem["m_split"], b + 1)
                    for h in range(2):
                        need(pe, sem["exp_done"], b * 2 + h - 1)
                        for e in range(2):
                            c = 2 * h + e
                            o = b_st[h][:, e * S:(e + 1) * S]
                            pe.matmul(o, kb[:, c].rearrange("p h s -> p (h s)"), q[:, c], start=True, stop=False)
                            last = pe.matmul(o, sel3[:, c], mt[:], start=False, stop=True)
                        last.then_inc(sem["st_done"], 1)

                def pv(b):
                    for h in range(2):
                        pe.wait_ge(sem["exp_done"], b * 2 + h + 1)
                        need(pe, sem["sum_taken"], b * 2 + h)
                        for e in range(2):
                            last = pe.matmul(b_sum[:, e * S:(e + 1) * S], pr.c("onesb"), pt[:, 2 * h + e], start=True, stop=True)
                        last.then_inc(sem["sum_done"], 1)
                        need(pe, sem["o_taken"], b * 2 + h)
                        pe.wait_ge(sem["vb_ready"], b + 1)
                        for e in range(2):
                            last = pe.matmul(b_o[:, e * S:(e + 1) * S], vb[:, 2 * h + e].rearrange("p s d -> p (s d)"), pt[:, 2 * h + e],
                                             start=True, stop=True)
                        last.then_inc(sem["o_done"], 1)

                def y(b):
                    pe.wait_ge(sem["o_taken"], b * 2 + 2)
                    if isinstance(b, int) and b == B - 1:
                        pe.wait_ge(sem["x_done"], B - 1)
                    else:
                        pe.wait_ge(sem["xt_lo"], B if isinstance(b, int) and b == B - 2 else b + 3)
                    for t in range(2):
                        for c in range(NC):
                            last = pe.matmul(b_turn[:, t * P:(t + 1) * P], on[:, c, t * P:(t + 1) * P], wo[:, c], start=(c == 0), stop=(c == NC - 1))
                    last.then_inc(sem["y_done"], 1)

                passes(pe, {"turn": turn, "proj": proj, "scores": scores, "maxima": maxima, "weights": weights, "pv": pv, "y": y})

            @block.scalar
            def _(act):
                for c in range(NC):
                    act.wait_ge(sem["prep_pe"], c + 1)
                    act.copy(kt_all[:, c].rearrange("p b s -> p (b s)"), pr.bank[c][:]).then_inc(sem["prep_act"], 1)
                for e in range(B):
                    act.wait_ge(sem["prep_pe"], NC + e + 1)
                    act.copy(v_all[:, e], pr.bank[(NC + e) % 8][:]).then_inc(sem["prep_act"], 1)

                def turn(b):
                    act.wait_ge(sem["xn_turned"], b + 1)
                    need(act, sem["q_done"], b * 2)
                    act.copy(xt_hi[:], b_turn[:, 0:S]).then_inc(sem["xt_hi"], 1)

                def proj(b):
                    need(act, sem["st_done"], b * 2)
                    for h in range(2):
                        act.wait_ge(sem["q_done"], b * 2 + h + 1)
                        act.copy(q[:, 2 * h:2 * h + 2].rearrange("p c s -> p (c s)"), b_q[:]).then_inc(sem["q_taken"], 1)

                def maxima(b):
                    act.wait_ge(sem["m_turned"], b + 1)
                    need(act, sem["m_split"], b)
                    act.activation(hm[:].bitcast(F32R), b_mt[:, 0:S], ACT.Copy, scale=pr.c("a16")).then_inc(sem["m_hi"], 1)

                def weights(b):
                    need(act, sem["o_done"], b * 2)
                    for h in range(2):
                        act.wait_ge(sem["st_done"], b * 2 + h + 1)
                        act.activation(pt[:, 2 * h:2 * h + 2].rearrange("p c s -> p (c s)"), b_st[h][:], ACT.Exp, scale=scale).then_inc(sem["exp_done"], 1)

                passes(act, {"turn": turn, "proj": proj, "maxima": maxima, "weights": weights})

            @block.vector
            def _(dve):
                dve.wait_ge(sem["loaded"], 80)
                dve.tensor_copy(wq_hi[:], wq[:]).then_inc(sem["prep_dve"], 1)
                dve.wait_ge(sem["prep_dve"], 1)
                dve.tensor_tensor(wq_lo[:], wq[:], wq_hi[:].bitcast(F32), ALU.subtract).then_inc(sem["prep_dve"], 1)
                dve.tensor_scalar(sel3[:].rearrange("p c n -> p (c n)"), pr.c("self3"), -1.0, None, ALU.mult).then_inc(sem["prep_dve"], 1)
                dve.wait_ge(sem["prep_act"], 12)
                dve.wait_ge(sem["prep_pool"], 3)

                def norm(b):
                    for t in range(2):
                        dve.bn_stats(st6[:, t:t + 1], pr.x[:, bass.ds(b * 2 + t, 1)]).then_inc(sem["stats"], 1)
                    need(dve, sem["rstd"], b)
                    dve.wait_ge(sem["stats"], b * 2 + 2)
                    settled(dve, sem)
                    for t in range(2):
                        last = dve.bn_aggr(mv[:, t], st6[:, t])
                    last.then_inc(sem["moments"], 1)

                def scale_x(b):
                    dve.wait_ge(sem["rstd"], b + 1)
                    need(dve, sem["xn_turned"], b)
                    for t in range(2):
                        last = dve.tensor_scalar(xn[:, t:t + 1], pr.x[:, bass.ds(b * 2 + t, 1)], mv[:, t, 0:1], rstd[:, t:t + 1],
                                                 ALU.subtract, ALU.mult)
                    last.then_inc(sem["xn_ready"], 1)

                def turn(b):
                    dve.wait_ge(sem["xt_hi"], b + 1)
                    need(dve, sem["q_done"], b * 2)
                    dve.tensor_tensor(xt_lo[:], b_turn[:, 0:S], xt_hi[:].bitcast(F32), ALU.subtract).then_inc(sem["xt_lo"], 1)

                def scores(b):
                    for t in range(2):
                        dve.wait_ge(sem["sc_done"], b * 2 + t + 1)
                        dve.tensor_reduce(mc[:, t], b_sc[:].rearrange("p (h s) -> p h s", s=S2), AX_X, ALU.max).then_inc(sem["sc_taken"], 1)
                    dve.wait_ge(sem["sc_taken"], b * 2 + 2)
                    need(dve, sem["m_turned"], b)
                    dve.tensor_copy(mx[:].rearrange("p t j c -> p (t j) c")[:, :, 0:2],
                                    mc[:].rearrange("p t j -> p (t j)").unsqueeze(2).to_broadcast([P, 2 * H3, 2])).then_inc(sem["m_ready"], 1)

                def maxima(b):
                    dve.wait_ge(sem["m_hi"], b + 1)
                    need(dve, sem["st_done"], b * 2)
                    dve.tensor_tensor(mt[:], b_mt[:, 0:S], hm[:], ALU.add).then_inc(sem["m_split"], 1)

                def pv(b):
                    for h in range(2):
                        pr_rs = rs[:, 2 * h:2 * h + 2].rearrange("p c s -> p (c s)")
                        pr_on = on[:, 2 * h:2 * h + 2].rearrange("p c s -> p (c s)")
                        dve.wait_ge(sem["sum_done"], b * 2 + h + 1)
                        dve.reciprocal(pr_rs, b_sum[:]).then_inc(sem["sum_taken"], 1)
                        dve.wait_ge(sem["o_done"], b * 2 + h + 1)
                        dve.wait_ge(sem["sum_taken"], b * 2 + h + 1)
                        need(dve, sem["y_done"], b)
                        dve.tensor_tensor(pr_on, b_o[:], pr_rs, ALU.mult).then_inc(sem["o_taken"], 1)

                def y(b):
                    dve.wait_ge(sem["y_done"], b + 1)
                    dve.wait_ge(sem["x_bias"], b + 1)
                    xb = pr.x[:, tiles(b, 2)]
                    dve.scalar_tensor_tensor(xb, b_turn[:, 0:S].rearrange("p (t d) -> p t d", t=2), tg, xb, ALU.mult, ALU.add).then_inc(sem["x_done"], 1)

                passes(dve, {"norm": norm, "scale": scale_x, "turn": turn, "scores": scores, "maxima": maxima, "pv": pv, "y": y})



def ffn(pr, layer):
    nc, ins = pr.nc, pr.ins
    n = f"L{layer}f"
    C = {0: E0 * X0 // P, 1: E1 * 3, 2: HID2 // P, 3: E3 * X3 // P + 1}[layer]
    R = {0: 4, 1: 3, 2: 3, 3: 5}[layer]
    E = {0: E0, 1: E1, 2: 0, 3: E3}[layer]
    K = {0: K0, 1: K1, 2: 0, 3: K3}[layer]
    NS = 3 if layer == 2 else 2
    DUP = P // E if E else 0
    W = E + 8 - K
    T = TOK // P
    HAS_UP = layer != 0
    GATED = {0: range(4), 1: range(24), 2: range(0), 3: range(4)}[layer]
    FUNC = {0: ACT.Relu, 1: ACT.Gelu, 2: ACT.Silu, 3: ACT.Silu}[layer]
    SENTINEL = LOWEST
    TAKEN = 3 * LOWEST

    def rows(c):
        return 96 if layer == 1 and c % 3 == 2 else P

    def weights_at(c):
        if layer == 0:
            return c * P, None, 512 + c * P
        if layer == 1:
            e, k = divmod(c, 3)
            return e * X1 + k * P, 2816 + e * X1 + k * P, 5632 + e * 384 + k * P
        if layer == 2:
            return c * P, 384 + c * P, 768 + c * P
        return (1152 + c * P, 1664 + c * P, 2176 + c * P) if c < 4 else (2688, 2816, 2944)

    def distance(c):
        last = [k for k in range(c) if k % NS == c % NS] or [k - C for k in range(C) if k % NS == c % NS]
        return c - max(last)

    def gate_slot(c):
        return (c // 3) % 2 if layer == 1 else c % 2

    def gate_distance(c):
        at = gate_slot(c)
        last = [k for k in GATED if k < c and gate_slot(k) == at] or [k - C for k in GATED if gate_slot(k) == at]
        return c - max(last)

    with nc.cleanup_on_exit(), ExitStack() as scope:
        def sb(name, shape, dt=F32):
            return scope.enter_context(nc.sbuf_tensor(f"{n}_{name}", shape, dt))

        st6 = sb("st6", [P, T, 6])
        mv = sb("mv", [P, T, 2])
        ve = sb("ve", [P, T])
        rstd = sb("rstd", [P, T])
        eps = sb("eps", [P, T])
        neg_half = sb("neg_half", [P, T])
        xn = sb("xn", [P, T, D])
        xt_hi = sb("xt_hi", [P, NI, TOK], F32R)
        xt_lo = sb("xt_lo", [P, NI, TOK], F32R)
        a = sb("a", [P, R, TOK])
        h = sb("h", [P, R, TOK])
        h_hi = sb("h_hi", [P, R, TOK], F32R)
        h_lo = sb("h_lo", [P, R, TOK], F32R)
        yt = sb("yt", [P, TOK])
        if E:
            xt_raw = sb("xt_raw", [P, TOK])
            router = sb("router", [P, E])
            sel = sb("sel", [P, E if layer == 1 else 512], F32R)
            pe_ = sb("pe", [P, T, E])
            p1 = sb("p1", [P, T, E])
            cand = sb("cand", [P, T, W])
            top8 = sb("top8", [P, T, 8])
            want = sb("want", [P, T, 8])
            left = sb("left", [P, T, W])
            picked = sb("picked", [P, T, E])
            total = sb("total", [P, T])
            total2 = sb("total2", [P, T])
            total3 = sb("total3", [P, T])
            gx = sb("gx", [P, T, E, DUP])
            hg = sb("hg", [P, TOK])
            gts = sb("gts", [P, NI, TOK], F32R)
            extra = sb("extra", [P, E])
        if layer == 0:
            sel_rows = sb("sel_rows", [E0, D])
        if layer == 1:
            bias_col = sb("bias_col", [P, 1])
        if layer == 2:
            wi = sb("wi", [P, 9, P], I32)
            wf = sb("wf", [P, 9, P])
        if layer == 3:
            gs = sb("gs", [P, T, NG3 + 8 - 2])
            gtop = sb("gtop", [P, T, 8])
            gwant = sb("gwant", [P, T, 8])
            gleft = sb("gleft", [P, T, NG3 + 8 - 2])

        sem = pr.sems("loaded", "prep_pe", "prep_act", "prep_dve", "settled", "stats", "moments", "var_eps", "rstd", "xn_ready", "xn_turned",
                     "xt_raw", "xt_hi", "xt_lo", "logits_done", "logits_exp", "logits_less", "routed", "gates_turned", "gates_hi",
                     "gts_ready", "up_done", "gate_done", "act_done", "half_done", "h_done", "hi_done", "lo_done", "down_done",
                     "yt_ready", "y_turned", "x_done")
        b_g = (pr.bank[0], pr.bank[1], pr.bank[4])
        b_u = (pr.bank[2], pr.bank[3], pr.bank[6])
        b_gate = (pr.bank[4], pr.bank[6])
        b_y, b_turn = pr.bank[5], pr.bank[7]
        tg = pr.gates[:, 4 + layer:5 + layer]
        hi, lo = pr.big_hi, pr.big_lo
        NROUTE = {0: 20, 1: 20, 2: 0, 3: 30}[layer]
        PREP_DVE = {0: 7, 1: 6, 2: 8, 3: 8}[layer]
        PREP_ACT = {0: 0, 1: 0, 2: 3, 3: 0}[layer]
        LOADED = 16 * {0: 2, 1: 2, 2: 3, 3: 2}[layer]

        def front(i):
            stages = [[("norm", i)], [("scale", i)], [("turn", i)]]
            return stages + ([[("logits", i)], [("gates", i)]] if E else [])

        def order(i):
            steps = []
            more = not (isinstance(i, int) and i == NI - 1)
            late = not (isinstance(i, int) and i == 0)
            at = {0: (0, 1, 2, 3, 3), 1: (3, 5, 7, 8, 14), 2: (0, 1, 2), 3: (0, 1, 3, 3, 4)}[layer]
            stages = front(i + 1) if more else []
            for c in range(C):
                steps += [("up", i, c)]
                if c >= 1 or late:
                    steps += [("split", i, c - 1) if c >= 1 else ("split", i - 1, C - 1)]
                if c >= 2 or late:
                    steps += [("down", i, c - 2) if c >= 2 else ("down", i - 1, C + c - 2)]
                if late and c == 1:
                    steps += [("y_copy", i - 1)]
                if late and c == 2:
                    steps += [("y_turn", i - 1)]
                for k, stage in enumerate(stages):
                    if at[k] == c:
                        steps += stage
            return steps

        flush = [("split", NI - 1, C - 1), ("down", NI - 1, C - 2), ("down", NI - 1, C - 1), ("y_copy", NI - 1), ("y_turn", NI - 1)]

        def passes(eng, does):
            def run(steps):
                for step, *at in steps:
                    if step in does:
                        does[step](*at)
            for stage in front(0):
                run(stage)
            run(order(0))
            with eng.Fori(1, NI - 1) as i:
                run(order(i))
            run(order(NI - 1))
            run(flush)

        with nc.Block() as block:
            @block.sync
            def _(sp):
                if layer == 0:
                    loads = ((sel_rows[:], ins["L0_ffn_expert_sel"]), (extra[:, 0:1], ins["L0_ffn_route_scale"].partition_broadcast(P)))
                elif layer == 1:
                    loads = ((router[:], ins["L1_ffn_router_w"]), (bias_col[:], ins["L1_ffn_bias"].rearrange("(p a) -> p a", a=1)))
                elif layer == 2:
                    loads = ((wi[:, 0:3], ins["L2_ffn_w_gate"].rearrange("(c p) d -> p c d", p=P)),
                             (wi[:, 3:6], ins["L2_ffn_w_up"].rearrange("(c p) d -> p c d", p=P)),
                             (wi[:, 6:9], ins["L2_ffn_w_down"].rearrange("d (c p) -> d c p", p=P)))
                else:
                    loads = ((router[:], ins["L3_ffn_gate_w"]), (extra[:], ins["L3_ffn_gate_bias"].partition_broadcast(P)))
                for dst, src in loads:
                    sp.dma_start(dst, src).then_inc(sem["loaded"], 16)

            @block.gpsimd
            def _(pool):
                pool.wait_ge(sem["prep_dve"], 2)

                def norm(i):
                    pool.wait_ge(sem["moments"], i + 1)
                    pool.tensor_tensor(ve[:], mv[:, :, 1], eps[:], ALU.add).then_inc(sem["var_eps"], 1)
                    pool.wait_ge(sem["var_eps"], i + 1)
                    need(pool, sem["xn_ready"], i)
                    pool.tensor_tensor(rstd[:], ve[:], neg_half[:], ALU.pow).then_inc(sem["rstd"], 1)

                passes(pool, {"norm": norm})

            @block.tensor
            def _(pe):
                pe.wait_ge(sem["loaded"], LOADED)
                if layer == 0:
                    pe.transpose(b_turn[:, 0:E0], sel_rows[:], pr.id(E0)).then_inc(sem["prep_pe"], 1)
                if layer == 2:
                    for m in range(3):
                        pe.wait_ge(sem["prep_dve"], 2 + m + 1)
                        for k in range(3):
                            last = pe.transpose(pr.bank[m][:, k * P:(k + 1) * P], wf[:, 3 * m + k], pr.id())
                        last.then_inc(sem["prep_pe"], 1)
                pe.wait_ge(sem["prep_dve"], PREP_DVE)

                def turn(i):
                    pe.wait_ge(sem["xn_ready"], i + 1)
                    need(pe, sem["x_done"], i - 1)
                    need(pe, sem["gts_ready"] if E else sem["xt_lo"], i)
                    for t in range(T):
                        last = pe.transpose(b_turn[:, t * P:(t + 1) * P], xn[:, t], pr.id())
                    last.then_inc(sem["xn_turned"], 1)

                def logits(i):
                    pe.wait_ge(sem["xt_raw"], i + 1)
                    pe.wait_ge(sem["xt_lo"], i + 1)
                    for t in range(T):
                        last = pe.matmul(b_turn[:, t * E:(t + 1) * E], xt_raw[:, t * P:(t + 1) * P], router[:], start=True, stop=True)
                    last.then_inc(sem["logits_done"], 1)

                def gates(i):
                    pe.wait_ge(sem["routed"], i * NROUTE + NROUTE)
                    for t in range(T):
                        last = pe.transpose(b_turn[:, t * P:(t + 1) * P], gx[:, t].rearrange("p e u -> p (e u)"), pr.id())
                    last.then_inc(sem["gates_turned"], 1)

                def up(i, c):
                    m = rows(c)
                    first, second, _down = weights_at(c)
                    xh = xt_hi[:, bass.ds(i, 1)].rearrange("p a t -> p (a t)")
                    xl = xt_lo[:, bass.ds(i, 1)].rearrange("p a t -> p (a t)")
                    pe.wait_ge(sem["xt_lo"], i + 1)
                    need(pe, sem["h_done"], i * C + (c - distance(c) + 1))
                    for at, bank in ((first, b_g[c % NS]),) + (((second, b_u[c % NS]),) if HAS_UP else ()):
                        pe.matmul(bank[0:m], hi[:, at:at + m], xh, start=True, stop=False)
                        pe.matmul(bank[0:m], hi[:, at:at + m], xl, start=False, stop=False)
                        last = pe.matmul(bank[0:m], lo[:, at:at + m], xh, start=False, stop=True)
                    last.then_inc(sem["up_done"], 1)
                    if c in GATED and (layer != 1 or c % 3 == 0):
                        pe.wait_ge(sem["gts_ready"], i + 1)
                        need(pe, sem["h_done"], i * C + (c - gate_distance(c) + 1))
                        lhs = sel[:, c // 3:c // 3 + 1].to_broadcast([P, P]) if layer == 1 else sel[:, c * P:(c + 1) * P]
                        pe.matmul(b_gate[gate_slot(c)][:], lhs, gts[:, bass.ds(i, 1)].rearrange("p a t -> p (a t)"),
                                  start=True, stop=True).then_inc(sem["gate_done"], 1)

                def down(i, c):
                    m, r, at = rows(c), c % R, weights_at(c)[2]
                    pe.wait_ge(sem["lo_done"], i * C + (c + 1))
                    if c == 0:
                        need(pe, sem["yt_ready"], i)
                    pe.matmul(b_y[:], hi[0:m, at:at + P], h_hi[0:m, r], start=(c == 0), stop=False)
                    pe.matmul(b_y[:], hi[0:m, at:at + P], h_lo[0:m, r], start=False, stop=False)
                    pe.matmul(b_y[:], lo[0:m, at:at + P], h_hi[0:m, r], start=False, stop=(c == C - 1)).then_inc(sem["down_done"], 1)

                def y_turn(i):
                    pe.wait_ge(sem["yt_ready"], i + 1)
                    if E:
                        if isinstance(i, int) and i == NI - 1:
                            pe.wait_ge(sem["gts_ready"], NI)
                        else:
                            pe.wait_ge(sem["gts_ready"], i + 2)
                    else:
                        pe.wait_ge(sem["xt_lo"], NI if isinstance(i, int) and i == NI - 1 else i + 2)
                    if isinstance(i, int) and i == NI - 1:
                        pe.wait_ge(sem["x_done"], i)
                    for t in range(T):
                        last = pe.transpose(b_turn[:, t * P:(t + 1) * P], yt[:, t * P:(t + 1) * P], pr.id())
                    last.then_inc(sem["y_turned"], 1)

                passes(pe, {"turn": turn, "logits": logits, "gates": gates, "up": up, "down": down, "y_turn": y_turn})

            @block.scalar
            def _(act):
                if layer == 2:
                    for m in range(3):
                        act.wait_ge(sem["prep_pe"], m + 1)
                        act.copy(hi[:, m * 384:(m + 1) * 384], pr.bank[m][:, 0:384]).then_inc(sem["prep_act"], 1)
                if layer == 1:
                    act.wait_ge(sem["loaded"], LOADED)

                def turn(i):
                    act.wait_ge(sem["xn_turned"], i + 1)
                    if E:
                        need(act, sem["logits_done"], i)
                        act.copy(xt_raw[:], b_turn[:]).then_inc(sem["xt_raw"], 1)
                    act.copy(xt_hi[:, bass.ds(i, 1)].rearrange("p a t -> p (a t)"), b_turn[:]).then_inc(sem["xt_hi"], 1)

                def logits(i):
                    scores = b_turn[:, 0:T * E].rearrange("p (t e) -> p t e", e=E)
                    if layer == 1:
                        act.wait_ge(sem["logits_less"], i + 1)
                        act.activation(pe_[:], p1[:], ACT.Exp).then_inc(sem["logits_exp"], 1)
                    else:
                        act.wait_ge(sem["logits_done"], i + 1)
                        need(act, sem["routed"], i * NROUTE)
                        act.activation(pe_[:], scores, ACT.Exp, scale=-1.0).then_inc(sem["logits_exp"], 1)

                def gates(i):
                    act.wait_ge(sem["gates_turned"], i + 1)
                    need(act, sem["gts_ready"], i)
                    act.activation(hg[:].bitcast(F32R), b_turn[:], ACT.Copy, scale=pr.c("a8" if layer == 0 else "a16")).then_inc(sem["gates_hi"], 1)

                def up(i, c):
                    m = rows(c)
                    act.wait_ge(sem["up_done"], i * C + (c + 1))
                    need(act, sem["h_done"], i * C + (c + 1 - R))
                    act.activation(a[0:m, c % R], b_g[c % NS][0:m], FUNC).then_inc(sem["act_done"], 1)

                def split(i, c):
                    m = rows(c)
                    act.wait_ge(sem["h_done"], i * C + (c + 1))
                    if isinstance(i, int) or R != C or c != C - 1:
                        need(act, sem["down_done"], i * C + (c + 1 - R))
                    act.copy(h_hi[0:m, c % R], h[0:m, c % R]).then_inc(sem["hi_done"], 1)

                def y_copy(i):
                    act.wait_ge(sem["down_done"], i * C + C)
                    if isinstance(i, int) and i == NI - 1:
                        act.wait_ge(sem["y_turned"], i)
                    if layer == 1:
                        act.activation(yt[:], b_y[:], ACT.Identity, bias=bias_col[:]).then_inc(sem["yt_ready"], 1)
                    else:
                        act.copy(yt[:], b_y[:]).then_inc(sem["yt_ready"], 1)

                passes(act, {"turn": turn, "logits": logits, "gates": gates, "up": up, "split": split, "y_copy": y_copy})

            @block.vector
            def _(dve):
                count = [0]

                def prep(ins_):
                    count[0] += 1
                    ins_.then_inc(sem["prep_dve"], 1)
                    dve.wait_ge(sem["prep_dve"], count[0])
                prep(dve.memset(eps[:], LN_EPS))
                prep(dve.memset(neg_half[:], -0.5))
                if layer == 2:
                    dve.wait_ge(sem["loaded"], LOADED)
                    for m in range(3):
                        prep(dve.tensor_scalar(wf[:, 3 * m:3 * m + 3], wi[:, 3 * m:3 * m + 3], 1.0 / 127.0, None, ALU.mult))
                    for m in range(3):
                        cols = slice(m * 384, (m + 1) * 384)
                        dve.wait_ge(sem["prep_act"], m + 1)
                        prep(dve.tensor_tensor(lo[:, cols], pr.bank[m][:, 0:384], hi[:, cols].bitcast(F32), ALU.subtract))
                if E:
                    prep(dve.memset(gx[:], 0.0))
                    prep(dve.memset(cand[:], SENTINEL))
                    prep(dve.memset(want[:], SENTINEL))
                    prep(dve.tensor_copy(sel[:], pr.c({0: "self0", 1: "e8", 3: "self3"}[layer])))
                    dve.wait_ge(sem["loaded"], LOADED)
                if layer == 0:
                    dve.wait_ge(sem["prep_pe"], 1)
                    prep(dve.tensor_copy(router[:], b_turn[:, 0:E0]))
                if layer == 3:
                    prep(dve.memset(gs[:], SENTINEL))
                    prep(dve.memset(gwant[:], SENTINEL))
                PREPARED = count[0]
                assert PREPARED == PREP_DVE, PREPARED

                def norm(i):
                    for t in range(T):
                        last = dve.bn_stats(st6[:, t:t + 1], pr.x[:, bass.ds(i * T + t, 1)])
                    last.then_inc(sem["stats"], 1)
                    dve.wait_ge(sem["stats"], i + 1)
                    need(dve, sem["rstd"], i)
                    settled(dve, sem)
                    for t in range(T):
                        last = dve.bn_aggr(mv[:, t], st6[:, t])
                    last.then_inc(sem["moments"], 1)

                def scale(i):
                    dve.wait_ge(sem["rstd"], i + 1)
                    need(dve, sem["xn_turned"], i)
                    for t in range(T):
                        last = dve.tensor_scalar(xn[:, t:t + 1], pr.x[:, bass.ds(i * T + t, 1)], mv[:, t, 0:1], rstd[:, t:t + 1],
                                                 ALU.subtract, ALU.mult)
                    last.then_inc(sem["xn_ready"], 1)

                def turn(i):
                    dve.wait_ge(sem["xt_hi"], i + 1)
                    at = bass.ds(i, 1)
                    dve.tensor_tensor(xt_lo[:, at].rearrange("p a t -> p (a t)"), b_turn[:],
                                      xt_hi[:, at].rearrange("p a t -> p (a t)").bitcast(F32), ALU.subtract).then_inc(sem["xt_lo"], 1)

                def logits(i):
                    done = [0]

                    def step(ins_, k=1, settle=False):
                        done[0] += k
                        ins_.then_inc(sem["routed"], k)
                        dve.wait_ge(sem["routed"], i * NROUTE + done[0])
                        if settle:
                            settled(dve, sem)

                    def choose(cand, top, want, left, k):
                        for t in range(T):
                            last = dve.max(top[:, t], cand[:, t])
                        step(last)
                        step(dve.tensor_copy(want[:, :, 0:k], top[:, :, 0:k]), settle=True)
                        for t in range(T):
                            last = dve.match_replace(left[:, t], want[:, t], cand[:, t], TAKEN)
                        step(last)

                    def per_token(v):
                        return v[:].unsqueeze(2).to_broadcast([P, T, E])

                    need(dve, sem["gates_turned"], i)
                    if layer == 1:
                        scores = b_turn[:, 0:T * E].rearrange("p (t e) -> p t e", e=E)
                        dve.wait_ge(sem["logits_done"], i + 1)
                        need(dve, sem["logits_exp"], i)
                        step(dve.tensor_reduce(total[:], scores, AX_X, ALU.max))
                        dve.tensor_tensor(p1[:], scores, per_token(total), ALU.subtract).then_inc(sem["logits_less"], 1)
                        dve.wait_ge(sem["logits_exp"], i + 1)
                        step(dve.tensor_reduce(total2[:], pe_[:], AX_X, ALU.add))
                        step(dve.reciprocal(total3[:], total2[:]))
                        step(dve.tensor_tensor(cand[:, :, 0:E], pe_[:], per_token(total3), ALU.mult), settle=True)
                        choose(cand, top8, want, left, K)
                        for u in range(2):
                            last = dve.scalar_tensor_tensor(gx[:, :, :, u], left[:, :, 0:E], 2 * LOWEST, cand[:, :, 0:E], ALU.is_lt, ALU.mult)
                        step(last, NROUTE - done[0])
                        return
                    dve.wait_ge(sem["logits_exp"], i + 1)
                    step(dve.tensor_scalar(p1[:], pe_[:], 1.0, None, ALU.add))
                    if layer == 0:
                        score = cand[:, :, 0:E]
                        step(dve.reciprocal(score, p1[:]), settle=True)
                    else:
                        score = picked[:]
                        step(dve.reciprocal(pe_[:], p1[:]))
                        step(dve.tensor_tensor(score, pe_[:], extra[:].unsqueeze(1).to_broadcast([P, T, E]), ALU.add))
                        pairs = score.rearrange("p t (g e) -> p t g e", e=2)
                        step(dve.tensor_tensor(gs[:, :, 0:NG3], pairs[:, :, :, 0], pairs[:, :, :, 1], ALU.add), settle=True)
                        choose(gs, gtop, gwant, gleft, 2)
                        for e in range(2):
                            last = dve.scalar_tensor_tensor(cand[:, :, 0:E].rearrange("p t (g e) -> p t g e", e=2)[:, :, :, e], gleft[:, :, 0:NG3],
                                                            2 * LOWEST, pairs[:, :, :, e], ALU.is_lt, ALU.mult)
                        step(last, settle=True)
                    choose(cand, top8, want, left, K)
                    step(dve.scalar_tensor_tensor(p1[:], left[:, :, 0:E], 2 * LOWEST, score, ALU.is_lt, ALU.mult))
                    step(dve.tensor_reduce(total[:], p1[:], AX_X, ALU.add))
                    if layer == 0:
                        step(dve.tensor_scalar(total2[:], total[:], 1e-9, None, ALU.max))
                        step(dve.reciprocal(total[:], total2[:]))
                        step(dve.tensor_scalar(total3[:], total[:], extra[:, 0:1], None, ALU.mult))
                    else:
                        step(dve.tensor_scalar(total2[:], total[:], 1e-20, None, ALU.add))
                        step(dve.reciprocal(total[:], total2[:]))
                        step(dve.tensor_scalar(total3[:], total[:], SC3, None, ALU.mult))
                    step(dve.tensor_tensor(gx[:, :, :, 0:2], p1[:].unsqueeze(3).to_broadcast([P, T, E, 2]),
                                           total3[:].unsqueeze(2).unsqueeze(3).to_broadcast([P, T, E, 2]), ALU.mult), NROUTE - done[0])

                def gates(i):
                    dve.wait_ge(sem["gates_hi"], i + 1)
                    dve.tensor_tensor(gts[:, bass.ds(i, 1)].rearrange("p a t -> p (a t)"), b_turn[:], hg[:], ALU.add).then_inc(sem["gts_ready"], 1)

                def up(i, c):
                    m, r = rows(c), c % R
                    dve.wait_ge(sem["act_done"], i * C + (c + 1))
                    need(dve, sem["lo_done"], i * C + (c + 1 - R))
                    if c in GATED:
                        e = c // 3 if layer == 1 else c
                        gate = b_gate[gate_slot(c)][0:m]
                        n_gates = 8 if layer == 1 else len(GATED)
                    if HAS_UP:
                        last = dve.tensor_tensor(h[0:m, r], a[0:m, r], b_u[c % NS][0:m], ALU.mult)
                        if c in GATED:
                            last.then_inc(sem["half_done"], 1)
                            dve.wait_ge(sem["half_done"], i * len(GATED) + (c + 1))
                            dve.wait_ge(sem["gate_done"], i * n_gates + (e + 1))
                            last = dve.tensor_tensor(h[0:m, r], h[0:m, r], gate, ALU.mult)
                    else:
                        dve.wait_ge(sem["gate_done"], i * n_gates + (e + 1))
                        last = dve.tensor_tensor(h[0:m, r], a[0:m, r], gate, ALU.mult)
                    last.then_inc(sem["h_done"], 1)

                def split(i, c):
                    m, r = rows(c), c % R
                    dve.wait_ge(sem["hi_done"], i * C + (c + 1))
                    dve.tensor_tensor(h_lo[0:m, r], h[0:m, r], h_hi[0:m, r].bitcast(F32), ALU.subtract).then_inc(sem["lo_done"], 1)

                def y_turn(i):
                    dve.wait_ge(sem["y_turned"], i + 1)
                    xb = pr.x[:, tiles(i, T)]
                    dve.scalar_tensor_tensor(xb, b_turn[:].rearrange("p (t d) -> p t d", t=T), tg, xb, ALU.mult, ALU.add).then_inc(sem["x_done"], 1)

                passes(dve, {"norm": norm, "scale": scale, "turn": turn, "logits": logits, "gates": gates, "up": up, "split": split,
                             "y_turn": y_turn})



def store(pr):
    stored = pr.sem("stored")
    with pr.nc.Block() as block:

        @block.sync
        def _(sp):
            ov = pr.out.rearrange("b (t p) d -> p (b t) d", p=P)
            for h in range(2):
                sp.dma_start(ov[:, 8 * h:8 * h + 8], pr.x[:, 8 * h:8 * h + 8]).then_inc(stored, 16)
            sp.wait_ge(stored, 32)


def build(nc, ins, out):
    with ExitStack() as ctx:
        pr = Program(nc, ctx, ins, out)
        setup(pr)
        attention(pr, 0, own_keys=False, masked=False, biased=True, scale=HD ** -0.5)
        ffn(pr, 0)
        attention(pr, 1, own_keys=True, masked=False, biased=False, scale=HD ** -0.5)
        ffn(pr, 1)
        attention(pr, 2, own_keys=False, masked=True, biased=True, scale=D ** -0.5)
        ffn(pr, 2)
        attention3(pr)
        ffn(pr, 3)
        store(pr)


def constants():
    import numpy as np
    p = np.arange(P)[:, None]
    i = np.arange(P)[None, :]
    j = np.arange(4 * P)[None, :]
    part = (p % 32) // HD
    pair = np.arange(2 * P)[None, :]
    head_sel = -((p // 32 == 2 * (pair // P) + (pair % P) // 64) & (p % 32 < 2)).astype(np.float32)
    cols = {
        "ident": p == i,
        "aq": -(part >= 2).astype(np.float32), "ak": -(part % 2 == 1).astype(np.float32),
        "am": -(p % 32 != 0).astype(np.float32), "amask": -(p >= 64).astype(np.float32),
        "a8": -(p % 8 != 0).astype(np.float32), "a16": -(p % 16 != 0).astype(np.float32),
        "half": p // 64 == np.arange(2)[None, :], "head4": p // 32 == np.arange(4)[None, :],
        "selc": head_sel, "selc0": head_sel * (pair % 64 != 0),
        "negs": -((p % 32 < 2) & (i >= 0)).astype(np.float32),
        "i2": p % 64 == i % 64,
        "self0": (p // 8 == 4 * (j // P) + (j % P) // 32) & (p % 8 < 2),
        "self3": (p // 16 == 2 * (j // P) + (j % P) // 64) & (p % 16 < 2),
        "e8": (p // 16 == np.arange(8)[None, :]) & (p % 16 < 2),
        "onesb": p // 64 == i // 64,
    }
    out = np.zeros((P, NCONST), np.float32)
    for name, (at, n) in CONST.items():
        out[:, at:at + n] = cols[name]
    return out


_INS = ["x", "ctx_1024", "mask_Bx1xSxS2_ff0", "g_xattn", "g_ffn",
        "L0_xattn_Wq", "L0_xattn_bq", "L0_xattn_Wkv", "L0_xattn_bkv", "L0_xattn_Wo", "L0_xattn_bo",
        "L0_ffn_expert_sel", "L0_ffn_keys", "L0_ffn_values", "L0_ffn_route_scale",
        "L1_xattn_Wq", "L1_xattn_Wk", "L1_xattn_Wv", "L1_xattn_gate", "L1_xattn_ln_g", "L1_xattn_ln_b", "L1_xattn_Wp", "L1_xattn_bp",
        "L1_ffn_router_w", "L1_ffn_w1", "L1_ffn_v1", "L1_ffn_w2", "L1_ffn_bias",
        "L2_xattn_Wq", "L2_xattn_bq", "L2_xattn_Wk", "L2_xattn_bk", "L2_xattn_Wv", "L2_xattn_bv", "L2_xattn_Wo", "L2_xattn_bo",
        "L2_ffn_w_gate", "L2_ffn_w_up", "L2_ffn_w_down",
        "L3_xattn_Wq", "L3_xattn_Wk", "L3_xattn_Wv", "L3_xattn_Wo", "L3_xattn_bo",
        "L3_ffn_gate_w", "L3_ffn_gate_bias", "L3_ffn_w_gate", "L3_ffn_w_up", "L3_ffn_w_down",
        "L3_ffn_sw_gate", "L3_ffn_sw_up", "L3_ffn_sw_down"]


def kernel(**inputs):
    import numpy as _np
    import concourse.bacc as _bacc
    from concourse import mybir as _mybir
    from concourse.bass_utils import run_bass_kernel_spmd as _run

    nc = _bacc.Bacc("TRN2", target_bir_lowering=False, num_devices=1)
    arrays, ins = {}, {}
    values = {name: _np.ascontiguousarray(inputs[name]) for name in _INS}
    values["const"] = constants()
    for name, a in values.items():
        arrays[f"in_{name}_dram"] = a
        ins[name] = nc.dram_tensor(f"in_{name}_dram", a.shape, _mybir.dt.from_np(a.dtype), kind="ExternalInput").ap()
    out = nc.dram_tensor("out_0_dram", (B, S, D), F32, kind="ExternalOutput").ap()
    build(nc, ins, out)
    r = _run(nc, [arrays], core_ids=[0])
    return r.results[0]["out_0_dram"]
```

```python
from contextlib import ExitStack

import concourse.bass as bass
from concourse import mybir

F32 = mybir.dt.float32
F32R = mybir.dt.float32r
BF16 = mybir.dt.bfloat16
I32 = mybir.dt.int32
ALU = mybir.AluOpType
ACT = mybir.ActivationFunctionType
AX_X = mybir.AxisListType.X

P = 128
B, S, D, S2 = 8, 256, 128, 64
NT = B * S // P
LN_EPS = 1e-5
H, HD = 16, 8
NG, GH = 4, 4
H3, HD3 = 8, 64
E0, K0, X0 = 16, 4, 32
E1, K1, X1 = 8, 2, 352
HID2 = 384
E3, K3, X3 = 8, 2, 64
NG3 = 4
SC3 = 2.5
TOK = 512
NI = B * S // TOK
LOWEST = -1e30

CONST = {}
_at = 0
for _name, _n in (("ident", 128), ("aq", 1), ("ak", 1), ("am", 1), ("amask", 1), ("a8", 1), ("a16", 1), ("half", 2), ("half_past", 2), ("head4", 4), ("am1", 1), ("neg1", 1),
                  ("selc", 256), ("i2", 128), ("self0", 512), ("self3", 512), ("e8", 8),
                  ("sum3", 512)):
    CONST[_name] = (_at, _n)
    _at += _n
NCONST = _at


def need(eng, sem, value):
    if isinstance(value, int) and value <= 0:
        return
    eng.wait_ge(sem, value)


def settled(eng, sem):
    eng.sem_inc(sem["settled"], 1)


class Program:

    def __init__(self, nc, ctx, ins, out):
        self.nc, self.ins, self.out = nc, ins, out
        self.ctx = ctx
        sb = self.sb
        self.x = sb("x", [P, NT, D], F32)
        self.const = sb("const", [P, NCONST], F32)
        self.ctx_t2 = sb("ctx_t2", [P, B, 2, S2], F32)
        self.ctx_hi = sb("ctx_hi", [P, B * S2], F32R)
        self.ctx_lo = sb("ctx_lo", [P, B * S2], F32R)
        self.gates = sb("gates", [P, 8], F32)
        self.w_att = sb("w_att", [P, 3, 4, D], F32)
        self.big_hi = sb("big_hi", [P, 8704], F32R)
        self.big_lo = sb("big_lo", [P, 8704], F32R)
        self.st6 = sb("st6", [P, NT, 6], F32)
        self.eps = sb("eps", [P, NT], F32)
        self.neg_half = sb("neg_half", [P, NT], F32)
        self.bank = [ctx.enter_context(nc.psum_tensor(f"bank{i}", [P, 512], F32)) for i in range(8)]
        self.nsem = 0

    def sb(self, name, shape, dt):
        return self.ctx.enter_context(self.nc.sbuf_tensor(name, shape, dt))

    def sem(self, name):
        self.nsem += 1
        return self.nc.alloc_semaphore(name=f"s{self.nsem}_{name}")

    def sems(self, *names):
        return {name: self.sem(name) for name in names}

    def c(self, name):
        a, n = CONST[name]
        return self.const[:, a:a + n]

    def id(self, n=P):
        return self.const[0:n, 0:n]


def tiles(b, n):
    return bass.ds(b * n, n)



def setup(pr):
    nc, ins = pr.nc, pr.ins
    with nc.cleanup_on_exit(), ExitStack() as scope:
        tmp = scope.enter_context(nc.sbuf_tensor("ctx_rows", [P, 4, D], F32))
        x_in, const_in, ctx_in, g_in, w_in = (pr.sem(n) for n in ("x_in", "const_in", "ctx_in", "g_in", "w_in"))
        eps_set, ctx_turned, ctx_hi, ctx_lo = (pr.sem(n) for n in ("eps_set", "ctx_turned", "ctx_hi", "ctx_lo"))
        turn = pr.bank[0]
        with nc.Block() as block:
            @block.sync
            def _(sp):
                sp.dma_start(pr.const[:], ins["const"]).then_inc(const_in, 16)
                sp.dma_start(tmp[:], ins["ctx_1024"].rearrange("(a b) s d -> (b s) a d", b=2)).then_inc(ctx_in, 16)
                xv = ins["x"].rearrange("b (t p) d -> p (b t) d", p=P)
                for h in range(2):
                    sp.dma_start(pr.x[:, 8 * h:8 * h + 8], xv[:, 8 * h:8 * h + 8]).then_inc(x_in, 16)
                sp.dma_start(pr.gates[:, 0:4], ins["g_xattn"].partition_broadcast(P)).then_inc(g_in, 16)
                sp.dma_start(pr.gates[:, 4:8], ins["g_ffn"].partition_broadcast(P)).then_inc(g_in, 16)
                w = pr.w_att
                for dst, src in (
                        (w[:, 0, 0], ins["L0_xattn_Wq"]), (w[:, 0, 1:3], ins["L0_xattn_Wkv"].rearrange("p (a n) -> p a n", a=2)),
                        (w[:, 0, 3], ins["L0_xattn_Wo"]),
                        (w[:, 1, 0], ins["L1_xattn_Wq"]), (w[:, 1, 1], ins["L1_xattn_Wk"]),
                        (w[:, 1, 2], ins["L1_xattn_Wv"]), (w[:, 1, 3], ins["L1_xattn_Wp"]),
                        (w[:, 2, 0], ins["L2_xattn_Wq"]), (w[:, 2, 1], ins["L2_xattn_Wk"]),
                        (w[:, 2, 2], ins["L2_xattn_Wv"]), (w[:, 2, 3], ins["L2_xattn_Wo"])):
                    sp.dma_start(dst, src).then_inc(w_in, 16)
                sp.wait_ge(x_in, 32)
                sp.wait_ge(w_in, 11 * 16)

            @block.tensor
            def _(pe):
                pe.wait_ge(const_in, 16)
                pe.wait_ge(ctx_in, 16)
                for a in range(4):
                    last = pe.transpose(turn[:, a * P:(a + 1) * P], tmp[:, a], pr.id())
                last.then_inc(ctx_turned, 1)

            @block.scalar
            def _(act):
                act.wait_ge(g_in, 32)
                act.activation(pr.gates[:], pr.gates[:], ACT.Tanh)
                act.wait_ge(ctx_turned, 1)
                act.copy(pr.ctx_hi[:], turn[:]).then_inc(ctx_hi, 1)

            @block.vector
            def _(dve):
                dve.memset(pr.eps[:], LN_EPS)
                dve.memset(pr.neg_half[:], -0.5)
                dve.wait_ge(ctx_hi, 1)
                turned = turn[:].rearrange("p (b s) -> p b s", s=S2)
                dve.tensor_tensor(pr.ctx_lo[:], turn[:], pr.ctx_hi[:].bitcast(F32), ALU.subtract)
                dve.tensor_copy(pr.ctx_t2[:], turned.unsqueeze(2).to_broadcast([P, B, 2, S2]))
                dve.wait_ge(x_in, 32)
                for tile in range(NT):
                    dve.bn_stats(pr.st6[:, tile], pr.x[:, tile])



def attention(pr, layer, own_keys, masked, biased, scale, extra=None):
    nc, ins = pr.nc, pr.ins
    gated = own_keys
    n = f"L{layer}"
    NS = 5 if own_keys else 1
    U = NG * NS
    MASK_SCALE = -1e9 / scale
    with nc.cleanup_on_exit(), ExitStack() as scope:
        def sb(name, shape, dt=F32):
            return scope.enter_context(nc.sbuf_tensor(f"{n}_{name}", shape, dt))

        wf = sb("wf", [P, 4, D]) if gated else None
        wx = sb("wx", [P, 4, NG * P], F32R)
        kc_all = sb("kc_all", [P, NG, B, S2], F32R)
        kc = sb("kc", [P, NG, GH, S2], F32R)
        vc_all = sb("vc_all", [P, B, D])
        vc = sb("vc", [P, H // 2, 32])
        bias_row = sb("bias_row", [1, 4, D]) if biased else None
        bias_x = sb("bias_x", [1, 2, NG * P]) if biased else None
        bias_c = sb("bias_c", [P, 2, NG])
        bias_ca = sb("bias_ca", [P, 2, NG])
        ones1 = sb("ones1", [1, P])
        bo = sb("bo", [P, D])
        selc = sb("selc", [P, 2, P], F32R) if not gated else None
        mv = sb("mv", [P, NT, 2])
        ve = sb("ve", [P, NT])
        rstd = sb("rstd", [P, NT])
        xn = sb("xn", [P, 2, D])
        xt_hi = sb("xt_hi", [P, S], F32R)
        xt_lo = sb("xt_lo", [P, S], F32R)
        part = sb("part", [P, 2, S])
        q = sb("q", [P, NG, S], F32R)
        hk = q[:, 0:2].rearrange("p g s -> p (g s)").bitcast(F32)
        mc = sb("mc", [P, 2, GH])
        mx = sb("mx", [P, 2, 2, GH, 32])
        hm = sb("hm", [P, S])
        mt = sb("mt", [P, 2, S], F32R)
        pt = sb("pt", [P, 2, 2 * NS, 512])
        ot = sb("ot", [P, 2, S])
        rc = sb("rc", [P, 2 * H])
        on = sb("on", [P, 2, D])
        o2t = sb("o2t", [P, S])
        if own_keys:
            xt_raw = sb("xt_raw", [P, S])
            k = sb("k", [P, NG, S], F32R)
            ms = sb("ms", [P, 2, GH])
            vs = sb("vs", [P, 2, H, 32])
            v_own = sb("v_own", [P, 2, D])
            hq = sb("hq", [P, S])
            gate_row = sb("gate_row", [P, H])
            wvg = sb("wvg", [P, D])
            vg_all = sb("vg_all", [P, B, D])
            ln_gb = sb("ln_gb", [P, 2])
            o16 = sb("o16", [P, 2, D], BF16)
            st6b = sb("st6b", [P, 2, 6])
            mvb = sb("mvb", [P, 2, 2])
            veb = sb("veb", [P, 2])
            rstdb = sb("rstdb", [P, 2])
            raw = sb("raw", [P, 1, 1088])
        if masked:
            mask2 = sb("mask2", [P, NT, 2, S2])
            mk = sb("mk", [P, 2, P])
            hmk = sb("hmk", [P, S])
            msk = sb("msk", [P, S], F32R)
            msk_all = sb("msk_all", [P, B, S], F32R)
            i2 = sb("i2", [P, P], F32R)
        if layer == 0:
            raw0 = sb("raw0", [P, 2, 512])

        sem = pr.sems("loaded", "prep_pe", "prep_act", "prep_dve", "settled", "prep_pool", "stats", "moments", "var_eps",
                     "rstd", "xn_ready", "xn_turned", "xt_hi", "xt_lo", "proj_done", "proj_hi", "qk_split", "kc_ready",
                     "sc_done", "sc_taken", "m_ready", "m_turned", "m_hi", "hq_ready", "m_split", "st_done", "exp_done", "v_proj",
                     "v_ready", "v_spread", "vc_ready", "pv_done", "ot_taken", "o_turned", "rc_ready", "o_norm", "o_stats", "o_moments", "o_round",
                     "o_var", "o_rstd", "on_ready", "on_turned", "o2t_ready", "y_done", "x_bias", "x_done", "mk_ready",
                     "mk_turned", "mk_hi", "mk_split", "mk_kept", "stage_in", "stage_hi", "stage_split", "w0_in")
        mask_a = sb("mask_a", [P, 1])
        DVE_WEIGHTS = 10 if biased else 9
        DVE_READY = DVE_WEIGHTS + 4 + (2 if gated else 1) + (2 if masked else 0)
        ACT_READY = 6 + (4 if gated else 0)
        POOL_READY = 6 + (7 if gated else 0)
        LOADED = 16 * {0: 4, 1: 4, 2: 7}[layer]
        on_ready = sem["on_ready"] if gated else sem["o_norm"]
        b_proj, b_turn, b_sc, b_st, b_mt, b_o = (pr.bank[0], pr.bank[1], pr.bank[2:4], pr.bank[4:6], pr.bank[6], pr.bank[7])
        w = [wf[:, i] if gated else pr.w_att[:, layer, i] for i in range(4)]
        w_raw = [pr.w_att[:, layer, i] for i in range(4)]
        tg = pr.gates[:, layer:layer + 1]

        def banks(step, b, g):
            return [(step, b, g, i) for i in range(NS)]

        def mixed(*lists):
            return [steps[k] for k in range(max(map(len, lists))) for steps in lists if k < len(steps)]

        first = [("mask_in", 0), ("scale", 0), ("turn", 0), ("mask", 0)] \
            + [s for g in (0, 1) for s in (("proj", 0, g), ("keys", 0, g))] + banks("scores", 0, 0) + [("proj", 0, 2), ("keys", 0, 2)] \
            + banks("scores", 0, 1) + [("maxima", 0, 0)]

        def order(b):
            more = not (isinstance(b, int) and b == B - 1)
            late = not (isinstance(b, int) and b == 0)

            def group(k):
                return [(b, k)] if k < NG else [(b + 1, k - NG)] if more else []
            begin = [[("values", b)], [], [], []]
            end = [[], [], [], []]
            if more:
                begin[0] += [("scale", b + 1), ("mask_in", b + 1)]
                end[0] += [("turn", b + 1)]
                end[1] += [("mask", b + 1)]
            if late:
                begin[2] += [("o_turn", b - 1), ("o_norm", b - 1)]
                begin[3] += [("o_scale", b - 1), ("on_turn", b - 1)]
                end[3] += [("y", b - 1)]
            old = [("pv", b - 1, 1, i) for i in range(NS)] if late else []
            new = [("pv", b, 0, i) for i in range(NS)]
            pv = [old[:3], old[3:] + [("spread", b)], new[:3], new[3:]]
            steps = []
            for g in range(NG):
                steps += begin[g]
                ahead = [s for at in group(g + 2) for s in banks("scores", *at)]
                steps += ahead[:1]
                for at in group(g + 3):
                    steps += [("proj", *at), ("keys", *at)]
                for at in group(g + 1):
                    steps += [("maxima", *at)]
                steps += mixed(banks("weights", b, g), ahead[1:], pv[g]) + end[g]
            return steps

        flush = [("pv", B - 1, 1, i) for i in range(NS)] + [("o_turn", B - 1), ("o_norm", B - 1), ("o_scale", B - 1), ("on_turn", B - 1),
                                                            ("y", B - 1)]

        def passes(eng, does):
            def run(steps):
                for step, *at in steps:
                    if step in does:
                        does[step](*at)
            run(first)
            run(order(0))
            run(order(1))
            with eng.Fori(2, B - 1) as b:
                run(order(b))
            run(order(B - 1))
            run(flush)

        with nc.Block() as block:
            @block.sync
            def _(sp):
                if biased:
                    names = {0: ("L0_xattn_bq", "L0_xattn_bkv", "L0_xattn_bo"), 2: ("L2_xattn_bq", "L2_xattn_bk", "L2_xattn_bv", "L2_xattn_bo")}[layer]
                    at = 0
                    for name in names:
                        m = ins[name].shape[0]
                        sp.dma_start(bias_row[0:1, :, :].rearrange("a r d -> a (r d)")[:, at:at + m],
                                     ins[name].rearrange("(a n) -> a n", a=1)).then_inc(sem["loaded"], 16)
                        at += m
                    total = 16 * len(names)
                else:
                    total = 0
                sp.dma_start(bo[:], ins[{0: "L0_xattn_bo", 1: "L1_xattn_bp", 2: "L2_xattn_bo"}[layer]].partition_broadcast(P)).then_inc(sem["loaded"], 16)
                if gated:
                    sp.dma_start(gate_row[:], ins["L1_xattn_gate"].rearrange("a h b c -> (a h b c)").partition_broadcast(P)).then_inc(sem["loaded"], 16)
                    sp.dma_start(ln_gb[:, 0:1], ins["L1_xattn_ln_g"].rearrange("(p a) -> p a", a=1)).then_inc(sem["loaded"], 16)
                    sp.dma_start(ln_gb[:, 1:2], ins["L1_xattn_ln_b"].rearrange("(p a) -> p a", a=1)).then_inc(sem["loaded"], 16)
                if masked:
                    for h in range(2):
                        sp.dma_start(mask2[:, :, h], ins["mask_Bx1xSxS2_ff0"].rearrange("b a (t p) s -> p (b a t) s", p=P)).then_inc(sem["loaded"], 16)
                if layer == 0:
                    sp.dma_start(raw0[:, 0].rearrange("p (e h) -> p e h", e=E0), ins["L0_ffn_keys"].rearrange("e p h -> p e h")).then_inc(sem["w0_in"], 16)
                    sp.dma_start(raw0[:, 1].rearrange("p (c v) -> p c v", c=4),
                                 ins["L0_ffn_values"].rearrange("(c e) h v -> (e h) c v", e=4)).then_inc(sem["w0_in"], 16)
                if own_keys:
                    def expert(e):
                        dst = raw[:, 0]
                        es = bass.ds(e, 1)
                        sp.dma_start(dst[:, 0:352].unsqueeze(1), ins["L1_ffn_w1"][es].rearrange("e p f -> p e f")).then_inc(sem["stage_in"], 16)
                        sp.dma_start(dst[:, 352:704].unsqueeze(1), ins["L1_ffn_v1"][es].rearrange("e p f -> p e f")).then_inc(sem["stage_in"], 16)
                        sp.dma_start(dst[:, 704:960].rearrange("p (e k v) -> p e k v", e=1, k=2),
                                     ins["L1_ffn_w2"][es, 0:256].rearrange("e (k p) v -> p e k v", p=P)).then_inc(sem["stage_in"], 16)
                        sp.dma_start(dst[0:96, 960:1088].unsqueeze(1), ins["L1_ffn_w2"][es, 256:352].rearrange("e p v -> p e v")).then_inc(sem["stage_in"], 16)
                    expert(0)
                    with sp.Fori(0, B - 1) as e:
                        sp.wait_ge(sem["stage_split"], e + 1)
                        expert(e + 1)

            @block.gpsimd
            def _(pool):
                pool.wait_ge(sem["moments"], 1)
                pool.tensor_tensor(ve[:], mv[:, :, 1], pr.eps[:], ALU.add).then_inc(sem["var_eps"], 1)
                pool.wait_ge(sem["var_eps"], 1)
                pool.tensor_tensor(rstd[:], ve[:], pr.neg_half[:], ALU.pow).then_inc(sem["rstd"], 1)
                pool.memset(mx[:], 0.0).then_inc(sem["prep_pool"], 1)
                pool.memset(kc[:].bitcast(F32), 0.0).then_inc(sem["prep_pool"], 1)
                pool.memset(vc[:], 0.0).then_inc(sem["prep_pool"], 1)
                pool.wait_ge(sem["prep_pool"], 3)
                pool.memset(vc[0:64, :, 8:9], 1.0).then_inc(sem["prep_pool"], 1)
                pool.wait_ge(sem["prep_pool"], 4)
                pool.memset(vc[64:128, :, 24:25], 1.0).then_inc(sem["prep_pool"], 1)
                pool.wait_ge(sem["prep_pool"], 5)
                if own_keys:
                    pool.memset(vs[:], 0.0).then_inc(sem["prep_pool"], 1)
                    pool.wait_ge(sem["prep_pool"], 6)
                    by_pair = vs[:].rearrange("p k (a s) c -> p k a s c", s=2)
                    for kt in range(2):
                        pool.memset(by_pair[:, kt, :, 0, 8:9], 1.0).then_inc(sem["prep_pool"], 1)
                        pool.memset(by_pair[:, kt, :, 1, 24:25], 1.0).then_inc(sem["prep_pool"], 1)
                    pool.wait_ge(sem["prep_pool"], 10)
                    for r, row in enumerate((0, 64)):
                        pool.memset(vc[row:row + 1], 0.0).then_inc(sem["prep_pool"], 1)
                        pool.wait_ge(sem["prep_pool"], 11 + r)
                pool.wait_ge(sem["loaded"], LOADED)
                pool.tensor_scalar(bo[:], bo[:], tg, None, ALU.mult).then_inc(sem["prep_pool"], 1)
                pool.wait_ge(sem["prep_dve"], DVE_READY)
                pool.wait_ge(sem["prep_act"], ACT_READY)
                pool.wait_ge(sem["prep_pool"], POOL_READY)

                def turn(b):
                    pool.wait_ge(sem["xn_ready"], b + 1)
                    xb = pr.x[:, tiles(b, 2)]
                    pool.tensor_tensor(xb, xb, bo[:].unsqueeze(1).to_broadcast([P, 2, D]), ALU.add).then_inc(sem["x_bias"], 1)

                def keys(b, g):
                    need(pool, sem["st_done"], b * U + (g + 1) * NS - U)
                    pool.tensor_tensor(kc[:, g], kc_all[:, g, bass.ds(b, 1)].bitcast(F32).to_broadcast([P, GH, S2]),
                                       pr.c("head4").unsqueeze(2).to_broadcast([P, GH, S2]), ALU.mult).then_inc(sem["kc_ready"], 1)

                def values(b):
                    need(pool, sem["pv_done"], b * 2)
                    src = vc_all[:, bass.ds(b, 1)].rearrange("p e (a s d) -> p (e a) s d", s=2, d=HD)
                    for s in range(2):
                        last = pool.tensor_tensor(vc[:, :, 16 * s:16 * s + HD], src[:, :, s],
                                                  pr.c("half_past" if gated else "half")[:, s:s + 1].unsqueeze(2).to_broadcast([P, H // 2, HD]), ALU.mult)
                    last.then_inc(sem["vc_ready"], 1)

                def spread(b):
                    values(b)
                    if own_keys:
                        pool.wait_ge(sem["v_ready"], b + 1)
                        need(pool, sem["pv_done"], b * 2)
                        settled(pool, sem)
                        dst = vs[:].rearrange("p k (a s) c -> p k a (s c)", s=2)
                        for kt in range(2):
                            for s in range(2):
                                src = v_own[:, kt].rearrange("p (a s d) -> p a s d", s=2, d=HD)[:, :, s]
                                last = pool.tensor_copy(dst[:, kt, :, 48 * s:48 * s + HD], src)
                        last.then_inc(sem["v_spread"], 1)
                        split(b)
                    if layer == 0 and isinstance(b, int) and b == 0:
                        split0()

                def split0():
                    pool.wait_ge(sem["w0_in"], 32)
                    for i in range(2):
                        part_of = slice(512 * i, 512 * i + 512)
                        pool.tensor_copy(pr.big_hi[:, part_of], raw0[:, i]).then_inc(sem["stage_hi"], 1)
                        pool.wait_ge(sem["stage_hi"], i + 1)
                        pool.tensor_tensor(pr.big_lo[:, part_of], raw0[:, i], pr.big_hi[:, part_of].bitcast(F32), ALU.subtract)

                def split(e):
                    pool.wait_ge(sem["stage_in"], e * 64 + 64)
                    for dst, op, in1 in ((pr.big_hi, None, None), (pr.big_lo, ALU.subtract, pr.big_hi)):
                        if op is not None:
                            pool.wait_ge(sem["stage_hi"], e + 1)
                        for rows, a, m, at in ((P, 0, 352, e * 352), (P, 352, 352, e * 352 + 2816), (P, 704, 256, e * 384 + 5632),
                                               (96, 960, 128, e * 384 + 5632 + 256)):
                            o = dst[0:rows, bass.ds(at, m)]
                            i0 = raw[0:rows, 0, a:a + m]
                            if op is None:
                                last = pool.tensor_copy(o, i0)
                            else:
                                last = pool.tensor_tensor(o, i0, in1[0:rows, bass.ds(at, m)].bitcast(F32), op)
                        last.then_inc(sem["stage_hi"] if op is None else sem["stage_split"], 1)

                def mask(b):
                    if masked:
                        pool.wait_ge(sem["mk_split"], b + 1)
                        pool.tensor_copy(msk_all[:, bass.ds(b, 1)], msk[:].bitcast(F32).unsqueeze(1)).then_inc(sem["mk_kept"], 1)

                def mask_in(b):
                    if masked:
                        need(pool, sem["mk_turned"], b)
                        pool.tensor_copy(mk[:], mask2[:, tiles(b, 2)].rearrange("p t h s -> p t (h s)")).then_inc(sem["mk_ready"], 1)

                def o_norm(b):
                    if gated:
                        pool.wait_ge(sem["o_moments"], b + 1)
                        pool.tensor_tensor(veb[:], mvb[:, :, 1], pr.eps[:, 0:2], ALU.add).then_inc(sem["o_var"], 1)
                        pool.wait_ge(sem["o_var"], b + 1)
                        pool.tensor_tensor(rstdb[:], veb[:], pr.neg_half[:, 0:2], ALU.pow).then_inc(sem["o_rstd"], 1)

                passes(pool, {"spread": spread, "turn": turn, "keys": keys, "mask": mask, "mask_in": mask_in, "o_norm": o_norm})

            @block.tensor
            def _(pe):
                if gated:
                    for i in range(4):
                        last = pe.transpose(b_sc[0][:, i * P:(i + 1) * P], w_raw[i], pr.id())
                    last.then_inc(sem["prep_pe"], 1)
                if biased:
                    pe.wait_ge(sem["prep_dve"], 3)
                    for i in range(2):
                        for g in range(NG):
                            last = pe.matmul(b_sc[1][:, i * NG + g:i * NG + g + 1], bias_x[0:1, i, g * P:(g + 1) * P], ones1[0:1, 0:1],
                                             start=True, stop=True)
                    last.then_inc(sem["prep_pe"], 1)
                pe.wait_ge(sem["prep_dve"], DVE_WEIGHTS)
                for g, bank in enumerate((b_st[0], b_st[1], b_mt, b_o)):
                    cols = slice(g * P, (g + 1) * P)
                    pe.matmul(bank[:], wx[:, 2, cols], pr.ctx_hi[:], start=True, stop=False)
                    pe.matmul(bank[:], wx[:, 2, cols], pr.ctx_lo[:], start=False, stop=False)
                    pe.matmul(bank[:], wx[:, 3, cols], pr.ctx_hi[:], start=False, stop=True).then_inc(sem["prep_pe"], 1)
                for h, bank in enumerate((b_proj, b_turn)):
                    if biased:
                        pe.matmul(bank[:], ones1[:], bias_row[0:1, 2:3, :].to_broadcast([1, 4, D]), start=True, stop=False, skip_group_check=True)
                    for e in range(4):
                        last = pe.matmul(bank[:, e * D:(e + 1) * D], pr.ctx_t2[:, 4 * h + e].rearrange("p a s -> p (a s)"), w[2],
                                         start=not biased, stop=True, skip_group_check=True)
                    last.then_inc(sem["prep_pe"], 1)
                if gated:
                    for h in range(2):
                        pe.wait_ge(sem["prep_dve"], DVE_READY)
                        for e in range(4):
                            last = pe.matmul(b_sc[h][:, e * D:(e + 1) * D], pr.ctx_t2[:, 4 * h + e, 0, 0:1].to_broadcast([P, P]), wvg[:],
                                             start=True, stop=True, skip_group_check=True)
                        last.then_inc(sem["prep_pe"], 1)
                pe.wait_ge(sem["prep_dve"], DVE_READY)
                pe.wait_ge(sem["prep_act"], ACT_READY)
                pe.wait_ge(sem["prep_pool"], POOL_READY)

                def turn(b):
                    pe.wait_ge(sem["xn_ready"], b + 1)
                    if own_keys:
                        need(pe, sem["v_ready"], b)
                    need(pe, sem["x_done"], b - 2)
                    need(pe, sem["xt_lo"], b)
                    for t in range(2):
                        last = pe.transpose(b_turn[:, t * P:(t + 1) * P], xn[:, t], pr.id())
                    last.then_inc(sem["xn_turned"], 1)

                def mask(b):
                    if masked:
                        pe.wait_ge(sem["mk_ready"], b + 1)
                        need(pe, sem["m_split"], b * NG - 1)
                        for t in range(2):
                            last = pe.transpose(b_mt[:, t * P:(t + 1) * P], mk[:, t], pr.id())
                        last.then_inc(sem["mk_turned"], 1)

                def proj(b, g):
                    pe.wait_ge(sem["xt_lo"], b + 1)
                    need(pe, sem["qk_split"], b * NG + g)
                    cols = slice(g * P, (g + 1) * P)
                    for i in range(2 if own_keys else 1):
                        o = b_proj[:, i * S:(i + 1) * S]
                        pe.matmul(o, wx[:, 2 * i, cols], xt_hi[:], start=True, stop=False)
                        pe.matmul(o, wx[:, 2 * i, cols], xt_lo[:], start=False, stop=False)
                        last = pe.matmul(o, wx[:, 2 * i + 1, cols], xt_hi[:], start=False, stop=True)
                    last.then_inc(sem["proj_done"], 1)

                def scores(b, g, i):
                    at = g * NS
                    need(pe, sem["sc_taken"], b * U + (at + i - 1))
                    o = b_sc[(at + i) % 2]
                    if i == 0:
                        pe.wait_ge(sem["qk_split"], b * NG + g + 1)
                        pe.wait_ge(sem["kc_ready"], b * NG + g + 1)
                        if masked:
                            pe.wait_ge(sem["mk_split"], b + 1)
                        for t in range(2):
                            ts = slice(t * P, (t + 1) * P)
                            last = pe.matmul(o[:, t * S:(t + 1) * S], q[:, g, ts], kc[:, g], start=True, stop=not masked)
                            if masked:
                                last = pe.matmul(o[:, t * S:(t + 1) * S], msk[:, ts], i2[:, 0:S2].unsqueeze(1).to_broadcast([P, GH, S2]),
                                                 start=False, stop=True)
                    else:
                        rows = slice(32 * (i - 1), 32 * i)
                        for t in range(2):
                            last = pe.matmul(o[:, t * S:(t + 1) * S], q[rows, g, t * P:(t + 1) * P], k[rows, g], start=True, stop=True)
                    last.then_inc(sem["sc_done"], 1)

                def maxima(b, g):
                    pe.wait_ge(sem["m_ready"], b * NG + g + 1)
                    need(pe, sem["m_split"], b * NG + g)
                    if masked:
                        if g < NG - 1:
                            pe.wait_ge(sem["mk_split"], b + 1)
                        elif not (isinstance(b, int) and b == B - 1):
                            pe.wait_ge(sem["mk_split"], b + 2)
                    for t in range(2):
                        last = pe.transpose(b_mt[:, t * P:(t + 1) * P], mx[:, g % 2, t].rearrange("p j c -> p (j c)"), pr.id())
                    last.then_inc(sem["m_turned"], 1)

                def weights(b, g, i):
                    at = g * NS
                    need(pe, sem["exp_done"], b * U + (at + i - 1))
                    o = b_st[(at + i) % 2]
                    if i == 0:
                        pe.wait_ge(sem["m_split"], b * NG + g + 1)
                        if masked:
                            pe.wait_ge(sem["mk_kept"], b + 1)
                        for pair in range(2):
                            op = o[:, pair * S:(pair + 1) * S]
                            keys_of = kc[:, g, 2 * pair:2 * pair + 2].rearrange("p j s -> p (j s)")
                            if gated:
                                last = pe.matmul(op, keys_of, mt[:, g % 2], start=True, stop=True)
                                continue
                            pe.matmul(op, keys_of, q[:, g], start=True, stop=False)
                            if masked:
                                pe.matmul(op, i2[:], msk_all[:, bass.ds(b, 1)].rearrange("p a s -> p (a s)"), start=False, stop=False)
                            last = pe.matmul(op, selc[:, pair], mt[:, g % 2], start=False, stop=True)
                    else:
                        rows = slice(32 * (i - 1), 32 * i)
                        for kt in range(2):
                            op = o[:, kt * S:(kt + 1) * S]
                            last = pe.matmul(op, k[rows, g, kt * P:(kt + 1) * P], mt[rows, g % 2], start=True, stop=True)
                    last.then_inc(sem["st_done"], 1)

                def values(b):
                    if own_keys:
                        need(pe, sem["x_done"], b - 1)
                        pe.wait_ge(sem["xt_lo"], b + 1)
                        for kt in range(2):
                            last = pe.matmul(b_turn[:, kt * P:(kt + 1) * P], xt_raw[:, kt * P:(kt + 1) * P], w[2], start=True, stop=True)
                        last.then_inc(sem["v_proj"], 1)

                def pv(b, o, i):
                    pe.wait_ge(sem["exp_done"], b * U + ((2 * o + 1) * NS + (1, 4, 4, 5, 5)[i]))
                    if i == 0:
                        pe.wait_ge(sem["vc_ready"], b + 1)
                        if own_keys:
                            pe.wait_ge(sem["v_spread"], b + 1)
                        need(pe, sem["ot_taken"], b * 2 + o)
                    for quad in range(4):
                        g, pair = divmod(quad, 2)
                        out = b_o[32 * quad:32 * quad + 32, 0:S]
                        if i == 0:
                            lhs, rhs = vc[:, 4 * o + quad], pt[:, o, g * NS, pair * S:(pair + 1) * S]
                        else:
                            s, kt = divmod(i - 1, 2)
                            lhs = vs[:, kt, 8 * o + 2 * quad + s]
                            rhs = pt[:, o, g * NS + 1 + 2 * pair + s, kt * S:(kt + 1) * S]
                        last = pe.matmul(out, lhs, rhs, start=(i == 0), stop=(i == NS - 1))
                    if i == NS - 1:
                        last.then_inc(sem["pv_done"], 1)

                def o_turn(b):
                    pe.wait_ge(sem["ot_taken"], b * 2 + 2)
                    if isinstance(b, int) and b == B - 1:
                        pe.wait_ge(sem["x_done"], B - 1)
                    elif isinstance(b, int) and b == B - 2:
                        pe.wait_ge(sem["x_done"], B - 2)
                        pe.wait_ge(sem["xt_lo"], B)
                        if own_keys:
                            pe.wait_ge(sem["v_ready"], B)
                    else:
                        pe.wait_ge(sem["xt_lo"], b + 3)
                    for t in range(2):
                        for o in range(2):
                            last = pe.transpose(b_turn[:, (2 * t + o) * P:(2 * t + o + 1) * P], ot[:, o, t * P:(t + 1) * P], pr.id())
                    last.then_inc(sem["o_turned"], 1)

                def on_turn(b):
                    pe.wait_ge(on_ready, b + 1)
                    for t in range(2):
                        last = pe.transpose(b_turn[:, t * P:(t + 1) * P], on[:, t], pr.id())
                    last.then_inc(sem["on_turned"], 1)

                def y(b):
                    pe.wait_ge(sem["o2t_ready"], b + 1)
                    for t in range(2):
                        last = pe.matmul(b_turn[:, t * P:(t + 1) * P], o2t[:, t * P:(t + 1) * P], w[3], start=True, stop=True)
                    last.then_inc(sem["y_done"], 1)

                passes(pe, {"turn": turn, "mask": mask, "proj": proj, "scores": scores, "maxima": maxima, "weights": weights,
                            "values": values, "pv": pv, "o_turn": o_turn, "on_turn": on_turn, "y": y})

            @block.scalar
            def _(act):
                if gated:
                    act.wait_ge(sem["prep_pe"], 1)
                    act.copy(wf[:], b_sc[0][:].rearrange("p (i n) -> p i n", i=4)).then_inc(sem["prep_act"], 1)
                    act.wait_ge(sem["loaded"], LOADED)
                    act.activation(gate_row[:], gate_row[:], ACT.Tanh).then_inc(sem["prep_act"], 1)
                pe_at = 1 if gated or biased else 0
                n_act = 2 if gated else 0
                for g, bank in enumerate((b_st[0], b_st[1], b_mt, b_o)):
                    act.wait_ge(sem["prep_pe"], pe_at + g + 1)
                    act.wait_ge(sem["prep_dve"], DVE_WEIGHTS + g)
                    act.activation(hk.bitcast(F32R), bank[:], ACT.Identity, bias=bias_ca[:, 1, g:g + 1], scale=pr.c("ak")).then_inc(sem["prep_act"], 1)
                for h, bank in enumerate((b_proj, b_turn)):
                    act.wait_ge(sem["prep_pe"], pe_at + 5 + h)
                    act.copy(vc_all[:, 4 * h:4 * h + 4].rearrange("p e d -> p (e d)"), bank[:]).then_inc(sem["prep_act"], 1)
                if gated:
                    for h in range(2):
                        act.wait_ge(sem["prep_pe"], pe_at + 7 + h)
                        act.copy(vg_all[:, 4 * h:4 * h + 4].rearrange("p e d -> p (e d)"), b_sc[h][:]).then_inc(sem["prep_act"], 1)

                def turn(b):
                    act.wait_ge(sem["xn_turned"], b + 1)
                    need(act, sem["proj_done"], b * NG)
                    if own_keys:
                        need(act, sem["v_proj"], b)
                        act.copy(xt_raw[:], b_turn[:, 0:S])
                    act.copy(xt_hi[:], b_turn[:, 0:S]).then_inc(sem["xt_hi"], 1)

                def mask(b):
                    if masked:
                        act.wait_ge(sem["mk_turned"], b + 1)
                        need(act, sem["mk_split"], b)
                        act.activation(hmk[:].bitcast(F32R), b_mt[:, 0:S], ACT.Copy, scale=mask_a[:]).then_inc(sem["mk_hi"], 1)

                def proj(b, g):
                    act.wait_ge(sem["proj_done"], b * NG + g + 1)
                    need(act, sem["qk_split"], b * NG + g)
                    for i in range(2 if own_keys else 1):
                        last = act.activation(part[:, i].bitcast(F32R), b_proj[:, i * S:(i + 1) * S], ACT.Identity,
                                              bias=bias_ca[:, i, g:g + 1], scale=pr.c("ak" if i else "aq"))
                    last.then_inc(sem["proj_hi"], 1)

                def maxima(b, g):
                    act.wait_ge(sem["m_turned"], b * NG + g + 1)
                    need(act, sem["m_split"], b * NG + g)
                    act.activation(hm[:].bitcast(F32R), b_mt[:, 0:S], ACT.Copy, scale=pr.c("am1" if gated else "am")).then_inc(sem["m_hi"], 1)

                def weights(b, g, i):
                    if i == 0:
                        need(act, sem["pv_done"], b * 2 + (g // 2 - 1))
                    act.wait_ge(sem["st_done"], b * U + (g * NS + i + 1))
                    act.activation(pt[:, g // 2, (g % 2) * NS + i], b_st[(g * NS + i) % 2][:], ACT.Exp, scale=scale).then_inc(sem["exp_done"], 1)

                def values(b):
                    if own_keys:
                        act.wait_ge(sem["v_proj"], b + 1)
                        need(act, sem["v_spread"], b)
                        last = act.copy(v_own[:].rearrange("p k d -> p (k d)"), b_turn[:, 0:S])
                        last.then_inc(sem["v_ready"], 1)

                def pv(b, o, i):
                    if i < NS - 1:
                        return
                    act.wait_ge(sem["pv_done"], b * 2 + o + 1)
                    need(act, sem["o_turned"], b)
                    act.copy(ot[:, o], b_o[:, 0:S]).then_inc(sem["ot_taken"], 1)

                def on_turn(b):
                    act.wait_ge(sem["on_turned"], b + 1)
                    need(act, sem["y_done"], b)
                    if gated:
                        act.activation(o2t[:], b_turn[:, 0:S], ACT.Identity, bias=ln_gb[:, 1:2], scale=ln_gb[:, 0:1]).then_inc(sem["o2t_ready"], 1)
                    else:
                        act.copy(o2t[:], b_turn[:, 0:S]).then_inc(sem["o2t_ready"], 1)

                passes(act, {"turn": turn, "mask": mask, "proj": proj, "maxima": maxima, "weights": weights, "values": values,
                             "pv": pv, "on_turn": on_turn})

            @block.vector
            def _(dve):
                count = [0]

                def prep(ins_, wait=True):
                    count[0] += 1
                    ins_.then_inc(sem["prep_dve"], 1)
                    if wait:
                        dve.wait_ge(sem["prep_dve"], count[0])
                for tile in range(NT):
                    last = dve.bn_aggr(mv[:, tile], pr.st6[:, tile])
                last.then_inc(sem["moments"], 1)
                prep(dve.memset(ones1[:], 1.0))
                if biased:
                    dve.wait_ge(sem["loaded"], LOADED)
                    prep(dve.tensor_copy(bias_x[:].rearrange("a i (h t d) -> a i h t d", t=4, d=HD)[:, 0],
                                         bias_row[0:1, 0, :].rearrange("a (h d) -> a h d", d=HD).unsqueeze(2).to_broadcast([1, H, 4, HD])))
                    dve.tensor_copy(bias_x[:].rearrange("a i (h t d) -> a i h t d", t=4, d=HD)[:, 1],
                                    bias_row[0:1, 1, :].rearrange("a (h d) -> a h d", d=HD).unsqueeze(2).to_broadcast([1, H, 4, HD])).then_inc(sem["prep_dve"], 1)
                    count[0] += 1
                if gated:
                    prep(dve.memset(wx[:].rearrange("p w (h t d) -> p (w h) t d", t=4, d=HD)[:, :, 3].bitcast(F32), 0.0))
                    dve.wait_ge(sem["prep_act"], 1)
                for i in range(2):
                    src = w[i].rearrange("p (h d) -> p h d", d=HD).unsqueeze(2).to_broadcast([P, H, 4, HD])
                    hi, lo = (wx[:, 2 * i + e].rearrange("p (h t d) -> p h t d", t=4, d=HD) for e in range(2))
                    if gated:
                        src, hi, lo = src[:, :, 0:3], hi[:, :, 0:3], lo[:, :, 0:3]
                    prep(dve.tensor_copy(hi, src))
                    prep(dve.tensor_tensor(lo, src, hi.bitcast(F32), ALU.subtract))
                if biased:
                    dve.wait_ge(sem["prep_pe"], 1)
                    prep(dve.tensor_copy(bias_c[:].rearrange("p i g -> p (i g)"), b_sc[1][:, 0:2 * NG]))
                    prep(dve.tensor_scalar(bias_ca[:, 0], bias_c[:, 0], pr.c("aq"), None, ALU.mult))
                    prep(dve.tensor_scalar(bias_ca[:, 1], bias_c[:, 1], pr.c("ak"), None, ALU.mult))
                else:
                    prep(dve.memset(bias_c[:], 0.0))
                    prep(dve.tensor_copy(bias_c[:, 1], pr.c("neg1").to_broadcast([P, NG])))
                    prep(dve.memset(bias_ca[:], 0.0))
                assert count[0] == DVE_WEIGHTS, count
                n_act = 2 if gated else 0
                for g, bank in enumerate((b_st[0], b_st[1], b_mt, b_o)):
                    dve.wait_ge(sem["prep_act"], n_act + g + 1)
                    prep(dve.scalar_tensor_tensor(kc_all[:, g].rearrange("p b s -> p (b s)"), bank[:], bias_c[:, 1, g:g + 1], hk, ALU.add, ALU.add))
                if gated:
                    dve.wait_ge(sem["prep_act"], n_act + 6)
                    prep(dve.memset(kc_all[:].rearrange("p g b s -> p (g b) s")[:, :, 0:1].bitcast(F32), 0.0))
                    prep(dve.tensor_tensor(wvg[:].rearrange("p (h d) -> p h d", d=HD), w[2].rearrange("p (h d) -> p h d", d=HD),
                                           gate_row[:].unsqueeze(2).to_broadcast([P, H, HD]), ALU.mult))
                else:
                    prep(dve.tensor_copy(selc[:].rearrange("p a n -> p (a n)"), pr.c("selc")))
                if masked:
                    dve.wait_ge(sem["loaded"], LOADED)
                    prep(dve.tensor_copy(i2[:], pr.c("i2")))
                    prep(dve.tensor_scalar(mask_a[:], pr.c("amask"), MASK_SCALE, None, ALU.mult))
                assert count[0] == DVE_READY, count
                dve.wait_ge(sem["rstd"], 1)

                def scale_x(b):
                    need(dve, sem["xn_turned"], b)
                    for t in range(2):
                        tile = bass.ds(b * 2 + t, 1)
                        last = dve.tensor_scalar(xn[:, t:t + 1], pr.x[:, tile], mv[:, tile, 0], rstd[:, tile], ALU.subtract, ALU.mult)
                    last.then_inc(sem["xn_ready"], 1)

                def turn(b):
                    dve.wait_ge(sem["xt_hi"], b + 1)
                    need(dve, sem["proj_done"], b * NG)
                    dve.tensor_tensor(xt_lo[:], b_turn[:, 0:S], xt_hi[:].bitcast(F32), ALU.subtract).then_inc(sem["xt_lo"], 1)

                def mask(b):
                    if masked:
                        dve.wait_ge(sem["mk_hi"], b + 1)
                        need(dve, sem["sc_done"], b * U)
                        need(dve, sem["mk_kept"], b)
                        dve.scalar_tensor_tensor(msk[:], b_mt[:, 0:S], MASK_SCALE, hmk[:], ALU.mult, ALU.add).then_inc(sem["mk_split"], 1)

                def proj(b, g):
                    dve.wait_ge(sem["proj_hi"], b * NG + g + 1)
                    need(dve, sem["st_done"], b * U + (g + 1) * NS - U)
                    for i in range(2 if own_keys else 1):
                        last = dve.scalar_tensor_tensor((k if i else q)[:, g], b_proj[:, i * S:(i + 1) * S], bias_c[:, i, g:g + 1],
                                                        part[:, i], ALU.add, ALU.add)
                    last.then_inc(sem["qk_split"], 1)

                def scores(b, g, i):
                    start = 1 if gated else 0
                    at = g * NS
                    dve.wait_ge(sem["sc_done"], b * U + (at + i + 1))
                    bank = b_sc[(at + i) % 2][:]
                    if i == 0:
                        need(dve, sem["m_ready"], b * NG + g)
                        by_head = bank.rearrange("p (t j s) -> p (t j) s", t=2, s=S2)
                        dve.tensor_reduce(mc[:].rearrange("p t j -> p (t j)"), by_head[:, :, start:], AX_X, ALU.max).then_inc(sem["sc_taken"], 1)
                    else:
                        dve.tensor_reduce(ms[:, :, i - 1], bank.rearrange("p (t s) -> p t s", s=S), AX_X, ALU.max).then_inc(sem["sc_taken"], 1)
                    if i < NS - 1:
                        return
                    dve.wait_ge(sem["sc_taken"], b * U + (at + NS))
                    need(dve, sem["m_turned"], b * NG + (g - 1))
                    at_row = 24 if gated else 0
                    dst = mx[:, g % 2].rearrange("p t j c -> p (t j) c")[:, :, at_row:at_row + 2]
                    mcb = mc[:].rearrange("p t j -> p (t j)").unsqueeze(2).to_broadcast([P, 2 * GH, 2])
                    if own_keys:
                        msb = ms[:].rearrange("p t j -> p (t j)").unsqueeze(2).to_broadcast([P, 2 * GH, 2])
                        dve.tensor_tensor(dst, mcb, msb, ALU.max).then_inc(sem["m_ready"], 1)
                    else:
                        dve.tensor_copy(dst, mcb).then_inc(sem["m_ready"], 1)

                def maxima(b, g):
                    dve.wait_ge(sem["m_hi"], b * NG + g + 1)
                    need(dve, sem["st_done"], b * U + (g - 1) * NS)
                    if gated:
                        need(dve, sem["m_split"], b * NG + g)
                        dve.wait_ge(sem["qk_split"], b * NG + (g + 1))
                        dve.tensor_tensor(hq[:], hm[:], q[:, g].bitcast(F32), ALU.add).then_inc(sem["hq_ready"], 1)
                        dve.wait_ge(sem["hq_ready"], b * NG + (g + 1))
                    dve.tensor_tensor(mt[:, g % 2], b_mt[:, 0:S], hq[:] if gated else hm[:], ALU.add).then_inc(sem["m_split"], 1)

                def o_norm(b):
                    dve.wait_ge(sem["o_turned"], b + 1)
                    by_head = b_turn[:].rearrange("p (h c) -> p h c", c=16)
                    dve.reciprocal(rc[:], by_head[:, :, 8]).then_inc(sem["rc_ready"], 1)
                    dve.wait_ge(sem["rc_ready"], b + 1)
                    need(dve, sem["on_turned"], b)
                    last = dve.tensor_tensor(on[:].rearrange("p t (h d) -> p (t h) d", d=HD), by_head[:, :, 0:HD],
                                             rc[:].unsqueeze(2).to_broadcast([P, 2 * H, HD]), ALU.mult)
                    last.then_inc(sem["o_norm"], 1)
                    if gated:
                        dve.wait_ge(sem["o_norm"], b + 1)
                        dve.tensor_tensor(o16[:], on[:], vg_all[:, bass.ds(b, 1)].to_broadcast([P, 2, D]), ALU.add).then_inc(sem["o_round"], 1)
                        dve.wait_ge(sem["o_round"], b + 1)
                        for t in range(2):
                            dve.bn_stats(st6b[:, t], o16[:, t]).then_inc(sem["o_stats"], 1)
                        need(dve, sem["o_rstd"], b)
                        dve.wait_ge(sem["o_stats"], b * 2 + 2)
                        settled(dve, sem)
                        for t in range(2):
                            last = dve.bn_aggr(mvb[:, t], st6b[:, t])
                        last.then_inc(sem["o_moments"], 1)

                def o_scale(b):
                    if gated:
                        dve.wait_ge(sem["o_rstd"], b + 1)
                        for t in range(2):
                            last = dve.tensor_scalar(on[:, t], o16[:, t], mvb[:, t, 0:1], rstdb[:, t:t + 1], ALU.subtract, ALU.mult)
                        last.then_inc(sem["on_ready"], 1)

                def y(b):
                    dve.wait_ge(sem["y_done"], b + 1)
                    dve.wait_ge(sem["x_bias"], b + 1)
                    xb = pr.x[:, tiles(b, 2)]
                    dve.scalar_tensor_tensor(xb, b_turn[:, 0:S].rearrange("p (t d) -> p t d", t=2), tg, xb, ALU.mult, ALU.add).then_inc(sem["x_done"], 1)

                passes(dve, {"scale": scale_x, "turn": turn, "mask": mask, "proj": proj, "scores": scores, "maxima": maxima,
                             "o_norm": o_norm, "o_scale": o_scale, "y": y})



def attention3(pr):
    nc, ins = pr.nc, pr.ins
    scale = HD3 ** -0.5
    NC = 4
    with nc.cleanup_on_exit(), ExitStack() as scope:
        def sb(name, shape, dt=F32):
            return scope.enter_context(nc.sbuf_tensor(f"L3_{name}", shape, dt))

        wq = sb("wq", [P, 512])
        wk = sb("wk", [P, 512])
        wv = sb("wv", [P, 512])
        wo = sb("wo", [P, NC, D])
        wq_hi = sb("wq_hi", [P, 512], F32R)
        wq_lo = sb("wq_lo", [P, 512], F32R)
        bo = sb("bo", [P, D])
        kt_all = sb("kt_all", [P, NC, B, S2])
        v_all = sb("v_all", [P, B, 512])
        kb = sb("kb", [P, NC, 2, S2])
        vb = sb("vb", [P, NC, 2, HD3])
        sel3 = sb("sel3", [P, NC, P], F32R)
        raw3 = sb("raw3", [P, 1920])
        mv = sb("mv", [P, NT, 2])
        ve = sb("ve", [P, NT])
        rstd = sb("rstd", [P, NT])
        xn = sb("xn", [P, 2, D])
        xt_hi = sb("xt_hi", [P, S], F32R)
        xt_lo = sb("xt_lo", [P, S], F32R)
        q = sb("q", [P, NC, S])
        mc = sb("mc", [P, 2, H3])
        mx = sb("mx", [P, 2, H3, 16])
        hm = sb("hm", [P, S])
        mt = sb("mt", [P, S], F32R)
        pt = sb("pt", [P, NC, S])
        rs = sb("rs", [P, S])
        hr = sb("hr", [P, S])
        rb = sb("rb", [P, 2, 512])
        rt = sb("rt", [P, S], F32R)
        self_ = sb("self", [P, NC, P], F32R)
        on = sb("on", [P, NC, S])
        sem = pr.sems("loaded", "w3_in", "prep_pe", "prep_act", "prep_dve", "settled", "prep_pool", "stats", "moments", "var_eps", "rstd",
                     "xn_ready", "xn_turned", "xt_hi", "xt_lo", "q_done", "q_taken", "kb_ready", "sc_done", "sc_taken", "m_ready",
                     "m_turned", "m_hi", "hq_ready", "m_split", "st_done", "exp_done", "sum_done", "r_ready", "r_hi", "r_split", "r_cast", "r_copied", "o_done", "o_taken", "y_done",
                     "x_bias", "x_done", "w3_hi", "vb_ready")
        b_q, b_turn, b_sc, b_sum, b_st, b_o = (pr.bank[0], pr.bank[1], (pr.bank[2], pr.bank[6]), pr.bank[3], pr.bank[4:6], (pr.bank[7], pr.bank[3]))
        b_mt = b_sc[0]
        tg = pr.gates[:, 3:4]

        first = [("scale", 0), ("turn", 0), ("proj", 0, 0), ("keys", 0, 0), ("proj", 0, 1), ("keys", 0, 1), ("scores", 0, 0), ("scores", 0, 1),
                 ("maxima", 0)]

        def order(b):
            more = not (isinstance(b, int) and b == B - 1)
            late = not (isinstance(b, int) and b == 0)
            steps = [("values", b)]
            if more:
                steps += [("scale", b + 1)]
            steps += [("weights", b, 0), ("weights", b, 1)]
            if more:
                steps += [("turn", b + 1)]
            steps += [("pv", b, 0), ("sums", b)]
            if more:
                steps += [("proj", b + 1, 0), ("keys", b + 1, 0)]
            if late:
                steps += [("y", b - 1)]
            if more:
                steps += [("proj", b + 1, 1), ("keys", b + 1, 1)]
            steps += [("parts", b)]
            if more:
                steps += [("scores", b + 1, 0), ("scores", b + 1, 1)]
            steps += [("pv", b, 1)]
            if more:
                steps += [("maxima", b + 1)]
            return steps + [("divide", b, 0), ("divide", b, 1)]

        def passes(eng, does):
            def run(steps):
                for step, *at in steps:
                    if step in does:
                        does[step](*at)
            run(first)
            run(order(0))
            run(order(1))
            with eng.Fori(2, B - 1) as b:
                run(order(b))
            run(order(B - 1))
            run([("y", B - 1)])

        with nc.Block() as block:
            @block.sync
            def _(sp):
                for dst, src in ((wq[:], ins["L3_xattn_Wq"]), (wk[:], ins["L3_xattn_Wk"]), (wv[:], ins["L3_xattn_Wv"]),
                                 (wo[:], ins["L3_xattn_Wo"].rearrange("(c p) n -> p c n", p=P)),
                                 (bo[:], ins["L3_xattn_bo"].partition_broadcast(P))):
                    sp.dma_start(dst, src).then_inc(sem["loaded"], 16)
                for a, name in ((0, "L3_ffn_w_gate"), (512, "L3_ffn_w_up")):
                    sp.dma_start(raw3[:, a:a + 512].rearrange("p (e i) -> p e i", e=E3), ins[name].rearrange("e p i -> p e i")).then_inc(sem["w3_in"], 16)
                sp.dma_start(raw3[:, 1024:1536].rearrange("p (c v) -> p c v", c=4), ins["L3_ffn_w_down"].rearrange("(c e) i v -> (e i) c v", e=2)).then_inc(sem["w3_in"], 16)
                for a, name in ((1536, "L3_ffn_sw_gate"), (1664, "L3_ffn_sw_up"), (1792, "L3_ffn_sw_down")):
                    sp.dma_start(raw3[:, a:a + P], ins[name]).then_inc(sem["w3_in"], 16)

            @block.gpsimd
            def _(pool):
                pool.wait_ge(sem["moments"], 1)
                pool.tensor_tensor(ve[:], mv[:, :, 1], pr.eps[:], ALU.add).then_inc(sem["var_eps"], 1)
                pool.wait_ge(sem["var_eps"], 1)
                pool.tensor_tensor(rstd[:], ve[:], pr.neg_half[:], ALU.pow).then_inc(sem["rstd"], 1)
                pool.memset(kb[:], 0.0).then_inc(sem["prep_pool"], 1)
                pool.memset(vb[:], 0.0).then_inc(sem["prep_pool"], 1)
                pool.memset(mx[:], 0.0).then_inc(sem["prep_pool"], 1)
                pool.wait_ge(sem["loaded"], 80)
                pool.tensor_scalar(bo[:], bo[:], tg, None, ALU.mult).then_inc(sem["prep_pool"], 1)
                pool.wait_ge(sem["prep_pool"], 4)
                pool.wait_ge(sem["prep_act"], 12)

                def turn(b):
                    pool.wait_ge(sem["xn_ready"], b + 1)
                    xb = pr.x[:, tiles(b, 2)]
                    pool.tensor_tensor(xb, xb, bo[:].unsqueeze(1).to_broadcast([P, 2, D]), ALU.add).then_inc(sem["x_bias"], 1)

                def keys(b, h):
                    need(pool, sem["st_done"], b * 2 + (h - 1))
                    pairs = slice(2 * h, 2 * h + 2)
                    for s in range(2):
                        last = pool.tensor_tensor(kb[:, pairs, s], kt_all[:, pairs, bass.ds(b, 1)].rearrange("p c e s -> p (c e) s"),
                                                  pr.c("half")[:, s:s + 1].unsqueeze(2).to_broadcast([P, 2, S2]), ALU.mult)
                    last.then_inc(sem["kb_ready"], 1)

                def split(b):
                    if isinstance(b, int) and b == 0:
                        pool.wait_ge(sem["w3_in"], 96)
                        pool.tensor_copy(pr.big_hi[:, 1152:1152 + 1920], raw3[:]).then_inc(sem["w3_hi"], 1)
                        pool.wait_ge(sem["w3_hi"], 1)
                        pool.tensor_tensor(pr.big_lo[:, 1152:1152 + 1920], raw3[:], pr.big_hi[:, 1152:1152 + 1920].bitcast(F32), ALU.subtract)

                def values(b):
                    need(pool, sem["o_done"], b * 2)
                    src = v_all[:, bass.ds(b, 1)].rearrange("p e (c s d) -> p (e c) s d", c=NC, s=2)
                    for s in range(2):
                        last = pool.tensor_tensor(vb[:, :, s], src[:, :, s],
                                                  pr.c("half")[:, s:s + 1].unsqueeze(2).to_broadcast([P, NC, HD3]), ALU.mult)
                    last.then_inc(sem["vb_ready"], 1)
                    split(b)

                passes(pool, {"turn": turn, "keys": keys, "values": values})

            @block.tensor
            def _(pe):
                pe.wait_ge(sem["loaded"], 80)
                for c in range(NC):
                    pe.matmul(pr.bank[c][:], wk[:, c * P:(c + 1) * P], pr.ctx_t2[:, :, 0], start=True, stop=True).then_inc(sem["prep_pe"], 1)
                for e in range(B):
                    bank = pr.bank[(NC + e) % 8]
                    if e >= 4:
                        pe.wait_ge(sem["prep_act"], e - 4 + 1)
                    pe.matmul(bank[:], pr.ctx_t2[:, e].rearrange("p a s -> p (a s)"), wv[:], start=True, stop=True).then_inc(sem["prep_pe"], 1)
                pe.wait_ge(sem["prep_act"], 12)
                pe.wait_ge(sem["prep_dve"], 4)
                pe.wait_ge(sem["prep_pool"], 4)

                def turn(b):
                    pe.wait_ge(sem["xn_ready"], b + 1)
                    need(pe, sem["xt_lo"], b)
                    need(pe, sem["x_done"], b - 2)
                    for t in range(2):
                        last = pe.transpose(b_turn[:, t * P:(t + 1) * P], xn[:, t], pr.id())
                    last.then_inc(sem["xn_turned"], 1)

                def proj(b, h):
                    pe.wait_ge(sem["xt_lo"], b + 1)
                    need(pe, sem["q_taken"], b * 2 + h)
                    for e in range(2):
                        cols = slice((2 * h + e) * P, (2 * h + e + 1) * P)
                        o = b_q[:, e * S:(e + 1) * S]
                        pe.matmul(o, wq_hi[:, cols], xt_hi[:], start=True, stop=False)
                        pe.matmul(o, wq_hi[:, cols], xt_lo[:], start=False, stop=False)
                        last = pe.matmul(o, wq_lo[:, cols], xt_hi[:], start=False, stop=True)
                    last.then_inc(sem["q_done"], 1)

                def scores(b, t):
                    pe.wait_ge(sem["q_taken"], b * 2 + 2)
                    pe.wait_ge(sem["kb_ready"], b * 2 + 2)
                    if t == 0:
                        need(pe, sem["m_split"], b)
                    else:
                        need(pe, sem["sc_taken"], b * 2)
                    for c in range(NC):
                        last = pe.matmul(b_sc[t][:, c * P:(c + 1) * P], q[:, c, t * P:(t + 1) * P], kb[:, c].rearrange("p h s -> p (h s)"),
                                         start=True, stop=True)
                    last.then_inc(sem["sc_done"], 1)

                def maxima(b):
                    pe.wait_ge(sem["m_ready"], b + 1)
                    for t in range(2):
                        last = pe.transpose(b_mt[:, t * P:(t + 1) * P], mx[:, t].rearrange("p j c -> p (j c)"), pr.id())
                    last.then_inc(sem["m_turned"], 1)

                def weights(b, h):
                    pe.wait_ge(sem["m_split"], b + 1)
                    need(pe, sem["r_copied"], b * 2 + (h - 1))
                    for e in range(2):
                        c = 2 * h + e
                        o = b_st[h][:, e * S:(e + 1) * S]
                        pe.matmul(o, kb[:, c].rearrange("p h s -> p (h s)"), q[:, c], start=True, stop=False)
                        last = pe.matmul(o, sel3[:, c], mt[:], start=False, stop=True)
                    last.then_inc(sem["st_done"], 1)

                def sums(b):
                    pe.wait_ge(sem["exp_done"], b * 2 + 2)
                    need(pe, sem["o_taken"], b * 2)
                    for c in range(NC):
                        last = pe.matmul(b_sum[:, 0:S], pr.c("sum3")[:, c * P:(c + 1) * P], pt[:, c], start=(c == 0), stop=(c == NC - 1))
                    last.then_inc(sem["sum_done"], 1)

                def pv(b, h):
                    if h == 0:
                        pe.wait_ge(sem["vb_ready"], b + 1)
                        pe.wait_ge(sem["exp_done"], b * 2 + 1)
                        need(pe, sem["o_taken"], b * 2 - 1)
                    else:
                        pe.wait_ge(sem["r_split"], b + 1)
                    for e in range(2):
                        last = pe.matmul(b_o[h][:, e * S:(e + 1) * S], vb[:, 2 * h + e].rearrange("p s d -> p (s d)"), pt[:, 2 * h + e],
                                         start=True, stop=True)
                    last.then_inc(sem["o_done"], 1)

                def divide(b, h):
                    pe.wait_ge(sem["r_split"], b + 1)
                    for e in range(2):
                        last = pe.matmul(b_st[h][:, e * S:(e + 1) * S], self_[:, 2 * h + e], rt[:], start=True, stop=True)
                    last.then_inc(sem["r_cast"], 1)

                def y(b):
                    pe.wait_ge(sem["o_taken"], b * 2 + 2)
                    if isinstance(b, int) and b == B - 1:
                        pe.wait_ge(sem["x_done"], B - 1)
                    elif isinstance(b, int) and b == B - 2:
                        pe.wait_ge(sem["xt_lo"], B)
                        pe.wait_ge(sem["x_done"], B - 2)
                    else:
                        pe.wait_ge(sem["xt_lo"], b + 3)
                    for t in range(2):
                        for c in range(NC):
                            last = pe.matmul(b_turn[:, t * P:(t + 1) * P], on[:, c, t * P:(t + 1) * P], wo[:, c], start=(c == 0), stop=(c == NC - 1))
                    last.then_inc(sem["y_done"], 1)

                passes(pe, {"turn": turn, "proj": proj, "scores": scores, "maxima": maxima, "weights": weights,
                            "sums": sums, "pv": pv, "divide": divide, "y": y})

            @block.scalar
            def _(act):
                for c in range(NC):
                    act.wait_ge(sem["prep_pe"], c + 1)
                    act.copy(kt_all[:, c].rearrange("p b s -> p (b s)"), pr.bank[c][:]).then_inc(sem["prep_act"], 1)
                for e in range(B):
                    act.wait_ge(sem["prep_pe"], NC + e + 1)
                    act.copy(v_all[:, e], pr.bank[(NC + e) % 8][:]).then_inc(sem["prep_act"], 1)

                def turn(b):
                    act.wait_ge(sem["xn_turned"], b + 1)
                    need(act, sem["q_done"], b * 2)
                    act.copy(xt_hi[:], b_turn[:, 0:S]).then_inc(sem["xt_hi"], 1)

                def proj(b, h):
                    need(act, sem["st_done"], b * 2 + (h - 1))
                    act.wait_ge(sem["q_done"], b * 2 + h + 1)
                    act.copy(q[:, 2 * h:2 * h + 2].rearrange("p c s -> p (c s)"), b_q[:]).then_inc(sem["q_taken"], 1)

                def maxima(b):
                    act.wait_ge(sem["m_turned"], b + 1)
                    need(act, sem["m_split"], b)
                    act.activation(hm[:].bitcast(F32R), b_mt[:, 0:S], ACT.Copy, scale=pr.c("a16")).then_inc(sem["m_hi"], 1)

                def weights(b, h):
                    need(act, sem["o_done"], b * 2 + (h - 1))
                    act.wait_ge(sem["st_done"], b * 2 + h + 1)
                    act.activation(pt[:, 2 * h:2 * h + 2].rearrange("p c s -> p (c s)"), b_st[h][:], ACT.Exp, scale=scale).then_inc(sem["exp_done"], 1)

                def parts(b):
                    act.wait_ge(sem["r_ready"], b + 1)
                    need(act, sem["r_split"], b)
                    act.activation(hr[:].bitcast(F32R), rs[:], ACT.Copy, scale=pr.c("a16")).then_inc(sem["r_hi"], 1)

                def divide(b, h):
                    act.wait_ge(sem["r_cast"], b * 2 + h + 1)
                    need(act, sem["o_taken"], b * 2 + (h - 1))
                    act.copy(rb[:, h], b_st[h][:]).then_inc(sem["r_copied"], 1)

                passes(act, {"turn": turn, "proj": proj, "maxima": maxima, "weights": weights, "parts": parts, "divide": divide})

            @block.vector
            def _(dve):
                for tile in range(NT):
                    last = dve.bn_aggr(mv[:, tile], pr.st6[:, tile])
                last.then_inc(sem["moments"], 1)
                dve.wait_ge(sem["loaded"], 80)
                dve.tensor_copy(wq_hi[:], wq[:]).then_inc(sem["prep_dve"], 1)
                dve.wait_ge(sem["prep_dve"], 1)
                dve.tensor_tensor(wq_lo[:], wq[:], wq_hi[:].bitcast(F32), ALU.subtract).then_inc(sem["prep_dve"], 1)
                dve.tensor_scalar(sel3[:].rearrange("p c n -> p (c n)"), pr.c("self3"), -1.0, None, ALU.mult).then_inc(sem["prep_dve"], 1)
                dve.tensor_copy(self_[:].rearrange("p c n -> p (c n)"), pr.c("self3")).then_inc(sem["prep_dve"], 1)
                dve.wait_ge(sem["prep_act"], 12)
                dve.wait_ge(sem["prep_pool"], 3)
                dve.wait_ge(sem["rstd"], 1)

                def scale_x(b):
                    need(dve, sem["xn_turned"], b)
                    for t in range(2):
                        tile = bass.ds(b * 2 + t, 1)
                        last = dve.tensor_scalar(xn[:, t:t + 1], pr.x[:, tile], mv[:, tile, 0], rstd[:, tile], ALU.subtract, ALU.mult)
                    last.then_inc(sem["xn_ready"], 1)

                def turn(b):
                    dve.wait_ge(sem["xt_hi"], b + 1)
                    need(dve, sem["q_done"], b * 2)
                    dve.tensor_tensor(xt_lo[:], b_turn[:, 0:S], xt_hi[:].bitcast(F32), ALU.subtract).then_inc(sem["xt_lo"], 1)

                def scores(b, t):
                    dve.wait_ge(sem["sc_done"], b * 2 + t + 1)
                    need(dve, sem["m_ready"], b)
                    dve.tensor_reduce(mc[:, t], b_sc[t][:].rearrange("p (h s) -> p h s", s=S2), AX_X, ALU.max).then_inc(sem["sc_taken"], 1)
                    if t == 0:
                        return
                    dve.wait_ge(sem["sc_taken"], b * 2 + 2)
                    need(dve, sem["m_turned"], b)
                    dve.tensor_copy(mx[:].rearrange("p t j c -> p (t j) c")[:, :, 0:2],
                                    mc[:].rearrange("p t j -> p (t j)").unsqueeze(2).to_broadcast([P, 2 * H3, 2])).then_inc(sem["m_ready"], 1)

                def maxima(b):
                    dve.wait_ge(sem["m_hi"], b + 1)
                    need(dve, sem["st_done"], b * 2)
                    dve.tensor_tensor(mt[:], b_mt[:, 0:S], hm[:], ALU.add).then_inc(sem["m_split"], 1)

                def sums(b):
                    dve.wait_ge(sem["sum_done"], b + 1)
                    need(dve, sem["r_split"], b)
                    dve.reciprocal(rs[:], b_sum[:, 0:S]).then_inc(sem["r_ready"], 1)

                def parts(b):
                    dve.wait_ge(sem["r_hi"], b + 1)
                    need(dve, sem["r_cast"], b * 2)
                    dve.tensor_tensor(rt[:], rs[:], hr[:], ALU.add).then_inc(sem["r_split"], 1)

                def divide(b, h):
                    half_on = on[:, 2 * h:2 * h + 2].rearrange("p c s -> p (c s)")
                    dve.wait_ge(sem["o_done"], b * 2 + h + 1)
                    dve.wait_ge(sem["r_copied"], b * 2 + h + 1)
                    need(dve, sem["y_done"], b)
                    dve.tensor_tensor(half_on, b_o[h][:], rb[:, h], ALU.mult).then_inc(sem["o_taken"], 1)

                def y(b):
                    dve.wait_ge(sem["y_done"], b + 1)
                    dve.wait_ge(sem["x_bias"], b + 1)
                    xb = pr.x[:, tiles(b, 2)]
                    dve.scalar_tensor_tensor(xb, b_turn[:, 0:S].rearrange("p (t d) -> p t d", t=2), tg, xb, ALU.mult, ALU.add).then_inc(sem["x_done"], 1)

                passes(dve, {"scale": scale_x, "turn": turn, "scores": scores, "maxima": maxima, "sums": sums, "parts": parts, "divide": divide, "y": y})



def ffn(pr, layer):
    nc, ins = pr.nc, pr.ins
    n = f"L{layer}f"
    C = {0: E0 * X0 // P, 1: E1 * 3, 2: HID2 // P, 3: E3 * X3 // P + 1}[layer]
    R = {0: 4, 1: 4, 2: 3, 3: 5}[layer]
    E = {0: E0, 1: E1, 2: 0, 3: E3}[layer]
    K = {0: K0, 1: K1, 2: 0, 3: K3}[layer]
    NS = 3 if layer == 2 else 2
    DUP = P // E if E else 0
    W = E + 8 - K
    T = TOK // P
    HAS_UP = layer != 0
    POOL_GATES = layer in (1, 3)
    SPLIT_LAG, DOWN_LAG = (2, 3) if POOL_GATES else (1, 2)
    GATED = {0: range(4), 1: range(24), 2: range(0), 3: range(4)}[layer]
    FUNC = {0: ACT.Relu, 1: ACT.Gelu, 2: ACT.Silu, 3: ACT.Silu}[layer]
    SENTINEL = LOWEST
    TAKEN = 3 * LOWEST

    def rows(c):
        return 96 if layer == 1 and c % 3 == 2 else P

    def weights_at(c):
        if layer == 0:
            return c * P, None, 512 + c * P
        if layer == 1:
            e, k = divmod(c, 3)
            return e * X1 + k * P, 2816 + e * X1 + k * P, 5632 + e * 384 + k * P
        if layer == 2:
            return c * P, 384 + c * P, 768 + c * P
        return (1152 + c * P, 1664 + c * P, 2176 + c * P) if c < 4 else (2688, 2816, 2944)

    def distance(c):
        last = [k for k in range(c) if k % NS == c % NS] or [k - C for k in range(C) if k % NS == c % NS]
        return c - max(last)

    def gate_slot(c):
        return (c // 3) % 2 if layer == 1 else c % 2

    def gate_distance(c):
        at = gate_slot(c)
        last = [k for k in GATED if k < c and gate_slot(k) == at] or [k - C for k in GATED if gate_slot(k) == at]
        return c - max(last)

    with nc.cleanup_on_exit(), ExitStack() as scope:
        def sb(name, shape, dt=F32):
            return scope.enter_context(nc.sbuf_tensor(f"{n}_{name}", shape, dt))

        mv = sb("mv", [P, NT, 2])
        ve = sb("ve", [P, NT])
        rstd = sb("rstd", [P, NT])
        xn = sb("xn", [P, T, D])
        xt_hi = sb("xt_hi", [P, NI, TOK], F32R)
        xt_lo = sb("xt_lo", [P, NI, TOK], F32R)
        a = sb("a", [P, R, TOK])
        h = sb("h", [P, R, TOK])
        h_hi = sb("h_hi", [P, R, TOK], F32R)
        h_lo = sb("h_lo", [P, R, TOK], F32R)
        yt = sb("yt", [P, TOK])
        if E:
            xt_raw = sb("xt_raw", [P, TOK])
            router = sb("router", [P, E])
            sel = sb("sel", [P, E if layer == 1 else 512], F32R)
            pe_ = sb("pe", [P, T, E])
            p1 = sb("p1", [P, T, E])
            cand = sb("cand", [P, T, W])
            top8 = sb("top8", [P, T, 8])
            want = sb("want", [P, T, 8])
            left = sb("left", [P, T, W])
            picked = sb("picked", [P, T, E])
            total = sb("total", [P, T])
            total2 = sb("total2", [P, T])
            total3 = sb("total3", [P, T])
            gx = sb("gx", [P, T, E, DUP])
            hg = sb("hg", [P, TOK])
            gts = sb("gts", [P, NI, TOK], F32R)
            extra = sb("extra", [P, E])
        if POOL_GATES:
            gb = sb("gb", [P, 2, TOK])
        if layer == 0:
            sel_rows = sb("sel_rows", [E0, D])
        if layer == 1:
            bias_col = sb("bias_col", [P, 1])
        if layer == 2:
            wi = sb("wi", [P, 9, P], I32)
            wf = sb("wf", [P, 9, P])
        if layer == 3:
            gs = sb("gs", [P, T, NG3 + 8 - 2])
            gtop = sb("gtop", [P, T, 8])
            gwant = sb("gwant", [P, T, 8])
            gleft = sb("gleft", [P, T, NG3 + 8 - 2])

        sem = pr.sems("loaded", "prep_pe", "prep_act", "prep_dve", "settled", "stats", "moments", "var_eps", "rstd", "xn_ready", "xn_turned",
                     "xt_raw", "xt_hi", "xt_lo", "logits_done", "logits_exp", "logits_less", "routed", "gates_turned", "gates_hi",
                     "gts_ready", "up_done", "gate_done", "act_done", "half_done", "h_done", "gate_copied", "hi_done", "lo_done", "down_done",
                     "yt_ready", "y_turned", "x_done")
        b_g = (pr.bank[0], pr.bank[1], pr.bank[4])
        b_u = (pr.bank[2], pr.bank[3], pr.bank[6])
        b_gate = (pr.bank[4], pr.bank[6])
        b_y, b_turn = pr.bank[5], pr.bank[7]
        tg = pr.gates[:, 4 + layer:5 + layer]
        hi, lo = pr.big_hi, pr.big_lo
        if not POOL_GATES:
            sem["half_done"] = sem["h_done"]
        N_GATES = {0: 4, 1: 8, 2: 0, 3: 4}[layer]
        NROUTE = {0: 20, 1: 20, 2: 0, 3: 30}[layer]
        PREP_DVE = {0: 5, 1: 4, 2: 6, 3: 6}[layer]
        PREP_ACT = {0: 0, 1: 0, 2: 3, 3: 0}[layer]
        LOADED = 16 * {0: 2, 1: 2, 2: 3, 3: 2}[layer]

        def front(i):
            stages = [[("scale", i)], [("turn", i)]]
            return stages + ([[("logits", i)]] if E else [])

        def order(i):
            steps = []
            more = not (isinstance(i, int) and i == NI - 1)
            late = not (isinstance(i, int) and i == 0)
            at = {0: (0, 1, 2), 1: (5, 7, 8), 2: (0, 2), 3: (0, 1, 2)}[layer]
            stages = front(i + 1) if more else []
            for c in range(C):
                steps += [("up", i, c)]
                if E and c == 0:
                    steps += [("gates", i)]
                steps += [("mul", i, c)]
                for step, lag in (("split", SPLIT_LAG), ("down", DOWN_LAG)):
                    if c >= lag:
                        steps += [(step, i, c - lag)]
                    elif late:
                        steps += [(step, i - 1, C + c - lag)]
                if late and c == DOWN_LAG - 1:
                    steps += [("y_copy", i - 1)]
                if late and c == 2 and not E:
                    steps += [("y_turn", i - 1)]
                for k, stage in enumerate(stages):
                    if at[k] == c:
                        steps += stage
                if late and E and c == {0: 3, 1: 11, 3: 3}[layer]:
                    steps += [("y_turn", i - 1)]
            return steps

        flush = [("split", NI - 1, C - k) for k in range(SPLIT_LAG, 0, -1)] + [("down", NI - 1, C - k) for k in range(DOWN_LAG, 0, -1)] \
            + [("y_copy", NI - 1), ("y_turn", NI - 1)]

        def passes(eng, does):
            def run(steps):
                for step, *at in steps:
                    if step in does:
                        does[step](*at)
            for stage in front(0):
                run(stage)
            run(order(0))
            with eng.Fori(1, NI - 1) as i:
                run(order(i))
            run(order(NI - 1))
            run(flush)

        with nc.Block() as block:
            @block.sync
            def _(sp):
                if layer == 0:
                    loads = ((sel_rows[:], ins["L0_ffn_expert_sel"]), (extra[:, 0:1], ins["L0_ffn_route_scale"].partition_broadcast(P)))
                elif layer == 1:
                    loads = ((router[:], ins["L1_ffn_router_w"]), (bias_col[:], ins["L1_ffn_bias"].rearrange("(p a) -> p a", a=1)))
                elif layer == 2:
                    loads = ((wi[:, 0:3], ins["L2_ffn_w_gate"].rearrange("(c p) d -> p c d", p=P)),
                             (wi[:, 3:6], ins["L2_ffn_w_up"].rearrange("(c p) d -> p c d", p=P)),
                             (wi[:, 6:9], ins["L2_ffn_w_down"].rearrange("d (c p) -> d c p", p=P)))
                else:
                    loads = ((router[:], ins["L3_ffn_gate_w"]), (extra[:], ins["L3_ffn_gate_bias"].partition_broadcast(P)))
                for dst, src in loads:
                    sp.dma_start(dst, src).then_inc(sem["loaded"], 16)

            @block.gpsimd
            def _(pool):
                pool.wait_ge(sem["moments"], 1)
                pool.tensor_tensor(ve[:], mv[:, :, 1], pr.eps[:], ALU.add).then_inc(sem["var_eps"], 1)
                pool.wait_ge(sem["var_eps"], 1)
                pool.tensor_tensor(rstd[:], ve[:], pr.neg_half[:], ALU.pow).then_inc(sem["rstd"], 1)

                def mul(i, c):
                    m, r = rows(c), c % R
                    pool.wait_ge(sem["half_done"], i * C + (c + 1))
                    if c not in GATED:
                        pool.wait_ge(sem["h_done"], i * C + c)
                        pool.sem_inc(sem["h_done"], 1)
                        return
                    e = c // 3 if layer == 1 else c
                    pool.wait_ge(sem["gate_copied"], i * N_GATES + (e + 1))
                    pool.tensor_tensor(h[0:m, r], h[0:m, r], gb[0:m, gate_slot(c)], ALU.mult).then_inc(sem["h_done"], 1)

                if POOL_GATES:
                    passes(pool, {"mul": mul})

            @block.tensor
            def _(pe):
                pe.wait_ge(sem["loaded"], LOADED)
                if layer == 0:
                    pe.transpose(b_turn[:, 0:E0], sel_rows[:], pr.id(E0)).then_inc(sem["prep_pe"], 1)
                if layer == 2:
                    for m in range(3):
                        pe.wait_ge(sem["prep_dve"], m + 1)
                        for k in range(3):
                            last = pe.transpose(pr.bank[m][:, k * P:(k + 1) * P], wf[:, 3 * m + k], pr.id())
                        last.then_inc(sem["prep_pe"], 1)
                pe.wait_ge(sem["prep_dve"], PREP_DVE)

                def turn(i):
                    pe.wait_ge(sem["xn_ready"], i + 1)
                    if E:
                        need(pe, sem["gts_ready"], i)
                    else:
                        need(pe, sem["x_done"], i)
                        need(pe, sem["xt_lo"], i)
                    for t in range(T):
                        last = pe.transpose(b_turn[:, t * P:(t + 1) * P], xn[:, t], pr.id())
                    last.then_inc(sem["xn_turned"], 1)

                def logits(i):
                    pe.wait_ge(sem["xt_raw"], i + 1)
                    pe.wait_ge(sem["xt_lo"], i + 1)
                    for t in range(T):
                        last = pe.matmul(b_turn[:, t * E:(t + 1) * E], xt_raw[:, t * P:(t + 1) * P], router[:], start=True, stop=True)
                    last.then_inc(sem["logits_done"], 1)

                def gates(i):
                    pe.wait_ge(sem["routed"], i * NROUTE + NROUTE)
                    need(pe, sem["x_done"], i)
                    for t in range(T):
                        last = pe.transpose(b_turn[:, t * P:(t + 1) * P], gx[:, t].rearrange("p e u -> p (e u)"), pr.id())
                    last.then_inc(sem["gates_turned"], 1)

                def up(i, c):
                    m = rows(c)
                    first, second, _down = weights_at(c)
                    xh = xt_hi[:, bass.ds(i, 1)].rearrange("p a t -> p (a t)")
                    xl = xt_lo[:, bass.ds(i, 1)].rearrange("p a t -> p (a t)")
                    pe.wait_ge(sem["xt_lo"], i + 1)
                    need(pe, sem["half_done"], i * C + (c - distance(c) + 1))
                    for at, bank in ((first, b_g[c % NS]),) + (((second, b_u[c % NS]),) if HAS_UP else ()):
                        pe.matmul(bank[0:m], hi[:, at:at + m], xh, start=True, stop=False)
                        pe.matmul(bank[0:m], hi[:, at:at + m], xl, start=False, stop=False)
                        last = pe.matmul(bank[0:m], lo[:, at:at + m], xh, start=False, stop=True)
                    last.then_inc(sem["up_done"], 1)

                def mul(i, c):
                    if c in GATED and (layer != 1 or c % 3 == 0):
                        pe.wait_ge(sem["gts_ready"], i + 1)
                        if POOL_GATES:
                            need(pe, sem["gate_copied"], i * N_GATES + ((c // 3 if layer == 1 else c) - 1))
                        else:
                            need(pe, sem["h_done"], i * C + (c - gate_distance(c) + 1))
                        lhs = sel[:, c // 3:c // 3 + 1].to_broadcast([P, P]) if layer == 1 else sel[:, c * P:(c + 1) * P]
                        pe.matmul(b_gate[gate_slot(c)][:], lhs, gts[:, bass.ds(i, 1)].rearrange("p a t -> p (a t)"),
                                  start=True, stop=True).then_inc(sem["gate_done"], 1)

                def down(i, c):
                    m, r, at = rows(c), c % R, weights_at(c)[2]
                    pe.wait_ge(sem["lo_done"], i * C + (c + 1))
                    if c == 0:
                        need(pe, sem["yt_ready"], i)
                    pe.matmul(b_y[:], hi[0:m, at:at + P], h_hi[0:m, r], start=(c == 0), stop=False)
                    pe.matmul(b_y[:], hi[0:m, at:at + P], h_lo[0:m, r], start=False, stop=False)
                    pe.matmul(b_y[:], lo[0:m, at:at + P], h_hi[0:m, r], start=False, stop=(c == C - 1)).then_inc(sem["down_done"], 1)

                def y_turn(i):
                    pe.wait_ge(sem["yt_ready"], i + 1)
                    if isinstance(i, int) and i == NI - 1:
                        pe.wait_ge(sem["x_done"], NI)
                    elif not E:
                        pe.wait_ge(sem["xt_lo"], i + 2)
                    elif isinstance(i, int) and i == NI - 2:
                        pe.wait_ge(sem["gts_ready"], NI)
                    else:
                        pe.wait_ge(sem["logits_less"] if layer == 1 else sem["logits_exp"], i + 3)
                    for t in range(T):
                        last = pe.transpose(b_turn[:, t * P:(t + 1) * P], yt[:, t * P:(t + 1) * P], pr.id())
                    last.then_inc(sem["y_turned"], 1)

                passes(pe, {"turn": turn, "logits": logits, "gates": gates, "up": up, "mul": mul, "down": down, "y_turn": y_turn})

            @block.scalar
            def _(act):
                if layer == 2:
                    for m in range(3):
                        act.wait_ge(sem["prep_pe"], m + 1)
                        act.copy(hi[:, m * 384:(m + 1) * 384], pr.bank[m][:, 0:384]).then_inc(sem["prep_act"], 1)
                if layer == 1:
                    act.wait_ge(sem["loaded"], LOADED)

                def turn(i):
                    act.wait_ge(sem["xn_turned"], i + 1)
                    if E:
                        need(act, sem["logits_done"], i)
                        act.copy(xt_raw[:], b_turn[:]).then_inc(sem["xt_raw"], 1)
                    act.copy(xt_hi[:, bass.ds(i, 1)].rearrange("p a t -> p (a t)"), b_turn[:]).then_inc(sem["xt_hi"], 1)

                def logits(i):
                    scores = b_turn[:, 0:T * E].rearrange("p (t e) -> p t e", e=E)
                    if layer == 1:
                        act.wait_ge(sem["logits_less"], i + 1)
                        act.activation(pe_[:], p1[:], ACT.Exp).then_inc(sem["logits_exp"], 1)
                    else:
                        act.wait_ge(sem["logits_done"], i + 1)
                        need(act, sem["routed"], i * NROUTE)
                        act.activation(pe_[:], scores, ACT.Exp, scale=-1.0).then_inc(sem["logits_exp"], 1)

                def gates(i):
                    act.wait_ge(sem["gates_turned"], i + 1)
                    need(act, sem["gts_ready"], i)
                    act.activation(hg[:].bitcast(F32R), b_turn[:], ACT.Copy, scale=pr.c("a8" if layer == 0 else "a16")).then_inc(sem["gates_hi"], 1)

                def up(i, c):
                    m = rows(c)
                    act.wait_ge(sem["up_done"], i * C + (c + 1))
                    need(act, sem["half_done"], i * C + (c + 1 - R))
                    act.activation(a[0:m, c % R], b_g[c % NS][0:m], FUNC).then_inc(sem["act_done"], 1)

                def mul(i, c):
                    if POOL_GATES and c in GATED and (layer != 1 or c % 3 == 0):
                        act.wait_ge(sem["gate_done"], i * N_GATES + ((c // 3 if layer == 1 else c) + 1))
                        need(act, sem["h_done"], i * C + (c - gate_distance(c) + 1))
                        act.copy(gb[:, gate_slot(c)], b_gate[gate_slot(c)][:]).then_inc(sem["gate_copied"], 1)

                def split(i, c):
                    m = rows(c)
                    act.wait_ge(sem["h_done"], i * C + (c + 1))
                    if isinstance(i, int) or R != C or c < C - SPLIT_LAG:
                        need(act, sem["down_done"], i * C + (c + 1 - R))
                    act.copy(h_hi[0:m, c % R], h[0:m, c % R]).then_inc(sem["hi_done"], 1)

                def y_copy(i):
                    act.wait_ge(sem["down_done"], i * C + C)
                    if isinstance(i, int) and i == NI - 1:
                        act.wait_ge(sem["y_turned"], i)
                    if layer == 1:
                        act.activation(yt[:], b_y[:], ACT.Identity, bias=bias_col[:]).then_inc(sem["yt_ready"], 1)
                    else:
                        act.copy(yt[:], b_y[:]).then_inc(sem["yt_ready"], 1)

                passes(act, {"turn": turn, "logits": logits, "gates": gates, "up": up, "mul": mul, "split": split, "y_copy": y_copy})

            @block.vector
            def _(dve):
                count = [0]

                def prep(ins_):
                    count[0] += 1
                    ins_.then_inc(sem["prep_dve"], 1)
                    dve.wait_ge(sem["prep_dve"], count[0])
                for tile in range(NT):
                    last = dve.bn_stats(pr.st6[:, tile], pr.x[:, tile])
                last.then_inc(sem["stats"], 1)
                dve.wait_ge(sem["stats"], 1)
                for tile in range(NT):
                    last = dve.bn_aggr(mv[:, tile], pr.st6[:, tile])
                last.then_inc(sem["moments"], 1)
                if layer == 2:
                    dve.wait_ge(sem["loaded"], LOADED)
                    for m in range(3):
                        prep(dve.tensor_scalar(wf[:, 3 * m:3 * m + 3], wi[:, 3 * m:3 * m + 3], 1.0 / 127.0, None, ALU.mult))
                    for m in range(3):
                        cols = slice(m * 384, (m + 1) * 384)
                        dve.wait_ge(sem["prep_act"], m + 1)
                        prep(dve.tensor_tensor(lo[:, cols], pr.bank[m][:, 0:384], hi[:, cols].bitcast(F32), ALU.subtract))
                if E:
                    prep(dve.memset(gx[:], 0.0))
                    prep(dve.memset(cand[:], SENTINEL))
                    prep(dve.memset(want[:], SENTINEL))
                    prep(dve.tensor_copy(sel[:], pr.c({0: "self0", 1: "e8", 3: "self3"}[layer])))
                    dve.wait_ge(sem["loaded"], LOADED)
                if layer == 0:
                    dve.wait_ge(sem["prep_pe"], 1)
                    prep(dve.tensor_copy(router[:], b_turn[:, 0:E0]))
                if layer == 3:
                    prep(dve.memset(gs[:], SENTINEL))
                    prep(dve.memset(gwant[:], SENTINEL))
                PREPARED = count[0]
                assert PREPARED == PREP_DVE, PREPARED

                dve.sem_inc(sem["x_done"], 1)
                dve.wait_ge(sem["rstd"], 1)

                def scale(i):
                    need(dve, sem["xn_turned"], i)
                    for t in range(T):
                        tile = bass.ds(i * T + t, 1)
                        last = dve.tensor_scalar(xn[:, t:t + 1], pr.x[:, tile], mv[:, tile, 0], rstd[:, tile], ALU.subtract, ALU.mult)
                    last.then_inc(sem["xn_ready"], 1)

                def turn(i):
                    dve.wait_ge(sem["xt_hi"], i + 1)
                    at = bass.ds(i, 1)
                    dve.tensor_tensor(xt_lo[:, at].rearrange("p a t -> p (a t)"), b_turn[:],
                                      xt_hi[:, at].rearrange("p a t -> p (a t)").bitcast(F32), ALU.subtract).then_inc(sem["xt_lo"], 1)

                def logits(i):
                    done = [0]

                    def step(ins_, k=1, settle=False):
                        done[0] += k
                        ins_.then_inc(sem["routed"], k)
                        dve.wait_ge(sem["routed"], i * NROUTE + done[0])
                        if settle:
                            settled(dve, sem)

                    def choose(cand, top, want, left, k):
                        for t in range(T):
                            last = dve.max(top[:, t], cand[:, t])
                        step(last)
                        step(dve.tensor_copy(want[:, :, 0:k], top[:, :, 0:k]), settle=True)
                        for t in range(T):
                            last = dve.match_replace(left[:, t], want[:, t], cand[:, t], TAKEN)
                        step(last)

                    def per_token(v):
                        return v[:].unsqueeze(2).to_broadcast([P, T, E])

                    need(dve, sem["gates_turned"], i)
                    if layer == 1:
                        scores = b_turn[:, 0:T * E].rearrange("p (t e) -> p t e", e=E)
                        dve.wait_ge(sem["logits_done"], i + 1)
                        need(dve, sem["logits_exp"], i)
                        step(dve.tensor_reduce(total[:], scores, AX_X, ALU.max))
                        dve.tensor_tensor(p1[:], scores, per_token(total), ALU.subtract).then_inc(sem["logits_less"], 1)
                        dve.wait_ge(sem["logits_exp"], i + 1)
                        step(dve.tensor_reduce(total2[:], pe_[:], AX_X, ALU.add))
                        step(dve.reciprocal(total3[:], total2[:]))
                        step(dve.tensor_tensor(cand[:, :, 0:E], pe_[:], per_token(total3), ALU.mult), settle=True)
                        choose(cand, top8, want, left, K)
                        for u in range(2):
                            last = dve.scalar_tensor_tensor(gx[:, :, :, u], left[:, :, 0:E], 2 * LOWEST, cand[:, :, 0:E], ALU.is_lt, ALU.mult)
                        step(last, NROUTE - done[0])
                        return
                    dve.wait_ge(sem["logits_exp"], i + 1)
                    step(dve.tensor_scalar(p1[:], pe_[:], 1.0, None, ALU.add))
                    if layer == 0:
                        score = cand[:, :, 0:E]
                        step(dve.reciprocal(score, p1[:]), settle=True)
                    else:
                        score = picked[:]
                        step(dve.reciprocal(pe_[:], p1[:]))
                        step(dve.tensor_tensor(score, pe_[:], extra[:].unsqueeze(1).to_broadcast([P, T, E]), ALU.add))
                        pairs = score.rearrange("p t (g e) -> p t g e", e=2)
                        step(dve.tensor_tensor(gs[:, :, 0:NG3], pairs[:, :, :, 0], pairs[:, :, :, 1], ALU.add), settle=True)
                        choose(gs, gtop, gwant, gleft, 2)
                        for e in range(2):
                            last = dve.scalar_tensor_tensor(cand[:, :, 0:E].rearrange("p t (g e) -> p t g e", e=2)[:, :, :, e], gleft[:, :, 0:NG3],
                                                            2 * LOWEST, pairs[:, :, :, e], ALU.is_lt, ALU.mult)
                        step(last, settle=True)
                    choose(cand, top8, want, left, K)
                    step(dve.scalar_tensor_tensor(p1[:], left[:, :, 0:E], 2 * LOWEST, score, ALU.is_lt, ALU.mult))
                    step(dve.tensor_reduce(total[:], p1[:], AX_X, ALU.add))
                    if layer == 0:
                        step(dve.tensor_scalar(total2[:], total[:], 1e-9, None, ALU.max))
                        step(dve.reciprocal(total[:], total2[:]))
                        step(dve.tensor_scalar(total3[:], total[:], extra[:, 0:1], None, ALU.mult))
                    else:
                        step(dve.tensor_scalar(total2[:], total[:], 1e-20, None, ALU.add))
                        step(dve.reciprocal(total[:], total2[:]))
                        step(dve.tensor_scalar(total3[:], total[:], SC3, None, ALU.mult))
                    step(dve.tensor_tensor(gx[:, :, :, 0:2], p1[:].unsqueeze(3).to_broadcast([P, T, E, 2]),
                                           total3[:].unsqueeze(2).unsqueeze(3).to_broadcast([P, T, E, 2]), ALU.mult), NROUTE - done[0])

                def gates(i):
                    dve.wait_ge(sem["gates_hi"], i + 1)
                    dve.tensor_tensor(gts[:, bass.ds(i, 1)].rearrange("p a t -> p (a t)"), b_turn[:], hg[:], ALU.add).then_inc(sem["gts_ready"], 1)

                def mul(i, c):
                    m, r = rows(c), c % R
                    dve.wait_ge(sem["act_done"], i * C + (c + 1))
                    need(dve, sem["lo_done"], i * C + (c + 1 - R))
                    if HAS_UP:
                        dve.tensor_tensor(h[0:m, r], a[0:m, r], b_u[c % NS][0:m], ALU.mult).then_inc(sem["half_done"], 1)
                    else:
                        dve.wait_ge(sem["gate_done"], i * N_GATES + (c + 1))
                        dve.tensor_tensor(h[0:m, r], a[0:m, r], b_gate[gate_slot(c)][0:m], ALU.mult).then_inc(sem["h_done"], 1)

                def split(i, c):
                    m, r = rows(c), c % R
                    dve.wait_ge(sem["hi_done"], i * C + (c + 1))
                    dve.tensor_tensor(h_lo[0:m, r], h[0:m, r], h_hi[0:m, r].bitcast(F32), ALU.subtract).then_inc(sem["lo_done"], 1)

                def y_turn(i):
                    dve.wait_ge(sem["y_turned"], i + 1)
                    xb = pr.x[:, tiles(i, T)]
                    dve.scalar_tensor_tensor(xb, b_turn[:].rearrange("p (t d) -> p t d", t=T), tg, xb, ALU.mult, ALU.add).then_inc(sem["x_done"], 1)
                    if layer < 3:
                        dve.wait_ge(sem["x_done"], i + 2)
                        settled(dve, sem)
                        for t in range(T):
                            tile = bass.ds(i * T + t, 1)
                            dve.bn_stats(pr.st6[:, tile], pr.x[:, tile])

                passes(dve, {"scale": scale, "turn": turn, "logits": logits, "gates": gates, "mul": mul, "split": split,
                             "y_turn": y_turn})



def store(pr):
    stored = pr.sem("stored")
    with pr.nc.Block() as block:

        @block.sync
        def _(sp):
            ov = pr.out.rearrange("b (t p) d -> p (b t) d", p=P)
            for h in range(2):
                sp.dma_start(ov[:, 8 * h:8 * h + 8], pr.x[:, 8 * h:8 * h + 8]).then_inc(stored, 16)
            sp.wait_ge(stored, 32)


def build(nc, ins, out):
    with ExitStack() as ctx:
        pr = Program(nc, ctx, ins, out)
        setup(pr)
        attention(pr, 0, own_keys=False, masked=False, biased=True, scale=HD ** -0.5)
        ffn(pr, 0)
        attention(pr, 1, own_keys=True, masked=False, biased=False, scale=HD ** -0.5)
        ffn(pr, 1)
        attention(pr, 2, own_keys=False, masked=True, biased=True, scale=D ** -0.5)
        ffn(pr, 2)
        attention3(pr)
        ffn(pr, 3)
        store(pr)


def constants():
    import numpy as np
    p = np.arange(P)[:, None]
    i = np.arange(P)[None, :]
    j = np.arange(4 * P)[None, :]
    part = (p % 32) // HD
    pair = np.arange(2 * P)[None, :]
    head_sel = -((p // 32 == 2 * (pair // P) + (pair % P) // 64) & (p % 32 < 2)).astype(np.float32)
    cols = {
        "ident": p == i,
        "aq": -(part >= 2).astype(np.float32), "ak": -(part % 2 == 1).astype(np.float32),
        "am": -(p % 32 != 0).astype(np.float32), "amask": -(p >= 64).astype(np.float32),
        "am1": -(p % 32 != 24).astype(np.float32), "neg1": -(p % 32 // 2 == 12).astype(np.float32),
        "a8": -(p % 8 != 0).astype(np.float32), "a16": -(p % 16 != 0).astype(np.float32),
        "half": p // 64 == np.arange(2)[None, :], "half_past": (p // 64 == np.arange(2)[None, :]) & (p % 64 > 0),
        "head4": p // 32 == np.arange(4)[None, :],
        "selc": head_sel,
        "i2": p % 64 == i % 64,
        "self0": (p // 8 == 4 * (j // P) + (j % P) // 32) & (p % 8 < 2),
        "self3": (p // 16 == 2 * (j // P) + (j % P) // 64) & (p % 16 < 2),
        "e8": (p // 16 == np.arange(8)[None, :]) & (p % 16 < 2),
        "sum3": (j % P) // 16 == 2 * (j // P) + p // 64,
    }
    out = np.zeros((P, NCONST), np.float32)
    for name, (at, n) in CONST.items():
        out[:, at:at + n] = cols[name]
    return out


_INS = ["x", "ctx_1024", "mask_Bx1xSxS2_ff0", "g_xattn", "g_ffn",
        "L0_xattn_Wq", "L0_xattn_bq", "L0_xattn_Wkv", "L0_xattn_bkv", "L0_xattn_Wo", "L0_xattn_bo",
        "L0_ffn_expert_sel", "L0_ffn_keys", "L0_ffn_values", "L0_ffn_route_scale",
        "L1_xattn_Wq", "L1_xattn_Wk", "L1_xattn_Wv", "L1_xattn_gate", "L1_xattn_ln_g", "L1_xattn_ln_b", "L1_xattn_Wp", "L1_xattn_bp",
        "L1_ffn_router_w", "L1_ffn_w1", "L1_ffn_v1", "L1_ffn_w2", "L1_ffn_bias",
        "L2_xattn_Wq", "L2_xattn_bq", "L2_xattn_Wk", "L2_xattn_bk", "L2_xattn_Wv", "L2_xattn_bv", "L2_xattn_Wo", "L2_xattn_bo",
        "L2_ffn_w_gate", "L2_ffn_w_up", "L2_ffn_w_down",
        "L3_xattn_Wq", "L3_xattn_Wk", "L3_xattn_Wv", "L3_xattn_Wo", "L3_xattn_bo",
        "L3_ffn_gate_w", "L3_ffn_gate_bias", "L3_ffn_w_gate", "L3_ffn_w_up", "L3_ffn_w_down",
        "L3_ffn_sw_gate", "L3_ffn_sw_up", "L3_ffn_sw_down"]


def kernel(**inputs):
    import numpy as _np
    import concourse.bacc as _bacc
    from concourse import mybir as _mybir
    from concourse.bass_utils import run_bass_kernel_spmd as _run

    nc = _bacc.Bacc("TRN2", target_bir_lowering=False, num_devices=1)
    arrays, ins = {}, {}
    values = {name: _np.ascontiguousarray(inputs[name]) for name in _INS}
    values["const"] = constants()
    for name, a in values.items():
        arrays[f"in_{name}_dram"] = a
        ins[name] = nc.dram_tensor(f"in_{name}_dram", a.shape, _mybir.dt.from_np(a.dtype), kind="ExternalInput").ap()
    out = nc.dram_tensor("out_0_dram", (B, S, D), F32, kind="ExternalOutput").ap()
    build(nc, ins, out)
    r = _run(nc, [arrays], core_ids=[0])
    return r.results[0]["out_0_dram"]
```
